# Optimizing a Trainium2 kernel written in Bass

```python
import numpy as np
import jax
import jax.numpy as jnp

def _softmax(x, axis=-1):
    return jax.nn.softmax(x, axis=axis)

def _gelu(x):
    return jax.nn.gelu(x, approximate=True)

def _silu(x):
    return jax.nn.silu(x)

def _sigmoid(x):
    return jax.nn.sigmoid(x)

def _layernorm(x, axis=-1, eps=1e-05):
    m = jnp.mean(x, axis=axis, keepdims=True)
    v = jnp.var(x, axis=axis, keepdims=True)
    return (x - m) / jnp.sqrt(v + eps)

def _scatter_add(tgt, idx, src, axis=0):
    return tgt.at[idx].add(src)

def _segment_sum(src, seg, n):
    return jax.ops.segment_sum(src, seg, n)
kernel_name = 'mk_adaln_d1_jaxref_r4_281666'

def setup_inputs(seed: int=0):
    np.random.seed(seed)
    _w = jnp.asarray

    def _L0_attn_setup():
        import jax, jax.numpy as jnp
        import numpy as np
        B, N, C, H, K = (4, 1024, 256, 16, 2)
        D = C // H

        def _kernel(x):
            return jax.nn.silu(x) + 0.5
        key = jax.random.key(seed)
        ks = jax.random.split(key, 8)
        s = 0.02
        x = jax.random.normal(ks[0], (B, N, C), jnp.float32)
        Wq = jax.random.normal(ks[1], (C, C), jnp.float32) * s
        bq = jnp.zeros((C,), jnp.float32)
        Wk = jax.random.normal(ks[2], (K, C, C), jnp.float32) * s
        bk = jnp.zeros((K, C), jnp.float32)
        Wv = jax.random.normal(ks[3], (K, C, C), jnp.float32) * s
        bv = jnp.zeros((K, C), jnp.float32)
        Wo = jax.random.normal(ks[4], (C, C), jnp.float32) * s
        bo = jnp.zeros((C,), jnp.float32)
        ln_g = jnp.ones((C,), jnp.float32)
        ln_b = jnp.zeros((C,), jnp.float32)
        return dict(x=x, Wq=Wq, bq=bq, Wk=Wk, bk=bk, Wv=Wv, bv=bv, Wo=Wo, bo=bo, ln_g=ln_g, ln_b=ln_b)
    _L0_attn_in = _L0_attn_setup()

    def _L0_ffn_setup():
        import jax, jax.numpy as jnp
        import numpy as np
        H = 256
        I = 4 * H
        E = 8
        K = 2
        B, S = (2, 256)
        STD = 0.02 / np.sqrt(H)
        key = jax.random.key(seed)
        ks = jax.random.split(key, 8)
        x = jax.random.normal(ks[0], (B, S, H), dtype=jnp.float32)
        gate_w = jax.random.normal(ks[1], (H, E), dtype=jnp.float32) * STD
        bias = jnp.zeros((E,), dtype=jnp.float32)
        up_w = jax.random.normal(ks[2], (E, H, I), dtype=jnp.float32) * STD
        up_b = jnp.zeros((E, I), dtype=jnp.float32)
        down_w = jax.random.normal(ks[3], (E, I, H), dtype=jnp.float32) * STD
        down_b = jnp.zeros((E, H), dtype=jnp.float32)
        sw_up = jax.random.normal(ks[4], (H, I), dtype=jnp.float32) * STD
        sb_up = jnp.zeros((I,), dtype=jnp.float32)
        sw_down = jax.random.normal(ks[5], (I, H), dtype=jnp.float32) * STD
        sb_down = jnp.zeros((H,), dtype=jnp.float32)
        return {'x': x, 'gate_w': gate_w, 'bias': bias, 'up_w': up_w, 'up_b': up_b, 'down_w': down_w, 'down_b': down_b, 'sw_up': sw_up, 'sb_up': sb_up, 'sw_down': sw_down, 'sb_down': sb_down}
    _L0_ffn_in = _L0_ffn_setup()
    _L0_c = _w((lambda *s: np.random.randn(*s).astype(np.float32) * 0.05)(1, 256))
    _L0_wmod = _w((lambda *s: np.random.randn(*s).astype(np.float32) * 0.05)(256, 6 * 256) * 256 ** (-0.5))
    _d = {'L0_attn_x': _L0_attn_in['x'], 'L0_attn_Wq': _L0_attn_in['Wq'], 'L0_attn_bq': _L0_attn_in['bq'], 'L0_attn_Wk': _L0_attn_in['Wk'], 'L0_attn_bk': _L0_attn_in['bk'], 'L0_attn_Wv': _L0_attn_in['Wv'], 'L0_attn_bv': _L0_attn_in['bv'], 'L0_attn_Wo': _L0_attn_in['Wo'], 'L0_attn_bo': _L0_attn_in['bo'], 'L0_attn_ln_g': _L0_attn_in['ln_g'], 'L0_attn_ln_b': _L0_attn_in['ln_b'], 'L0_ffn_gate_w': _L0_ffn_in['gate_w'], 'L0_ffn_bias': _L0_ffn_in['bias'], 'L0_ffn_up_w': _L0_ffn_in['up_w'], 'L0_ffn_up_b': _L0_ffn_in['up_b'], 'L0_ffn_down_w': _L0_ffn_in['down_w'], 'L0_ffn_down_b': _L0_ffn_in['down_b'], 'L0_ffn_sw_up': _L0_ffn_in['sw_up'], 'L0_ffn_sb_up': _L0_ffn_in['sb_up'], 'L0_ffn_sw_down': _L0_ffn_in['sw_down'], 'L0_ffn_sb_down': _L0_ffn_in['sb_down'], 'L0_c': _L0_c, 'L0_wmod': _L0_wmod}
    _x0 = _d['L0_attn_x']
    _d['L0_attn_x'] = jax.random.normal(jax.random.fold_in(jax.random.key(seed), 1), (1, 4096, 256), dtype=_x0.dtype)
    del _x0
    return _d

def reference(L0_attn_x, L0_attn_Wq, L0_attn_bq, L0_attn_Wk, L0_attn_bk, L0_attn_Wv, L0_attn_bv, L0_attn_Wo, L0_attn_bo, L0_attn_ln_g, L0_attn_ln_b, L0_ffn_gate_w, L0_ffn_bias, L0_ffn_up_w, L0_ffn_up_b, L0_ffn_down_w, L0_ffn_down_b, L0_ffn_sw_up, L0_ffn_sb_up, L0_ffn_sw_down, L0_ffn_sb_down, L0_c, L0_wmod):

    def _L0_attn_ref(x, Wq, bq, Wk, bk, Wv, bv, Wo, bo, ln_g, ln_b):
        import jax, jax.numpy as jnp
        import numpy as np
        B, N, C, H, K = (4, 1024, 256, 16, 2)
        D = C // H

        def _kernel(x):
            return jax.nn.silu(x) + 0.5
        dtype = x.dtype
        Bn, Nn, Cn = x.shape
        q = x + x @ Wq.T + bq
        ks = x[None] + jnp.einsum('bnc,kdc->kbnd', x, Wk) + bk[:, None, None, :]
        vs = x[None] + jnp.einsum('bnc,kdc->kbnd', x, Wv) + bv[:, None, None, :]
        q = q.reshape(Bn, Nn, H, D).transpose(0, 2, 1, 3)
        ks = ks.reshape(K, Bn, Nn, H, D).transpose(0, 1, 3, 2, 4)
        vs = vs.reshape(K, Bn, Nn, H, D).transpose(0, 1, 3, 2, 4)
        q = _kernel(q)
        ks = _kernel(ks)
        q = q / (jnp.linalg.norm(q, axis=-1, keepdims=True) + 1e-06)
        ks = ks / (jnp.linalg.norm(ks, axis=-1, keepdims=True) + 1e-06)
        scale = Nn ** (-0.5)
        ks = ks.astype(jnp.float32) * scale
        vs = vs.astype(jnp.float32) * scale
        states = jnp.einsum('kbhnd,kbhne->kbhde', ks, vs)
        state = jnp.prod(states, axis=0)
        out = jnp.einsum('bhnd,bhde->bhne', q.astype(jnp.float32), state)
        out = out.astype(dtype)
        out = out.transpose(0, 2, 1, 3).reshape(Bn, Nn, Cn)
        mu = out.mean(axis=-1, keepdims=True)
        var = out.var(axis=-1, keepdims=True)
        out = (out - mu) * jax.lax.rsqrt(var + 1e-05) * ln_g + ln_b
        out = out @ Wo.T + bo
        return out

    def _L0_ffn_ref(x, gate_w, bias, up_w, up_b, down_w, down_b, sw_up, sb_up, sw_down, sb_down):
        import jax, jax.numpy as jnp
        import numpy as np
        H = 256
        I = 4 * H
        E = 8
        K = 2
        B, S = (2, 256)
        STD = 0.02 / np.sqrt(H)
        b, s, h = x.shape
        xf = x.reshape(-1, h)
        T = xf.shape[0]
        scores = jax.nn.sigmoid(xf @ gate_w + bias)
        top_scores, top_idx = jax.lax.top_k(scores, K)
        top_scores = top_scores / (jnp.sum(top_scores, axis=-1, keepdims=True) + 1e-06)
        w = jnp.zeros((T, E), dtype=xf.dtype).at[jnp.arange(T)[:, None], top_idx].add(top_scores)
        up = jnp.einsum('th,ehi->tei', xf, up_w) + up_b
        hact = jax.nn.gelu(up, approximate=False)
        eo = jnp.einsum('tei,eih->teh', hact, down_w) + down_b
        combined = jnp.einsum('teh,te->th', eo * 0.1, w)
        shared = (jax.nn.gelu(xf @ sw_up + sb_up, approximate=False) @ sw_down + sb_down) * 0.1
        out = (shared + combined).reshape(b, s, h)
        out = out / (jnp.max(jnp.abs(out), axis=-1, keepdims=True) + 1e-06)
        return out
    x = L0_attn_x
    mod = (_silu(L0_c) @ L0_wmod).reshape(L0_c.shape[0], 6, 1, -1)
    sa, ca, ga, sb, cb, gb = (mod[:, 0], mod[:, 1], mod[:, 2], mod[:, 3], mod[:, 4], mod[:, 5])
    ga = (2 * (ga >= 0) - 1) * jnp.maximum(jnp.abs(ga), 0.25)
    gb = (2 * (gb >= 0) - 1) * jnp.maximum(jnp.abs(gb), 0.25)
    h = _layernorm(x, axis=-1) * (1 + ca) + sa
    x = x + ga * _L0_attn_ref(h, L0_attn_Wq, L0_attn_bq, L0_attn_Wk, L0_attn_bk, L0_attn_Wv, L0_attn_bv, L0_attn_Wo, L0_attn_bo, L0_attn_ln_g, L0_attn_ln_b)
    h = _layernorm(x, axis=-1) * (1 + cb) + sb
    x = x + gb * _L0_ffn_ref(h, L0_ffn_gate_w, L0_ffn_bias, L0_ffn_up_w, L0_ffn_up_b, L0_ffn_down_w, L0_ffn_down_b, L0_ffn_sw_up, L0_ffn_sb_up, L0_ffn_sw_down, L0_ffn_sb_down)
    return x

_drawn_inputs = setup_inputs


def setup_inputs(seed=0):
    import zlib

    import numpy as np

    out = dict(_drawn_inputs(seed))
    spreads = {'L0_attn_bq': (0.0, 2.0),
     'L0_attn_bk': (0.0, 2.0),
     'L0_attn_bv': (0.0, 0.301),
     'L0_attn_bo': (0.0, 0.33),
     'L0_attn_ln_g': (1.0, 0.6),
     'L0_attn_ln_b': (0.0, 0.8),
     'L0_ffn_bias': (0.0, 0.1),
     'L0_ffn_up_b': (0.0, 0.8),
     'L0_ffn_down_b': (0.0, 0.321),
     'L0_ffn_sb_up': (0.0, 0.8),
     'L0_ffn_sb_down': (0.0, 0.1)}
    factors = {'L0_attn_Wq': 9.223,
     'L0_attn_Wk': 8.0,
     'L0_attn_Wv': 8.0,
     'L0_ffn_up_w': 52.034,
     'L0_ffn_down_w': 8.0,
     'L0_ffn_sw_up': 37.449,
     'L0_ffn_sw_down': 8.0}
    for name, (base, spread) in spreads.items():
        noise = np.random.default_rng([zlib.crc32(name.encode()), seed]).standard_normal(out[name].shape)
        drawn = base * np.exp(spread * noise) if base else spread * noise
        out[name] = jnp.asarray(drawn.astype(out[name].dtype))
    for name, factor in factors.items():
        out[name] = (out[name] * factor).astype(out[name].dtype)
    return out
```

```python
from contextlib import ExitStack

import concourse.bass as bass
from concourse import mybir

ALU = mybir.AluOpType
ACT = mybir.ActivationFunctionType
F32 = mybir.dt.float32
F32R = mybir.dt.float32r
BF16 = mybir.dt.bfloat16
U32 = mybir.dt.uint32
I32 = mybir.dt.int32
AX = mybir.AxisListType

P = 128
N, C = 4096, 256
NT = N // P
TG = 4
NG = NT // TG
CK = C // P
HEADS, D = 16, 16
KV = 2
E, TOPK = 8, 2
INNER = 4 * C
MK = INNER // P
REG = N + P
ET = N * TOPK // P + E - 1
ETL = ET + 1
SLOT = 4 * CK * INNER
EPS_LN, EPS = 1e-5, 1e-6
HALF = 512
SRAW = 229312 - 2 * CK * INNER * 4


class Map:

    def __init__(self, nc, start):
        self.nc, self.at = nc, start

    def __call__(self, name, shape, dtype):
        size = 1
        for n in shape[1:]:
            size *= n
        size *= mybir.dt.size(dtype)
        t = self.nc.alloc_sbuf_tensor_at(name, shape, dtype, offset=self.at)
        self.at += -(-size // 64) * 64
        return t


def adaln_block(nc, x, Wq, bq, Wk, bk, Wv, bv, Wo, bo, ln_g, ln_b, gate_w, gate_b, up_w, up_b,
                down_w, down_b, sw_up, sb_up, sw_down, sb_down, c, wmod, hs, ys, shd, out):
    f32 = lambda ap: ap.bitcast(F32)
    ctx = ExitStack()
    sem = lambda name: ctx.enter_context(nc.semaphore(name))
    x_v = x[0].rearrange("(p t) c -> p t c", t=NT)
    out_v = out[0].rearrange("(p t) c -> p t c", t=NT)
    shd_v = shd.rearrange("(p t) c -> p t c", t=NT)

    waited = sem("waited")

    def wait(eng, semaphore, value):
        eng.wait_ge(semaphore, value)
        if not isinstance(value, int):
            eng.sem_inc(waited, 1)

    def rsqrt(link, y, x, t, between=lambda n: None):
        link(nc.vector.tensor_scalar(t.bitcast(I32), x.bitcast(I32), 1, None, ALU.logical_shift_right))
        link(nc.vector.tensor_scalar(y.bitcast(I32), t.bitcast(I32), -1.0, float(0x5F3759DF), ALU.mult, ALU.add))
        for n in range(3):
            between(n)
            link(nc.vector.tensor_tensor(t, y, y, ALU.mult))
            link(nc.vector.scalar_tensor_tensor(t, x, -0.5, t, ALU.mult, ALU.mult))
            link(nc.vector.scalar_tensor_tensor(y, t, 1.5, y, ALU.add, ALU.mult))

    RSQRT = 11

    keep = Map(nc, -(-nc.sbuf_base // 64) * 64)
    ident = keep("ident", [P, P], F32)
    one_f = keep("one_f", [P, P], F32)
    X = keep("X", [P, NT, C], F32)
    scale_a = keep("scale_a", [P, C], F32)
    shift_a = keep("shift_a", [P, C], F32)
    mv1 = keep("mv1", [P, NT, 2], F32)
    rs1 = keep("rs1", [P, 3, NT], F32)
    gate_a = keep("gate_a", [P, C], F32)
    scale_b = keep("scale_b", [P, C], F32)
    shift_b = keep("shift_b", [P, C], F32)
    gate_fb = keep("gate_fb", [P, C], F32)
    bo_row = keep("bo_row", [P, C], F32)
    sbd_row = keep("sbd_row", [P, C], F32)
    pos = keep("pos", [P, NT, TOPK], F32)
    ypos = keep("ypos", [P, NT, TOPK], U32)
    wtop = keep("wtop", [P, NT, TOPK], F32)
    run = keep("run", [P, E], F32)
    expo = keep("expo", [P, 2, 128], F32)
    iota_e = keep("iota_e", [P, E], F32)
    reg_e = keep("reg_e", [P, E], F32)
    etab = keep("etab", [P, ETL], I32)
    rtab = keep("rtab", [P, ETL], I32)
    stab = keep("stab", [P, ETL], I32)
    etab_end = keep("etab_end", [P, E], I32)
    phase = keep.at

    att = Map(nc, phase)
    su = att("su", [P, 2, CK, INNER], F32R)
    sd = att("sd", [P, 2, MK, C], F32R)
    wo = att("wo", [P, 2, CK, C], F32R)
    gw = att("gw", [P, 2, CK, E], F32R)
    gb_row = att("gb_row", [P, E], F32)
    sbu = att("sbu", [P, MK], F32)
    state = att("state", [P, CK, P], F32)
    heads = att("heads", [P, P // D], F32)
    tri = att("tri", [P, P], BF16)
    one_b = att("one_b", [P, P], BF16)
    qT = att("qT", [P, CK, NT * P], F32)
    after_q = att.at

    p1w = Map(nc, after_q)
    wkq = p1w("wkq", [P, 2, CK, (KV + 1) * C], F32R)
    wv = p1w("wv", [P, CK, KV * C], F32)
    bk_row = p1w("bk_row", [P, KV * C], F32)
    bv_row = p1w("bv_row", [P, KV * C], F32)
    bq_col = p1w("bq_col", [P, CK], F32)
    blocks = p1w("blocks", [P, P], F32)

    st = Map(nc, p1w.at)
    wnat = st("wnat", [P, 2 * KV + 2, CK, C], F32)
    mw = st("mw", [P, CK, 6 * C], F32)
    c_col = st("c_col", [P, CK], F32)
    c_act = st("c_act", [P, CK], F32)
    c_rows = st("c_rows", [P, CK, P], F32)
    mod = st("mod", [P, 6, C], F32)
    ga_abs = st("ga_abs", [P, 2, C], F32)
    ga_sgn = st("ga_sgn", [P, 2, C], F32)
    eye2 = st("eye2", [P, CK, C], F32)
    wtmp = st("wtmp", [P, CK, C], F32)
    lng_col = st("lng_col", [P, CK], F32)
    lnb_col = st("lnb_col", [P, CK], F32)
    lnb_rows = st("lnb_rows", [P, CK, P], F32)
    gw_raw = st("gw_raw", [P, CK, E], F32)
    bn0 = st("bn0", [P, NT, 6], F32)
    sraw = Map(nc, SRAW)("sraw", [P, 2, CK, INNER], F32)

    ld_c, ld_mod, ld_w, ld_row, ld_sh = [sem(n) for n in ("ld_c", "ld_mod", "ld_w", "ld_row", "ld_sh")]
    consts, c_silu, c_spread = sem("consts"), sem("c_silu"), sem("c_spread")
    mod_mm, mod_ok, wt_mm, wt_ok, dve0, pool0 = [sem(n) for n in (
        "mod_mm", "mod_ok", "wt_mm", "wt_ok", "dve0", "pool0")]
    bo_mm, x_stat = sem("bo_mm"), sem("x_stat")
    x_in = sem("x_in")

    with ExitStack() as mem, nc.Block() as block:
        ps = [mem.enter_context(nc.psum_tensor(f"set_ps{i}", [P, HALF], F32)) for i in range(8)]
        N_W, N_ROW = 6, 10

        @block.sync
        def _(sp):
            narrow = ctx.enter_context(nc.allow_non_contiguous_dma(reason="short vectors, a channel per partition"))
            sp.dma_start(c_col[:], c.rearrange("a (k p) -> p (a k)", p=P)).then_inc(ld_c, 16)
            sp.dma_start(mw[:], wmod.rearrange("(k p) n -> p k n", p=P)).then_inc(ld_mod, 16)
            for i, w in enumerate((Wq, Wk[0], Wk[1], Wv[0], Wv[1], Wo)):
                sp.dma_start(wnat[:, i], w.rearrange("(k p) n -> p k n", p=P)).then_inc(ld_w, 16)
            for dst, src in (
                (bk_row[:], bk.rearrange("k c -> (k c)").partition_broadcast(P)),
                (bv_row[:], bv.rearrange("k c -> (k c)").partition_broadcast(P)),
                (bo_row[:], bo.partition_broadcast(P)), (sbd_row[:], sb_down.partition_broadcast(P)),
                (gb_row[:], gate_b.partition_broadcast(P)),
                (bq_col[:], bq.rearrange("(k p) -> p k", p=P)),
                (lng_col[:], ln_g.rearrange("(k p) -> p k", p=P)),
                (lnb_col[:], ln_b.rearrange("(k p) -> p k", p=P)),
                (sbu[:], sb_up.rearrange("(k p) -> p k", p=P)),
                (gw_raw[:], gate_w.rearrange("(k p) e -> p k e", p=P)),
            ):
                sp.dma_start(dst, src).then_inc(ld_row, 16)
            with sp.Fori(0, NG) as g:
                sp.dma_start(X[:, bass.ds(g * TG, TG), :], x_v[:, bass.ds(g * TG, TG), :]).then_inc(x_in, 16)
                wait(sp, x_in, 16 * g + 16)
            sp.dma_start(sraw[:, 0], sw_up.rearrange("(k p) n -> p k n", p=P)).then_inc(ld_sh, 16)
            sp.dma_start(sraw[:, 1].rearrange("p k n -> p (k n)").rearrange("p (k n) -> p k n", k=MK),
                         sw_down.rearrange("(k p) n -> p k n", p=P)).then_inc(ld_sh, 16)

        @block.gpsimd
        def _(pool):
            step = [0]

            def link(ins):
                step[0] += 1
                ins.then_inc(pool0, 1)
                pool.wait_ge(pool0, step[0])

            link(nc.gpsimd.memset(ident[:], 0.0))
            link(nc.gpsimd.affine_select(out=ident[:], in_=ident[:], compare_op=ALU.not_equal, fill=1.0, base=0,
                                         pattern=[[-1, P]], channel_multiplier=1))
            link(nc.gpsimd.memset(eye2[:], 0.0))
            for k in range(CK):
                link(nc.gpsimd.affine_select(out=eye2[:, k], in_=eye2[:, k], compare_op=ALU.not_equal, fill=1.0,
                                             base=P * k, pattern=[[-1, C]], channel_multiplier=1))
            link(nc.gpsimd.memset(one_f[:], 1.0))
            link(nc.gpsimd.memset(one_b[:], 1.0))
            link(nc.gpsimd.memset(run[:], 0.0))
            link(nc.gpsimd.memset(expo[:, 0], 0.5))
            link(nc.gpsimd.memset(expo[:, 1], -0.5))
            link(nc.gpsimd.affine_select(out=tri[:], in_=one_b[:], compare_op=ALU.is_gt, fill=0.0, base=0,
                                         pattern=[[1, P]], channel_multiplier=-1))
            link(nc.gpsimd.affine_select(out=heads[:], in_=one_f[:, :P // D], compare_op=ALU.is_ge, fill=0.0,
                                         base=0, pattern=[[-D, P // D]], channel_multiplier=1))
            link(nc.gpsimd.affine_select(out=heads[:], in_=heads[:], compare_op=ALU.is_ge, fill=0.0,
                                         base=D - 1, pattern=[[D, P // D]], channel_multiplier=-1))
            bl = blocks[:].rearrange("p (h d) -> p h d", d=D)
            link(nc.gpsimd.affine_select(out=bl, in_=one_f[:].rearrange("p (h d) -> p h d", d=D),
                                         compare_op=ALU.is_ge, fill=0.0,
                                         base=0, pattern=[[-D, P // D], [0, D]], channel_multiplier=1))
            link(nc.gpsimd.affine_select(out=bl, in_=bl, compare_op=ALU.is_ge, fill=0.0,
                                         base=D - 1, pattern=[[D, P // D], [0, D]], channel_multiplier=-1))
            link(nc.gpsimd.iota(iota_e[:], [[1, E]], base=0, channel_multiplier=0,
                                allow_small_or_imprecise_dtypes=True))
            nc.gpsimd.iota(reg_e[:], [[REG, E]], base=0, channel_multiplier=0,
                           allow_small_or_imprecise_dtypes=True).then_inc(consts, 1)

        @block.scalar
        def _(act):
            act.wait_ge(ld_c, 16)
            nc.scalar.activation(c_act[:], c_col[:], ACT.Silu).then_inc(c_silu, 1)

        @block.tensor
        def _(pe):
            pe.wait_ge(c_spread, 1)
            pe.wait_ge(ld_mod, 16)
            for n in range(3):
                for k in range(CK):
                    mm = nc.tensor.matmul(ps[n][:], c_rows[:, k], mw[:, k, n * HALF:(n + 1) * HALF],
                                          start=(k == 0), stop=(k == CK - 1))
                mm.then_inc(mod_mm, 1)
            pe.wait_ge(ld_w, 16 * N_W)
            pe.wait_ge(consts, 1)
            for i in range(6):
                if i >= 3:
                    pe.wait_ge(wt_ok, i - 2)
                for k in range(CK):
                    for o in range(CK):
                        mm = nc.tensor.transpose(ps[3 + i % 3][:, k * C + o * P:k * C + (o + 1) * P],
                                                 wnat[:, i, o, k * P:(k + 1) * P], ident[:])
                mm.then_inc(wt_mm, 1)
            pe.wait_ge(wt_ok, 6)
            for k in range(CK):
                mm = nc.tensor.matmul(ps[6][:, 0:C], lnb_rows[:, k], wtmp[:, k], start=(k == 0), stop=(k == CK - 1))
            mm.then_inc(bo_mm, 1)

        @block.vector
        def _(dve):
            step = [0]

            def link(ins):
                step[0] += 1
                ins.then_inc(dve0, 1)
                dve.wait_ge(dve0, step[0])

            dve.wait_ge(c_silu, 1)
            nc.vector.tensor_copy(c_rows[:], c_act[:].unsqueeze(2).broadcast_to([P, CK, P])).then_inc(c_spread, 1)
            dve.wait_ge(mod_mm, 3)
            for n in range(3):
                link(nc.vector.tensor_copy(mod[:, 2 * n:2 * n + 2].rearrange("p a c -> p (a c)"), ps[n][:]))
            nc.vector.tensor_copy(shift_a[:], mod[:, 0])
            nc.vector.tensor_scalar(scale_a[:], mod[:, 1], 1.0, None, ALU.add)
            nc.vector.tensor_copy(shift_b[:], mod[:, 3])
            nc.vector.tensor_scalar(scale_b[:], mod[:, 4], 1.0, None, ALU.add)
            for i, (m, dst) in enumerate(((2, gate_a), (5, gate_fb))):
                link(nc.vector.tensor_scalar(ga_sgn[:, i], mod[:, m], 0.0, 2.0, ALU.is_ge, ALU.mult))
                link(nc.vector.scalar_tensor_tensor(ga_abs[:, i], mod[:, m], -1.0, mod[:, m], ALU.mult, ALU.max))
                link(nc.vector.tensor_scalar(ga_abs[:, i], ga_abs[:, i], 0.25, None, ALU.max))
                link(nc.vector.scalar_tensor_tensor(dst[:], ga_sgn[:, i], -1.0, ga_abs[:, i], ALU.add, ALU.mult))
            dve.wait_ge(ld_row, 16 * N_ROW)
            dve.wait_ge(consts, 1)
            flat = lambda t: t.rearrange("p k n -> p (k n)")
            for i in range(5):
                dve.wait_ge(wt_mm, i + 1)
                t2 = ps[3 + i % 3][:].rearrange("p (k n) -> p k n", k=CK)
                if i < 3:
                    col = (KV * C if i == 0 else (i - 1) * C)
                    nc.vector.tensor_tensor(wtmp[:], t2, eye2[:], ALU.add).then_inc(wt_ok, 1)
                    dve.wait_ge(wt_ok, i + 1)
                    link(nc.vector.tensor_copy(wkq[:, 0, :, col:col + C], wtmp[:]))
                    link(nc.vector.tensor_tensor(wkq[:, 1, :, col:col + C], wtmp[:],
                                                 f32(wkq[:, 0, :, col:col + C]), ALU.subtract))
                else:
                    nc.vector.tensor_tensor(wv[:, :, (i - 3) * C:(i - 2) * C], t2, eye2[:], ALU.add).then_inc(wt_ok, 1)
            dve.wait_ge(wt_mm, 6)
            link(nc.vector.tensor_copy(lnb_rows[:], lnb_col[:].unsqueeze(2).broadcast_to([P, CK, P])))
            nc.vector.tensor_copy(flat(wtmp[:]), ps[5][:]).then_inc(wt_ok, 1)
            dve.wait_ge(bo_mm, 1)
            link(nc.vector.tensor_tensor(bo_row[:], ps[6][:, 0:C], bo_row[:], ALU.add))
            link(nc.vector.tensor_tensor(bo_row[:], bo_row[:], gate_a[:], ALU.mult))
            for k in range(CK):
                link(nc.vector.scalar_tensor_tensor(wtmp[:, k], wtmp[:, k], lng_col[:, k:k + 1], gate_a[:],
                                                    ALU.mult, ALU.mult))
            link(nc.vector.tensor_copy(wo[:, 0], wtmp[:]))
            link(nc.vector.tensor_tensor(wo[:, 1], wtmp[:], f32(wo[:, 0]), ALU.subtract))
            link(nc.vector.tensor_copy(gw[:, 0], gw_raw[:]))
            link(nc.vector.tensor_tensor(gw[:, 1], gw_raw[:], f32(gw[:, 0]), ALU.subtract))
            link(nc.vector.tensor_scalar(sbd_row[:], sbd_row[:], 0.1, None, ALU.mult))
            with dve.Fori(0, NG) as g:
                wait(dve, x_in, 16 * g + 16)
                for t in range(TG):
                    nc.vector.bn_stats(bn0[:, bass.ds(TG * g + t, 1)].rearrange("p a n -> p (a n)"),
                                       X[:, bass.ds(TG * g + t, 1), :].rearrange("p a c -> p (a c)")
                                       ).then_inc(x_stat, 1)
            dve.wait_ge(x_stat, NT)
            for t in range(NT):
                last = nc.vector.bn_aggr(mv1[:, t], bn0[:, t])
            link(last)
            link(nc.vector.tensor_scalar(rs1[:, 1], mv1[:, :, 1], EPS_LN, None, ALU.add))
            rsqrt(link, rs1[:, 2], rs1[:, 1], rs1[:, 0])

    b1 = Map(nc, p1w.at)
    z1 = b1("z1", [P, TG, C], F32)
    h1 = b1("h1", [P, 2, TG, C + 1], F32)
    hT = b1("hT", [P, 2, 2, CK, HALF], F32R)
    kraw = b1("kraw", [P, 2, KV * C], F32)
    ks = b1("ks", [P, TG, KV * C], F32)
    ksq = b1("ksq", [P, 2, KV * C], F32)
    kn = b1("kn", [P, TG, KV * C], F32)
    kss = b1("kss", [P, TG, KV * HEADS], F32)
    krs = b1("krs", [P, TG, KV * HEADS], F32)
    kinv = b1("kinv", [P, TG, KV * HEADS], F32)
    ktmp = b1("ktmp", [P, TG, KV * HEADS], F32)
    zero_w = b1("zero_w", [P, C + 1], F32)
    assert b1.at <= SRAW and st.at <= SRAW

    names = ("z1_ok", "h1_ml", "h1_ok", "tp1", "hi1", "lo1", "k_mm", "k_ev", "k_silu", "k_sq", "k_red",
             "k_inv", "k_n", "g_mm", "q_mm", "q_silu", "h1_one", "sw_hi", "sw_lo")
    (z1_ok, h1_ml, h1_ok, tp1, hi1, lo1, k_mm, k_ev, k_silu, k_sq, k_red, k_inv, k_n, g_mm, q_mm, q_silu,
     h1_one, sw_hi, sw_lo) = [sem(n) for n in names]
    later = lambda g, n: not isinstance(g, int) or g >= n

    def groups(eng, body):
        body(0, 0, True)
        body(1, 1, True)
        with eng.Fori(1, NG // 2 - 1) as i:
            body(2 * i, 0, True)
            body(2 * i + 1, 1, True)
        body(NG - 2, 0, True)
        body(NG - 1, 1, False)

    with ExitStack() as mem:
        psG = mem.enter_context(nc.psum_tensor("psG", [P, 4, HALF], F32))
        with ExitStack() as mem1, nc.Block() as block:
            psK = mem1.enter_context(nc.psum_tensor("psK", [P, HALF], F32))
            psQ = mem1.enter_context(nc.psum_tensor("psQ", [P, HALF], F32))
            psT = mem1.enter_context(nc.psum_tensor("psT", [P, 2, HALF], F32))

            @block.vector
            def _(dve):
                def normalise(g, t):
                    if later(g, 1):
                        dve.wait_ge(h1_ok, TG * (g - 1) + t + 1)
                    n = TG * g + t
                    nc.vector.tensor_scalar(z1[:, t], X[:, bass.ds(n, 1), :].rearrange("p a c -> p (a c)"),
                                            mv1[:, bass.ds(n, 1), 0], rs1[:, 2, bass.ds(n, 1)],
                                            ALU.subtract, ALU.mult).then_inc(z1_ok, 1)

                def low(g, q, k):
                    dve.wait_ge(hi1, 2 * g + k + 1)
                    nc.vector.tensor_tensor(hT[:, q, 1, k], psT[:, k], f32(hT[:, q, 0, k]), ALU.subtract
                                            ).then_inc(lo1, 1)

                def unit(f, t):
                    if later(f, 1):
                        dve.wait_ge(g_mm, TG * (f - 1) + t + 1)
                    nc.vector.scalar_tensor_tensor(
                        kn[:, t].rearrange("p (h d) -> p h d", d=D),
                        ks[:, t].rearrange("p (h d) -> p h d", d=D), 0.5,
                        kinv[:, t].unsqueeze(2).broadcast_to([P, KV * HEADS, D]), ALU.add, ALU.mult
                    ).then_inc(k_n, 1)

                nc.vector.memset(h1[:, :, :, C:C + 1], 1.0).then_inc(h1_one, 1)
                nc.vector.memset(zero_w[:], 0.0).then_inc(h1_one, 1)
                for t in range(TG):
                    normalise(0, t)
                low(0, 0, 0)
                low(0, 0, 1)

                def body(g, q, more):
                    prev = later(g, 1)

                    def evac(t):
                        dve.wait_ge(k_mm, TG * g + t + 1)
                        if prev or t >= 2:
                            dve.wait_ge(k_silu, TG * g + t - 1)
                        nc.vector.tensor_tensor(kraw[:, t % 2], psK[:], bk_row[:], ALU.add).then_inc(k_ev, 1)

                    def reduce(t):
                        dve.wait_ge(k_sq, TG * g + t + 1)
                        nc.vector.tensor_reduce(kss[:, t], ksq[:, t % 2].rearrange("p (h d) -> p h d", d=D),
                                                AX.X, ALU.add).then_inc(k_red, 1)

                    n = [0]
                    STEPS = RSQRT + 3

                    def link(ins):
                        n[0] += 1
                        ins.then_inc(k_inv, 1)
                        dve.wait_ge(k_inv, STEPS * g + n[0])

                    def between(n):
                        if more and n >= 1:
                            low(g + 1, 1 - q, n - 1)

                    flat = lambda t: t[:].rearrange("p t h -> p (t h)")
                    if prev:
                        unit(g - 1, 0)
                    evac(0)
                    if prev:
                        unit(g - 1, 1)
                        unit(g - 1, 2)
                    evac(1)
                    if prev:
                        unit(g - 1, 3)
                    reduce(0)
                    evac(2)
                    reduce(1)
                    if more:
                        normalise(g + 1, 0)
                        normalise(g + 1, 1)
                    evac(3)
                    if more:
                        normalise(g + 1, 2)
                        normalise(g + 1, 3)
                    reduce(2)
                    reduce(3)
                    dve.wait_ge(k_red, TG * g + TG)
                    rsqrt(link, flat(krs), flat(kss), flat(ktmp), between)
                    link(nc.vector.tensor_scalar(flat(kss), flat(krs), EPS, 1.0, ALU.mult, ALU.add))
                    link(nc.vector.reciprocal(flat(ktmp), flat(kss)))
                    link(nc.vector.tensor_tensor(flat(kinv), flat(krs), flat(ktmp), ALU.mult))
                    assert n[0] == STEPS

                groups(dve, body)
                for t in range(TG):
                    unit(NG - 1, t)

            @block.gpsimd
            def _(pool):
                def modulate(g, q, t):
                    wait(pool, z1_ok, TG * g + t + 1)
                    nc.gpsimd.tensor_tensor(z1[:, t], z1[:, t], scale_a[:], ALU.mult).then_inc(h1_ml, 1)
                    wait(pool, h1_ml, TG * g + t + 1)
                    if later(g, 2):
                        wait(pool, g_mm, TG * (g - 2) + t + 1)
                    nc.gpsimd.tensor_tensor(h1[:, q, t, 0:C], z1[:, t], shift_a[:], ALU.add).then_inc(h1_ok, 1)

                for t in range(TG):
                    modulate(0, 0, t)

                def body(g, q, more):
                    for t in range(TG):
                        if more:
                            modulate(g + 1, 1 - q, t)
                        if isinstance(g, int) and g == 1:
                            split(t)

                def split(n):
                    a, k = n // 2, n % 2
                    src = sraw[:, a, k]
                    w = (su[:, :, k], sd[:, :, k * MK // 2:(k + 1) * MK // 2].rearrange("p b m n -> p b (m n)"))[a]
                    if n == 0:
                        pool.wait_ge(ld_sh, 32)
                    nc.gpsimd.tensor_copy(w[:, 0], src).then_inc(sw_hi, 1)
                    pool.wait_ge(sw_hi, n + 1)
                    nc.gpsimd.tensor_tensor(w[:, 1], src, f32(w[:, 0]), ALU.subtract).then_inc(sw_lo, 1)

                groups(pool, body)

            @block.scalar
            def _(act):
                def high(g, q, k):
                    act.wait_ge(tp1, 2 * g + k + 1)
                    nc.scalar.copy(hT[:, q, 0, k], psT[:, k]).then_inc(hi1, 1)

                high(0, 0, 0)
                high(0, 0, 1)

                def body(g, q, more):
                    def key(t):
                        act.wait_ge(k_ev, TG * g + t + 1)
                        if later(g, 1):
                            act.wait_ge(k_n, TG * (g - 1) + t + 1)
                        nc.scalar.activation(ks[:, t], kraw[:, t % 2], ACT.Silu).then_inc(k_silu, 1)
                        act.wait_ge(k_silu, TG * g + t + 1)
                        if later(g, 1) or t >= 2:
                            act.wait_ge(k_red, TG * g + t - 1)
                        nc.scalar.activation(ksq[:, t % 2], ks[:, t], ACT.Square, bias=expo[:, 0, 0:1]).then_inc(k_sq, 1)

                    def query(k):
                        act.wait_ge(q_mm, CK * g + k + 1)
                        nc.scalar.activation(qT[:, k, bass.ds(HALF * g, HALF)], psQ[:], ACT.Silu,
                                             bias=bq_col[:, k:k + 1]).then_inc(q_silu, 1)

                    for t in range(TG):
                        key(t)
                    query(0)
                    if more:
                        high(g + 1, 1 - q, 0)
                        high(g + 1, 1 - q, 1)
                    query(1)

                groups(act, body)

            @block.tensor
            def _(pe):
                pe.wait_ge(h1_one, 2)

                def turn(g, q, k):
                    if k == 0:
                        pe.wait_ge(h1_ok, TG * g + TG)
                    for t in range(TG):
                        mm = nc.tensor.transpose(psT[:, k, t * P:(t + 1) * P], h1[:, q, t, k * P:(k + 1) * P], ident[:])
                    mm.then_inc(tp1, 1)

                def keys(g, q, t):
                    if t == 0:
                        pe.wait_ge(lo1, 2 * g + 2)
                    if later(g, 1) or t:
                        pe.wait_ge(k_ev, TG * g + t)
                    n = 0
                    for k in range(CK):
                        for a, b in ((0, 0), (0, 1), (1, 0)):
                            mm = nc.tensor.matmul(psK[:], hT[:, q, a, k, t * P:(t + 1) * P],
                                                  wkq[:, b, k, 0:KV * C], start=(n == 0), stop=(n == 3 * CK - 1))
                            n += 1
                    mm.then_inc(k_mm, 1)

                def queries(g, q, o):
                    if later(g, 1) or o:
                        pe.wait_ge(q_silu, CK * g + o)
                    n = 0
                    for k in range(CK):
                        for a, b in ((0, 0), (0, 1), (1, 0)):
                            col = KV * C + o * P
                            mm = nc.tensor.matmul(psQ[:], wkq[:, b, k, col:col + P], hT[:, q, a, k],
                                                  start=(n == 0), stop=(n == 3 * CK - 1))
                            n += 1
                    mm.then_inc(q_mm, 1)

                def sums(f, r, t):
                    pe.wait_ge(k_n, TG * f + t + 1)
                    for j in range(4):
                        mm = nc.tensor.matmul(psG[:, j, 0:C + 1], kn[:, t, j * P:(j + 1) * P], h1[:, r, t],
                                              start=False, stop=False, skip_group_check=True)
                    mm.then_inc(g_mm, 1)

                for j in range(4):
                    nc.tensor.matmul(psG[:, j, 0:C + 1], zero_w[:, 0:P], zero_w[:],
                                     start=True, stop=False, skip_group_check=True)
                turn(0, 0, 0)
                turn(0, 0, 1)

                def body(g, q, more):
                    for t in range(TG):
                        keys(g, q, t)
                        if later(g, 1):
                            sums(g - 1, 1 - q, t)
                    queries(g, q, 0)
                    if more:
                        turn(g + 1, 1 - q, 0)
                        turn(g + 1, 1 - q, 1)
                    queries(g, q, 1)

                groups(pe, body)
                for t in range(TG):
                    sums(NG - 1, 1, t)

        s1 = Map(nc, p1w.at)
        Gs = s1("Gs", [P, 4, C + 1], F32)
        GT = s1("GT", [P, 4, CK, P], F32)
        sts = s1("sts", [P, 4, P], F32)
        g_cp, g_tp, g_tc, s_mm, s_dve = [sem(n) for n in ("g_cp", "g_tp", "g_tc", "s_mm", "s_dve")]
        with ExitStack() as mem1, nc.Block() as block:
            psA = mem1.enter_context(nc.psum_tensor("psA", [P, 2, HALF], F32))
            psS = mem1.enter_context(nc.psum_tensor("psS", [P, HALF], F32))

            @block.vector
            def _(dve):
                for j in range(4):
                    nc.vector.tensor_copy(Gs[:, j], psG[:, j, 0:C + 1]).then_inc(g_cp, 1)
                for b in range(2):
                    dve.wait_ge(g_tp, b + 1)
                    nc.vector.tensor_copy(GT[:, 2 * b:2 * b + 2].rearrange("p j k n -> p (j k n)"), psA[:, b]
                                          ).then_inc(g_tc, 1)
                dve.wait_ge(s_mm, 1)
                dve.wait_ge(g_cp, 4)
                for j in range(4):
                    kv, hf = j // 2, j % 2
                    nc.vector.scalar_tensor_tensor(sts[:, j], bv_row[:, kv * C + hf * P:kv * C + hf * P + P],
                                                   Gs[:, j, C:C + 1], psS[:, j * P:(j + 1) * P],
                                                   ALU.mult, ALU.add).then_inc(s_dve, 1)
                dve.wait_ge(s_dve, 4)
                for hf in range(CK):
                    nc.vector.scalar_tensor_tensor(sts[:, hf], sts[:, hf], float(N) ** -KV, sts[:, 2 + hf],
                                                   ALU.mult, ALU.mult).then_inc(s_dve, 1)
                dve.wait_ge(s_dve, 6)
                for hf in range(CK):
                    nc.vector.tensor_tensor(state[:, hf], sts[:, hf], blocks[:], ALU.mult)

            @block.tensor
            def _(pe):
                for j in range(4):
                    pe.wait_ge(g_cp, j + 1)
                    for k in range(CK):
                        at = (j % 2) * C + k * P
                        mm = nc.tensor.transpose(psA[:, j // 2, at:at + P], Gs[:, j, k * P:(k + 1) * P], ident[:])
                    if j % 2:
                        mm.then_inc(g_tp, 1)
                pe.wait_ge(g_tc, 2)
                for j in range(4):
                    kv, hf = j // 2, j % 2
                    for k in range(CK):
                        at = kv * C + hf * P
                        mm = nc.tensor.matmul(psS[:, j * P:(j + 1) * P], GT[:, j, k], wv[:, k, at:at + P],
                                              start=(k == 0), stop=(k == CK - 1))
                mm.then_inc(s_mm, 1)

    b2 = Map(nc, after_q)
    q5 = b2("q5", [P, CK, HALF], F32)
    qsq = b2("qsq", [P, CK, HALF], F32)
    nq = b2("nq", [P, 4, TG * HEADS], F32)
    oz = b2("oz", [P, TG, C], F32)
    bn2 = b2("bn2", [P, 2, TG, 6], F32)
    mv2 = b2("mv2", [P, 2, TG, 2], F32)
    rs2 = b2("rs2", [P, 2, 2, TG], F32)
    zT = b2("zT", [P, 2, CK, HALF], F32R)
    z2 = b2("z2", [P, TG, C], F32)
    h2 = b2("h2", [P, 2, TG, C], F32)
    h2T = b2("h2T", [P, 2, 2, CK, HALF], F32R)
    gf = b2("gf", [P, 2, HALF], F32)
    ghi = b2("ghi", [P, 3, HALF], F32R)
    glo = b2("glo", [P, 3, HALF], F32R)
    sh = b2("sh", [P, TG, C], F32)
    lg = b2("lg", [P, TG, E], F32)
    sc = b2("sc", [P, TG, E], F32)
    mx = b2("mx", [P, TG, E], F32)
    ix = b2("ix", [P, TG, E], U32)
    ixf = b2("ixf", [P, TG, TOPK], F32)
    oh = b2("oh", [P, TOPK, TG, E], F32)
    ohb = b2("ohb", [P, TG, E], BF16)
    rk = b2("rk", [P, TG, E], F32)
    rk2 = b2("rk2", [P, TG, E], F32)
    pf = b2("pf", [P, TG, TOPK], F32)
    post = b2("post", [P, 2, TG, TOPK], U32)
    dn = b2("dn", [P, 2, TG], F32)

    names = ("q_pre", "nm_mm", "nm_ev", "rq_ok", "o_mm", "o_ev", "stat2", "self2", "rse2",
             "rstd2", "zo_ok", "tz_mm", "tz_hi", "tz_lo", "xb_ok", "a_mm", "x_ev", "z2_ok", "h2_ml", "h2_ok",
             "th_mm", "th_hi", "th_lo", "gt_mm", "gt_ev", "gt_sc", "rt_dve", "rt_oh", "rt_mm", "pos_ok",
             "scat", "u_mm", "u_g", "u_hi", "u_lo", "d_mm", "sh_ev", "sh_st")
    (q_pre, nm_mm, nm_ev, rq_ok, o_mm, o_ev, stat2, self2, rse2, rstd2, zo_ok, tz_mm, tz_hi,
     tz_lo, xb_ok, a_mm, x_ev, z2_ok, h2_ml, h2_ok, th_mm, th_hi, th_lo, gt_mm, gt_ev, gt_sc, rt_dve, rt_oh,
     rt_mm, pos_ok, scat, u_mm, u_g, u_hi, u_lo, d_mm, sh_ev, sh_st) = [sem(n) for n in names]

    def staggered(eng, body):
        body(0, 0, True, False)
        body(1, 1, True, True)
        body(2, 0, True, True)
        with eng.Fori(1, NG // 2 - 1) as i:
            body(2 * i + 1, 1, True, True)
            body(2 * i + 2, 0, True, True)
        body(NG - 1, 1, True, True)
        body(NG, 0, False, True)

    PASSES = ((0, 0), (0, 1), (1, 0))

    with ExitStack() as mem, nc.Block() as block:
        psU = mem.enter_context(nc.psum_tensor("psU", [P, 2, HALF], F32))
        psY = mem.enter_context(nc.psum_tensor("psY", [P, 2, HALF], F32))
        psZ = mem.enter_context(nc.psum_tensor("psZ", [P, 2, HALF], F32))
        psO = mem.enter_context(nc.psum_tensor("psO", [P, HALF], F32))
        psM = mem.enter_context(nc.psum_tensor("psM", [P, HALF], F32))
        NORM, GATE, RANK, TOTAL = 0, 64, 96, 128

        @block.tensor
        def _(pe):
            def body(g, q, att_on, ffn_on):
                f, r = g - 1, 1 - q

                def norms():
                    pe.wait_ge(q_pre, 2 * g + 2)
                    if later(g, 2):
                        pe.wait_ge(rt_dve, 18 * g - 18)
                    for t in range(TG):
                        for k in range(CK):
                            at = NORM + t * HEADS + k * (P // D)
                            mm = nc.tensor.matmul(psM[:, at:at + P // D], qsq[:, k, t * P:(t + 1) * P], heads[:],
                                                  start=True, stop=True)
                    mm.then_inc(nm_mm, 1)

                def outs(h):
                    if later(g, 1) or h:
                        pe.wait_ge(o_ev, 2 * g + 1) if h else pe.wait_ge(x_ev, 2 * g)
                    for t in (2 * h, 2 * h + 1):
                        for k in range(CK):
                            at = (t % 2) * C + k * P
                            mm = nc.tensor.matmul(psO[:, at:at + P], q5[:, k, t * P:(t + 1) * P], state[:, k],
                                                  start=True, stop=True)
                    mm.then_inc(o_mm, 1)

                def turn_z(k):
                    pe.wait_ge(zo_ok, TG * g + TG)
                    if later(g, 1):
                        pe.wait_ge(th_lo, 2 * g - 1 + k)
                    for t in range(TG):
                        mm = nc.tensor.transpose(psZ[:, k, t * P:(t + 1) * P], oz[:, t, k * P:(k + 1) * P], ident[:])
                    mm.then_inc(tz_mm, 1)

                def attend(h):
                    pe.wait_ge(x_ev, 2 * g + 1) if h else pe.wait_ge(o_ev, 2 * g + 2)
                    if not h:
                        pe.wait_ge(tz_lo, 2 * g + 2)
                    for t in (2 * h, 2 * h + 1):
                        n = 0
                        for k in range(CK):
                            for a, b in PASSES:
                                mm = nc.tensor.matmul(psO[:, (t % 2) * C:(t % 2 + 1) * C],
                                                      zT[:, a, k, t * P:(t + 1) * P], wo[:, b, k],
                                                      start=(n == 0), stop=(n == 5))
                                n += 1
                    mm.then_inc(a_mm, 1)

                def turn_h(k):
                    pe.wait_ge(h2_ok, TG * g + TG)
                    pe.wait_ge(tz_lo, 2 * g + 1 + k)
                    for t in range(TG):
                        mm = nc.tensor.transpose(psZ[:, k, t * P:(t + 1) * P], h2[:, q, t, k * P:(k + 1) * P], ident[:])
                    mm.then_inc(th_mm, 1)

                def gate():
                    pe.wait_ge(th_lo, 2 * f + 2)
                    if att_on:
                        pe.wait_ge(nm_ev, g + 1)
                    for t in range(TG):
                        n = 0
                        for k in range(CK):
                            for a, b in PASSES:
                                mm = nc.tensor.matmul(psM[:, GATE + t * E:GATE + (t + 1) * E],
                                                      h2T[:, r, a, k, t * P:(t + 1) * P], gw[:, b, k],
                                                      start=(n == 0), stop=(n == 5))
                                n += 1
                    mm.then_inc(gt_mm, 1)

                def rank():
                    pe.wait_ge(rt_oh, f + 1)
                    nc.tensor.matmul(psM[:, RANK:RANK + TG * E], tri[:], ohb[:].rearrange("p t e -> p (t e)"),
                                     start=True, stop=False, skip_group_check=True)
                    for t in range(TG - 1):
                        n = TG - 1 - t
                        nc.tensor.matmul(psM[:, RANK + (t + 1) * E:RANK + TG * E].rearrange("p (t e) -> p t e", e=E),
                                         one_b[:], ohb[:, t:t + 1].broadcast_to([P, n, E]), start=False,
                                         stop=(t == TG - 2), skip_group_check=True)
                    for t in range(TG):
                        mm = nc.tensor.matmul(psM[:, TOTAL:TOTAL + E], one_b[:], ohb[:, t], start=(t == 0),
                                              stop=(t == TG - 1))
                    mm.then_inc(rt_mm, 1)

                def up(m):
                    if later(f, 1) or m >= 2:
                        pe.wait_ge(u_g, MK * f + m - 1)
                    if m == 0:
                        pe.wait_ge(th_lo, 2 * f + 2)
                    n = 0
                    for k in range(CK):
                        for a, b in PASSES:
                            mm = nc.tensor.matmul(psU[:, m % 2], su[:, b, k, m * P:(m + 1) * P], h2T[:, r, a, k],
                                                  start=(n == 0), stop=(n == 5))
                            n += 1
                    mm.then_inc(u_mm, 1)

                def down(m):
                    pe.wait_ge(u_lo, MK * f + m + 1)
                    if m == 0 and later(f, 1):
                        pe.wait_ge(sh_ev, 2 * f)
                    for t in range(TG):
                        for n, (a, b) in enumerate(PASSES):
                            lhs = (ghi, glo)[a][:, m % 3, t * P:(t + 1) * P]
                            mm = nc.tensor.matmul(psY[:, t // 2, (t % 2) * C:(t % 2 + 1) * C], lhs, sd[:, b, m],
                                                  start=(m == 0 and t % 2 == 0 and n == 0),
                                                  stop=(m == MK - 1 and n == 2), skip_group_check=True)
                    mm.then_inc(d_mm, 1)

                def chunk(m):
                    if ffn_on:
                        if m < MK:
                            up(m)
                        if m >= 2:
                            down(m - 2)

                if att_on:
                    norms()
                    outs(0)
                if ffn_on:
                    gate()
                chunk(0)
                if att_on:
                    outs(1)
                chunk(1)
                chunk(2)
                if ffn_on:
                    rank()
                if att_on:
                    turn_z(0)
                    turn_z(1)
                chunk(3)
                if att_on:
                    attend(0)
                chunk(4)
                if att_on:
                    attend(1)
                for m in range(5, MK + 2):
                    chunk(m)
                if att_on:
                    turn_h(0)
                    turn_h(1)

            staggered(pe, body)

        @block.scalar
        def _(act):
            def body(g, q, att_on, ffn_on):
                f, r = g - 1, 1 - q

                def queries():
                    if later(g, 1):
                        act.wait_ge(o_mm, 2 * g)
                    src = qT[:, :, bass.ds(HALF * g, HALF)]
                    nc.scalar.activation(q5[:], src, ACT.Identity, bias=expo[:, 0, 0:1]).then_inc(q_pre, 1)
                    nc.scalar.activation(qsq[:], src, ACT.Square, bias=expo[:, 0, 0:1]).then_inc(q_pre, 1)

                def high(mm, out, dst, k):
                    act.wait_ge(mm, 2 * g + k + 1)
                    nc.scalar.copy(dst[:, 0, k], psZ[:, k]).then_inc(out, 1)

                def gelu(m):
                    act.wait_ge(u_mm, MK * f + m + 1)
                    if later(f, 1) or m >= 2:
                        act.wait_ge(u_lo, MK * f + m - 1)
                    nc.scalar.activation(gf[:, m % 2], psU[:, m % 2], ACT.Gelu, bias=sbu[:, m:m + 1]).then_inc(u_g, 1)
                    act.wait_ge(u_g, MK * f + m + 1)
                    if later(f, 1) or m >= 3:
                        act.wait_ge(d_mm, MK * f + m - 2)
                    nc.scalar.copy(ghi[:, m % 3], gf[:, m % 2]).then_inc(u_hi, 1)

                def score():
                    act.wait_ge(gt_ev, f + 1)
                    nc.scalar.activation(sc[:], lg[:], ACT.Sigmoid).then_inc(gt_sc, 1)

                if att_on and isinstance(g, int) and g == 0:
                    queries()
                if ffn_on:
                    score()
                    gelu(0)
                    gelu(1)
                    gelu(2)
                if att_on:
                    high(tz_mm, tz_hi, zT, 0)
                    high(tz_mm, tz_hi, zT, 1)
                if ffn_on:
                    for m in range(3, MK):
                        gelu(m)
                if att_on:
                    if not (isinstance(g, int) and g == NG - 1):
                        g2 = g + 1
                        act.wait_ge(o_mm, 2 * g2)
                        src = qT[:, :, bass.ds(HALF * g2, HALF)]
                        nc.scalar.activation(q5[:], src, ACT.Identity, bias=expo[:, 0, 0:1]).then_inc(q_pre, 1)
                        nc.scalar.activation(qsq[:], src, ACT.Square, bias=expo[:, 0, 0:1]).then_inc(q_pre, 1)
                    high(th_mm, th_hi, h2T[:, q], 0)
                    high(th_mm, th_hi, h2T[:, q], 1)

            staggered(act, body)

        @block.vector
        def _(dve):
            def body(g, q, att_on, ffn_on):
                f, r = g - 1, 1 - q

                def tile(t):
                    return X[:, bass.ds(TG * g + t, 1), :].rearrange("p a c -> p (a c)")

                def norm_read():
                    dve.wait_ge(nm_mm, g + 1)
                    nc.vector.tensor_copy(nq[:, 0], psM[:, NORM:NORM + TG * HEADS]).then_inc(nm_ev, 1)

                def norm_inverse():
                    n = [0]
                    STEPS = RSQRT + 3

                    def link(ins):
                        n[0] += 1
                        ins.then_inc(rq_ok, 1)
                        dve.wait_ge(rq_ok, STEPS * g + n[0])

                    dve.wait_ge(nm_ev, g + 1)
                    rsqrt(link, nq[:, 2], nq[:, 0], nq[:, 3])
                    link(nc.vector.tensor_scalar(nq[:, 0], nq[:, 2], EPS, 1.0, ALU.mult, ALU.add))
                    link(nc.vector.reciprocal(nq[:, 3], nq[:, 0]))
                    link(nc.vector.tensor_tensor(nq[:, 1], nq[:, 2], nq[:, 3], ALU.mult))
                    assert n[0] == STEPS

                def out_read(h):
                    dve.wait_ge(o_mm, 2 * g + h + 1)
                    inv = nq[:, 1, 2 * h * HEADS:(2 * h + 2) * HEADS].unsqueeze(2).broadcast_to([P, 2 * HEADS, D])
                    nc.vector.tensor_tensor(oz[:, 2 * h:2 * h + 2].rearrange("p t (h d) -> p (t h) d", d=D),
                                            psO[:].rearrange("p (h d) -> p h d", d=D), inv, ALU.mult
                                            ).then_inc(o_ev, 1)
                    wait(dve, o_ev, 2 * g + h + 1)
                    for t in (2 * h, 2 * h + 1):
                        nc.vector.bn_stats(bn2[:, 0, t], oz[:, t]).then_inc(self2, 1)
                        wait(dve, self2, 8 * g + t + 1)
                        nc.vector.bn_aggr(mv2[:, 0, t], bn2[:, 0, t]).then_inc(stat2, 1)

                def out_norm():
                    dve.wait_ge(rstd2, 2 * g + 1)
                    for t in range(TG):
                        nc.vector.tensor_scalar(oz[:, t], oz[:, t], mv2[:, 0, t, 0:1], rs2[:, 0, 1, t:t + 1],
                                                ALU.subtract, ALU.mult).then_inc(zo_ok, 1)

                def low_z(k):
                    dve.wait_ge(tz_hi, 2 * g + k + 1)
                    nc.vector.tensor_tensor(zT[:, 1, k], psZ[:, k], f32(zT[:, 0, k]), ALU.subtract).then_inc(tz_lo, 1)

                def x_read(h):
                    dve.wait_ge(a_mm, 2 * g + h + 1)
                    dve.wait_ge(xb_ok, g + 1)
                    pair = X[:, bass.ds(TG * g + 2 * h, 2), :].rearrange("p t c -> p (t c)")
                    nc.vector.tensor_tensor(pair, psO[:], pair, ALU.add).then_inc(x_ev, 1)
                    wait(dve, x_ev, 2 * g + h + 1)
                    for t in (2 * h, 2 * h + 1):
                        nc.vector.bn_stats(bn2[:, 1, t], tile(t)).then_inc(self2, 1)
                        wait(dve, self2, 8 * g + TG + t + 1)
                        nc.vector.bn_aggr(mv2[:, 1, t], bn2[:, 1, t]).then_inc(stat2, 1)

                def x_norm():
                    dve.wait_ge(rstd2, 2 * g + 2)
                    if later(g, 1):
                        dve.wait_ge(h2_ok, TG * g)
                    for t in range(TG):
                        nc.vector.tensor_scalar(z2[:, t], tile(t), mv2[:, 1, t, 0:1], rs2[:, 1, 1, t:t + 1],
                                                ALU.subtract, ALU.mult).then_inc(z2_ok, 1)

                def low_h(k):
                    dve.wait_ge(th_hi, 2 * g + k + 1)
                    nc.vector.tensor_tensor(h2T[:, q, 1, k], psZ[:, k], f32(h2T[:, q, 0, k]), ALU.subtract
                                            ).then_inc(th_lo, 1)

                def low_g(m):
                    if ffn_on:
                        dve.wait_ge(u_hi, MK * f + m + 1)
                        nc.vector.tensor_tensor(glo[:, m % 3], gf[:, m % 2], f32(ghi[:, m % 3]), ALU.subtract
                                                ).then_inc(u_lo, 1)

                ROUTE = 18
                n = [0]

                def step(ins):
                    n[0] += 1
                    ins.then_inc(rt_dve, 1)
                    wait(dve, rt_dve, ROUTE * f + n[0])

                def gate_read():
                    dve.wait_ge(gt_mm, f + 1)
                    nc.vector.tensor_tensor(lg[:], psM[:, GATE:GATE + TG * E].rearrange("p (t e) -> p t e", e=E),
                                            gb_row[:].unsqueeze(1).broadcast_to([P, TG, E]), ALU.add
                                            ).then_inc(gt_ev, 1)

                def choose():
                    wait(dve, gt_sc, f + 1)
                    for t in range(TG):
                        step(nc.vector.max(mx[:, t], sc[:, t]))
                    for t in range(TG):
                        step(nc.vector.max_index(ix[:, t], mx[:, t], sc[:, t]))
                    step(nc.vector.tensor_copy(ixf[:], ix[:, :, 0:TOPK]))
                    for k in range(TOPK):
                        step(nc.vector.tensor_tensor(oh[:, k], iota_e[:].unsqueeze(1).broadcast_to([P, TG, E]),
                                                     ixf[:, :, k:k + 1].broadcast_to([P, TG, E]), ALU.is_equal))
                    nc.vector.tensor_tensor(ohb[:], oh[:, 0], oh[:, 1], ALU.add).then_inc(rt_oh, 1)
                    step(nc.vector.tensor_tensor(dn[:, 0], mx[:, :, 0], mx[:, :, 1], ALU.add))
                    step(nc.vector.tensor_scalar(dn[:, 0], dn[:, 0], EPS, None, ALU.add))
                    step(nc.vector.reciprocal(dn[:, 1], dn[:, 0]))
                    nc.vector.scalar_tensor_tensor(wtop[:, bass.ds(TG * f, TG), :], mx[:, :, 0:TOPK], 0.1,
                                                   dn[:, 1].unsqueeze(2).broadcast_to([P, TG, TOPK]),
                                                   ALU.mult, ALU.mult)

                def place():
                    dve.wait_ge(rt_mm, f + 1)
                    step(nc.vector.tensor_tensor(rk[:], psM[:, RANK:RANK + TG * E].rearrange("p (t e) -> p t e", e=E),
                                                 run[:].unsqueeze(1).broadcast_to([P, TG, E]), ALU.add))
                    step(nc.vector.tensor_tensor(rk[:], rk[:], reg_e[:].unsqueeze(1).broadcast_to([P, TG, E]), ALU.add))
                    step(nc.vector.tensor_tensor(run[:], psM[:, TOTAL:TOTAL + E], run[:], ALU.add))
                    for k in range(TOPK):
                        nc.vector.tensor_tensor(rk2[:], rk[:], oh[:, k], ALU.mult).then_inc(pf_ok, 1)
                        dve.wait_ge(pf_ok, 2 * TOPK * f + 2 * k + 1)
                        nc.vector.tensor_reduce(pf[:, :, k], rk2[:], AX.X, ALU.add).then_inc(pf_ok, 1)
                        dve.wait_ge(pf_ok, 2 * TOPK * f + 2 * k + 2)
                    step(nc.vector.tensor_copy(pos[:, bass.ds(TG * f, TG), :], pf[:]))
                    assert n[0] == ROUTE
                    nc.vector.tensor_copy(post[:, r], pf[:]).then_inc(pos_ok, 1)

                def shared_read():
                    dve.wait_ge(d_mm, MK * f + MK)
                    if later(f, 1):
                        dve.wait_ge(sh_st, 16 * f)
                    for h in range(2):
                        nc.vector.scalar_tensor_tensor(sh[:, 2 * h:2 * h + 2],
                                                       psY[:, h].rearrange("p (t c) -> p t c", c=C), 0.1,
                                                       sbd_row[:].unsqueeze(1).broadcast_to([P, 2, C]),
                                                       ALU.mult, ALU.add).then_inc(sh_ev, 1)

                if att_on:
                    norm_read()
                if ffn_on:
                    gate_read()
                if att_on:
                    norm_inverse()
                    out_read(0)
                low_g(0)
                if ffn_on:
                    choose()
                if att_on:
                    out_read(1)
                low_g(1)
                if att_on:
                    out_norm()
                low_g(2)
                if ffn_on:
                    place()
                if att_on:
                    low_z(0)
                    low_z(1)
                low_g(3)
                if att_on:
                    x_read(0)
                low_g(4)
                if att_on:
                    x_read(1)
                low_g(5)
                if att_on:
                    x_norm()
                low_g(6)
                low_g(7)
                if ffn_on:
                    shared_read()
                if att_on:
                    low_h(0)
                    low_h(1)

            pf_ok = sem("pf_ok")
            staggered(dve, body)

        @block.gpsimd
        def _(pool):
            def body(g, q, att_on, ffn_on):
                f, r = g - 1, 1 - q

                def rstd(i):
                    wait(pool, stat2, 8 * g + TG * (i + 1))
                    nc.gpsimd.tensor_scalar(rs2[:, i, 0], mv2[:, i, :, 1], EPS_LN, None, ALU.add).then_inc(rse2, 1)
                    wait(pool, rse2, 2 * g + i + 1)
                    nc.gpsimd.tensor_tensor(rs2[:, i, 1], rs2[:, i, 0], expo[:, 1, 0:TG], ALU.pow).then_inc(rstd2, 1)

                def bias():
                    xg = X[:, bass.ds(TG * g, TG), :]
                    nc.gpsimd.tensor_tensor(xg, xg, bo_row[:].unsqueeze(1).broadcast_to([P, TG, C]), ALU.add
                                            ).then_inc(xb_ok, 1)

                def scatter():
                    wait(pool, pos_ok, f + 1)
                    for t in range(TG):
                        for k in range(TOPK):
                            nc.gpsimd.indirect_dma_start(
                                out=hs[:, :], out_offset=bass.IndirectOffsetOnAxis(ap=post[:, r, t, k:k + 1], axis=0),
                                in_=h2[:, r, t], in_offset=None).then_inc(scat, 16)

                def modulate():
                    for t in range(TG):
                        wait(pool, z2_ok, TG * g + t + 1)
                        nc.gpsimd.tensor_tensor(z2[:, t], z2[:, t], scale_b[:], ALU.mult).then_inc(h2_ml, 1)
                        wait(pool, h2_ml, TG * g + t + 1)
                        if t == 0 and later(g, 2):
                            wait(pool, th_mm, 2 * g - 2)
                        nc.gpsimd.tensor_tensor(h2[:, q, t], z2[:, t], shift_b[:], ALU.add).then_inc(h2_ok, 1)

                if later(g, 2):
                    wait(pool, scat, 16 * TG * TOPK * (g - 1))
                if att_on:
                    bias()
                    rstd(0)
                if ffn_on:
                    scatter()
                if att_on:
                    rstd(1)
                    modulate()

            staggered(pool, body)

        @block.sync
        def _(sp):
            with sp.Fori(0, NG) as f:
                sp.wait_ge(sh_ev, 2 * f + 2)
                sp.dma_start(shd_v[:, bass.ds(TG * f, TG), :], sh[:]).then_inc(sh_st, 16)
            sp.wait_ge(sh_st, 16 * NG)

    b3 = Map(nc, phase)
    slots = b3("slots", [P, 2, SLOT], F32R)
    ubias = b3("ubias", [P, 2, INNER], F32)
    dbias = b3("dbias", [P, 2, C], F32)
    raw = b3("raw", [P, 2, CK * INNER], F32)
    hin = b3("hin", [P, 2, C], F32)
    eT = b3("eT", [P, 2, 2, CK, P], F32R)
    ub = b3("ub", [P, INNER], F32)
    ge = b3("ge", [P, 2, INNER], F32)
    gTh = b3("gTh", [P, INNER], F32R)
    gTl = b3("gTl", [P, INNER], F32R)
    yb = b3("yb", [P, 2, C], F32)
    io_t = b3("io_t", [P, ETL], F32)
    io_k = b3("io_k", [P, E, NT], F32)
    tcmp = b3("tcmp", [P, E, NT], F32)
    ntl = b3("ntl", [P, E], F32)
    upto = b3("upto", [P, E, E], F32)
    tsel = b3("tsel", [P, E, E], F32)
    tend = b3("tend", [P, E], F32)
    jump = b3("jump", [P, E], F32)
    alt = b3("alt", [P, E], F32)
    gecm = b3("gecm", [P, ETL, E], F32)
    gej = b3("gej", [P, ETL, E], F32)
    tabf = b3("tabf", [P, 4, ETL], F32)
    past = b3("past", [P, NT * TOPK, E - 1], F32)
    gap = b3("gap", [P, NT * TOPK], F32)
    padf = b3("padf", [P, E], F32)
    padp = b3("padp", [P, E], U32)
    iop = b3("iop", [P, 1], F32)
    zrow = b3("zrow", [P, C], F32)

    tb_c, tb_d, tb_pool, tb_ok, pad_ok, pad_st = [sem(n) for n in (
        "tb_c", "tb_d", "tb_pool", "tb_ok", "pad_ok", "pad_st")]
    with nc.Block() as block:
        @block.gpsimd
        def _(pool):
            n = [0]

            def link(ins):
                n[0] += 1
                ins.then_inc(tb_pool, 1)
                wait(pool, tb_pool, n[0])

            link(nc.gpsimd.iota(io_t[:], [[1, ETL]], base=0, channel_multiplier=0,
                                allow_small_or_imprecise_dtypes=True))
            link(nc.gpsimd.iota(io_k[:], [[0, E], [P, NT]], base=0, channel_multiplier=0,
                                allow_small_or_imprecise_dtypes=True))
            link(nc.gpsimd.iota(iop[:], [[1, 1]], base=0, channel_multiplier=1,
                                allow_small_or_imprecise_dtypes=True))
            link(nc.gpsimd.memset(upto[:], 1.0))
            link(nc.gpsimd.affine_select(out=upto[:], in_=upto[:], compare_op=ALU.is_ge, fill=0.0, base=0,
                                         pattern=[[1, E], [-1, E]], channel_multiplier=0))
            link(nc.gpsimd.memset(alt[:], -1.0))
            av = alt[:].rearrange("p (a b) -> p a b", b=2)[:, :, 0]
            link(nc.gpsimd.memset(av, 1.0))
            nc.gpsimd.memset(zrow[:], 0.0).then_inc(tb_c, 1)
            pool.wait_ge(pad_ok, 1)
            pool.wait_ge(tb_c, 1)
            for e in range(E):
                nc.gpsimd.indirect_dma_start(out=hs[:, :],
                                             out_offset=bass.IndirectOffsetOnAxis(ap=padp[:, e:e + 1], axis=0),
                                             in_=zrow[:], in_offset=None).then_inc(pad_st, 16)
            pool.wait_ge(pad_st, 16 * E)
            pool.wait_ge(scat, 16 * TG * TOPK * NG)

        @block.vector
        def _(dve):
            n = [0]

            def link(ins):
                n[0] += 1
                ins.then_inc(tb_d, 1)
                dve.wait_ge(tb_d, n[0])

            dve.wait_ge(tb_c, 1)
            link(nc.vector.tensor_tensor(padf[:], run[:], reg_e[:], ALU.add))
            link(nc.vector.tensor_scalar(padf[:], padf[:], iop[:, 0:1], None, ALU.add))
            nc.vector.tensor_copy(padp[:], padf[:]).then_inc(pad_ok, 1)
            link(nc.vector.tensor_tensor(tcmp[:], run[:].unsqueeze(2).broadcast_to([P, E, NT]), io_k[:], ALU.is_gt))
            link(nc.vector.tensor_reduce(ntl[:], tcmp[:], AX.X, ALU.add))
            link(nc.vector.tensor_scalar(ntl[:], ntl[:], 1.0, None, ALU.max))
            link(nc.vector.tensor_tensor(tsel[:], upto[:], ntl[:].unsqueeze(1).broadcast_to([P, E, E]), ALU.mult))
            link(nc.vector.tensor_reduce(tend[:], tsel[:], AX.X, ALU.add))
            link(nc.vector.tensor_copy(etab_end[:], tend[:]))
            link(nc.vector.tensor_tensor(gecm[:], io_t[:].unsqueeze(2).broadcast_to([P, ETL, E]),
                                         tend[:].unsqueeze(1).broadcast_to([P, ETL, E]), ALU.is_ge))
            last = gecm[:, :, 0:E - 1]
            link(nc.vector.tensor_reduce(tabf[:, 0], last, AX.X, ALU.add))
            link(nc.vector.tensor_tensor(gej[:, :, 0:E - 1], last,
                                         alt[:, 0:E - 1].unsqueeze(1).broadcast_to([P, ETL, E - 1]), ALU.mult))
            link(nc.vector.tensor_reduce(tabf[:, 1], gej[:, :, 0:E - 1], AX.X, ALU.add))
            link(nc.vector.tensor_scalar(jump[:], ntl[:], -float(P), float(REG), ALU.mult, ALU.add))
            link(nc.vector.tensor_tensor(gej[:, :, 0:E - 1], last,
                                         jump[:, 0:E - 1].unsqueeze(1).broadcast_to([P, ETL, E - 1]), ALU.mult))
            link(nc.vector.tensor_reduce(tabf[:, 2], gej[:, :, 0:E - 1], AX.X, ALU.add))
            link(nc.vector.scalar_tensor_tensor(tabf[:, 2], io_t[:], float(P), tabf[:, 2], ALU.mult, ALU.add))
            first = float((E - 1) * REG)
            link(nc.vector.tensor_scalar(tabf[:, 3], gecm[:, :, E - 1], -1.0, 1.0, ALU.mult, ALU.add))
            link(nc.vector.scalar_tensor_tensor(tabf[:, 2], tabf[:, 2], -first, tabf[:, 3], ALU.add, ALU.mult))
            link(nc.vector.tensor_scalar(tabf[:, 2], tabf[:, 2], first, None, ALU.add))
            at = pos[:].rearrange("p t k -> p (t k)")
            link(nc.vector.tensor_tensor(past[:], at.unsqueeze(2).broadcast_to([P, NT * TOPK, E - 1]),
                                         reg_e[:, 1:E].unsqueeze(1).broadcast_to([P, NT * TOPK, E - 1]), ALU.is_ge))
            link(nc.vector.tensor_tensor(past[:], past[:], jump[:, 0:E - 1].unsqueeze(1).broadcast_to(
                [P, NT * TOPK, E - 1]), ALU.mult))
            link(nc.vector.tensor_reduce(gap[:], past[:], AX.X, ALU.add))
            nc.vector.tensor_tensor(ypos[:].rearrange("p t k -> p (t k)"), at, gap[:], ALU.subtract)
            nc.vector.tensor_copy(etab[:], tabf[:, 0])
            nc.vector.tensor_copy(stab[:], tabf[:, 1])
            nc.vector.tensor_copy(rtab[:], tabf[:, 2])

    up_v = up_w.rearrange("e (k p) n -> e p k n", p=P)
    down_v = down_w.rearrange("e (k p) n -> e p k n", p=P)
    names = ("raw_in", "bias_in", "w_half", "w_ok", "ht_mm", "ht_hi", "ht_lo", "eu_mm", "eu_ev", "eu_g", "eg_mm",
             "eg_hi", "eg_lo", "ey_mm", "ey_ev")
    (raw_in, bias_in, w_half, w_ok, ht_mm, ht_hi, ht_lo, eu_mm, eu_ev, eu_g, eg_mm, eg_hi, eg_lo, ey_mm,
     ey_ev) = [sem(n) for n in names]
    h_in = [sem(f"h_in{i}") for i in range(2)]
    y_st = [sem(f"y_st{i}") for i in range(2)]

    def tiles(eng, body):
        body(0, 0, True, 0)
        body(1, 1, True, 0)
        with eng.Fori(1, ET // 2) as i:
            body(2 * i, 0, True, i)
            body(2 * i + 1, 1, True, i)
        body(ET - 1, 0, False, ET // 2)

    assert ET % 2 == 1
    with ExitStack() as mem, nc.Block() as block:
        psU = mem.enter_context(nc.psum_tensor("psUp", [P, 2, HALF], F32))
        psG2 = mem.enter_context(nc.psum_tensor("psGt", [P, 2, HALF], F32))
        psH = mem.enter_context(nc.psum_tensor("psH", [P, C], F32))
        psE = mem.enter_context(nc.psum_tensor("psE", [P, C], F32))

        @block.gpsimd
        def _(pool):
            def expert(e, s, reuse):
                if later(e, 1):
                    wait(pool, w_ok, e)
                pool.dma_start(raw[:, 0].rearrange("p (k n) -> p k n", k=CK),
                               up_v[bass.ds(e, 1)].rearrange("a p k n -> p (a k) n")).then_inc(raw_in, 16)
                pool.dma_start(raw[:, 1].rearrange("p (k n) -> p k n", k=MK),
                               down_v[bass.ds(e, 1)].rearrange("a p k n -> p (a k) n")).then_inc(raw_in, 16)
                if reuse:
                    pool.wait_ge(ey_ev, pool.value_load(etab_end[0:1, bass.ds(e - 2, 1)], min_val=0, max_val=ET))
                pool.dma_start(ubias[:, s], up_b[bass.ds(e, 1)].rearrange("a n -> (a n)").partition_broadcast(P)
                               ).then_inc(bias_in, 16)
                pool.dma_start(dbias[:, s], down_b[bass.ds(e, 1)].rearrange("a n -> (a n)").partition_broadcast(P)
                               ).then_inc(bias_in, 16)
                wait(pool, raw_in, 32 * e + 32)
                W = CK * INNER
                for i in range(2):
                    hi, lo = slots[:, s, 2 * i * W:(2 * i + 1) * W], slots[:, s, (2 * i + 1) * W:(2 * i + 2) * W]
                    nc.gpsimd.tensor_copy(hi, raw[:, i]).then_inc(w_half, 1)
                    if i:
                        wait(pool, bias_in, 32 * e + 32)
                    wait(pool, w_half, 3 * e + 2 * i + 1)
                    nc.gpsimd.tensor_tensor(lo, raw[:, i], f32(hi), ALU.subtract).then_inc(w_ok if i else w_half, 1)

            for e in range(2):
                expert(e, e, False)
            with pool.Fori(1, E // 2) as i:
                expert(2 * i, 0, True)
                expert(2 * i + 1, 1, True)

        @block.sync
        def _(sp):
            def body(j, u, more, i):
                if later(j, 2):
                    wait(sp, ht_mm, j - 1)
                row = sp.value_load(rtab[0:1, bass.ds(j, 1)], min_val=0, max_val=E * REG - P)
                sp.dma_start(hin[:, u], hs[bass.ds(row, P), :]).then_inc(h_in[u], 16)

            body(0, 0, True, 0)
            body(1, 1, True, 0)
            with sp.Fori(1, ETL // 2) as i:
                body(2 * i, 0, True, i)
                body(2 * i + 1, 1, True, i)

        @block.tensor
        def _(pe):
            W = CK * INNER

            def turn_h(j, u, i):
                pe.wait_ge(h_in[u], 16 * i + 16)
                if later(j, 1):
                    pe.wait_ge(ht_lo, j)
                for k in range(CK):
                    mm = nc.tensor.transpose(psH[:, k * P:(k + 1) * P], hin[:, u, k * P:(k + 1) * P], ident[:])
                mm.then_inc(ht_mm, 1)

            def up(j, u):
                e = pe.value_load(etab[0:1, bass.ds(j, 1)], min_val=0, max_val=E - 1)
                s = pe.value_load(stab[0:1, bass.ds(j, 1)], min_val=0, max_val=1)
                pe.wait_ge(w_ok, e + 1)
                pe.wait_ge(ht_lo, j + 1)
                for h in range(2):
                    if later(j, 1):
                        pe.wait_ge(eu_ev, 2 * j - 1 + h)
                    n = 0
                    for k in range(CK):
                        for a, b in PASSES:
                            at = b * W + k * INNER + h * HALF
                            mm = nc.tensor.matmul(psU[:, h], eT[:, u, a, k],
                                                  slots[:, bass.ds(s, 1), at:at + HALF].rearrange("p a n -> p (a n)"),
                                                  start=(n == 0), stop=(n == 5))
                            n += 1
                    mm.then_inc(eu_mm, 1)

            def turn_g(j, u):
                for h in range(2):
                    pe.wait_ge(eu_g, 2 * j + h + 1)
                    if later(j, 1):
                        pe.wait_ge(eg_lo, 2 * j - 1 + h)
                    for m in range(MK // 2):
                        mm = nc.tensor.transpose(psG2[:, h, m * P:(m + 1) * P],
                                                 ge[:, u, h * HALF + m * P:h * HALF + (m + 1) * P], ident[:])
                    mm.then_inc(eg_mm, 1)

            def down(j):
                s = pe.value_load(stab[0:1, bass.ds(j, 1)], min_val=0, max_val=1)
                if later(j, 1):
                    pe.wait_ge(ey_ev, j)
                n = 0
                for m in range(MK):
                    if m % (MK // 2) == 0:
                        pe.wait_ge(eg_lo, 2 * j + m // (MK // 2) + 1)
                    for a, b in PASSES:
                        at = (2 + b) * W + m * C
                        mm = nc.tensor.matmul(psE[:], (gTh, gTl)[a][:, m * P:(m + 1) * P],
                                              slots[:, bass.ds(s, 1), at:at + C].rearrange("p a n -> p (a n)"),
                                              start=(n == 0), stop=(n == 3 * MK - 1))
                        n += 1
                mm.then_inc(ey_mm, 1)

            turn_h(0, 0, 0)
            up(0, 0)
            turn_h(1, 1, 0)

            def body(j, u, more, i):
                turn_g(j, u)
                if more:
                    up(j + 1, 1 - u)
                    turn_h(j + 2, u, i + 1)
                down(j)

            tiles(pe, body)

        @block.scalar
        def _(act):
            def high(j, u):
                act.wait_ge(ht_mm, j + 1)
                nc.scalar.copy(eT[:, u, 0].rearrange("p k n -> p (k n)"), psH[:]).then_inc(ht_hi, 1)

            def gelu(j, u):
                for h in range(2):
                    act.wait_ge(eu_ev, 2 * j + h + 1)
                    nc.scalar.activation(ge[:, u, h * HALF:(h + 1) * HALF], ub[:, h * HALF:(h + 1) * HALF], ACT.Gelu
                                         ).then_inc(eu_g, 1)

            def body(j, u, more, i):
                for h in range(2):
                    act.wait_ge(eg_mm, 2 * j + h + 1)
                    if later(j, 1):
                        act.wait_ge(ey_mm, j)
                    nc.scalar.copy(gTh[:, h * HALF:(h + 1) * HALF], psG2[:, h]).then_inc(eg_hi, 1)
                if more:
                    high(j + 2, u)
                    gelu(j + 1, 1 - u)
                act.wait_ge(ey_ev, j + 1)
                act.dma_start(ys[bass.ds(P * j, P), :], yb[:, u]).then_inc(y_st[u], 16)

            high(0, 0)
            gelu(0, 0)
            high(1, 1)
            tiles(act, body)
            act.wait_ge(y_st[0], 16 * (ET // 2 + 1))
            act.wait_ge(y_st[1], 16 * (ET // 2))

        @block.vector
        def _(dve):
            def low(j, u):
                dve.wait_ge(ht_hi, j + 1)
                nc.vector.tensor_tensor(eT[:, u, 1].rearrange("p k n -> p (k n)"), psH[:],
                                        f32(eT[:, u, 0].rearrange("p k n -> p (k n)")), ALU.subtract).then_inc(ht_lo, 1)

            def bias(j):
                s = dve.value_load(stab[0:1, bass.ds(j, 1)], min_val=0, max_val=1)
                for h in range(2):
                    dve.wait_ge(eu_mm, 2 * j + h + 1)
                    if later(j, 1):
                        dve.wait_ge(eu_g, 2 * j - 1 + h)
                    nc.vector.tensor_tensor(ub[:, h * HALF:(h + 1) * HALF], psU[:, h],
                                            ubias[:, bass.ds(s, 1), h * HALF:(h + 1) * HALF].rearrange("p a n -> p (a n)"),
                                            ALU.add).then_inc(eu_ev, 1)

            def body(j, u, more, i):
                for h in range(2):
                    dve.wait_ge(eg_hi, 2 * j + h + 1)
                    nc.vector.tensor_tensor(gTl[:, h * HALF:(h + 1) * HALF], psG2[:, h],
                                            f32(gTh[:, h * HALF:(h + 1) * HALF]), ALU.subtract).then_inc(eg_lo, 1)
                if more:
                    bias(j + 1)
                    low(j + 2, u)
                s = dve.value_load(stab[0:1, bass.ds(j, 1)], min_val=0, max_val=1)
                dve.wait_ge(ey_mm, j + 1)
                if later(j, 2):
                    dve.wait_ge(y_st[u], 16 * i)
                nc.vector.tensor_tensor(yb[:, u], psE[:], dbias[:, bass.ds(s, 1), :].rearrange("p a n -> p (a n)"),
                                        ALU.add).then_inc(ey_ev, 1)

            low(0, 0)
            bias(0)
            low(1, 1)
            tiles(dve, body)

    b4 = Map(nc, phase)
    shf = b4("shf", [P, 2, TG, C], F32)
    yg = b4("yg", [P, 2, TG, TOPK, C], F32)
    pstage = b4("pstage", [P, 2, TG, TOPK], U32)
    acc = b4("acc", [P, 2, C], F32)
    outb = b4("outb", [P, 2, TG, C], F32)
    top = b4("top", [P, 2, 2, 1], F32)
    names = ("f_pos", "f_y0", "f_y1", "f_s0", "f_s1", "f_c", "f_ok", "f_o0", "f_o1")
    f_pos, f_y0, f_y1, f_s0, f_s1, f_c, f_ok, f_o0, f_o1 = [sem(n) for n in names]
    f_y, f_s, f_o = (f_y0, f_y1), (f_s0, f_s1), (f_o0, f_o1)

    def pairs(eng, body):
        body(0, 0, 0)
        body(1, 1, 0)
        with eng.Fori(1, NG // 2) as i:
            body(2 * i, 0, i)
            body(2 * i + 1, 1, i)

    with nc.Block() as block:
        @block.gpsimd
        def _(pool):
            def body(g, q, i):
                if later(g, 2):
                    wait(pool, f_ok, TG * (g - 1))
                nc.gpsimd.tensor_copy(pstage[:, q], ypos[:, bass.ds(TG * g, TG), :]).then_inc(f_pos, 1)
                wait(pool, f_pos, g + 1)
                for t in range(TG):
                    for k in range(TOPK):
                        nc.gpsimd.indirect_dma_start(
                            out=yg[:, q, t, k], out_offset=None, in_=ys[:, :],
                            in_offset=bass.IndirectOffsetOnAxis(ap=pstage[:, q, t, k:k + 1], axis=0)
                        ).then_inc(f_y[q], 16)

            pairs(pool, body)

        @block.sync
        def _(sp):
            def body(g, q, i):
                if later(g, 2):
                    sp.wait_ge(f_ok, TG * (g - 1))
                sp.dma_start(shf[:, q], shd_v[:, bass.ds(TG * g, TG), :]).then_inc(f_s[q], 16)

            pairs(sp, body)

        @block.scalar
        def _(act):
            def body(g, q, i):
                act.wait_ge(f_ok, TG * g + TG)
                act.dma_start(out_v[:, bass.ds(TG * g, TG), :], outb[:, q]).then_inc(f_o[q], 16)

            pairs(act, body)
            for q in range(2):
                act.wait_ge(f_o[q], 16 * (NG // 2))

        @block.vector
        def _(dve):
            def body(g, q, i):
                dve.wait_ge(f_s[q], 16 * i + 16)
                dve.wait_ge(f_y[q], 16 * TG * TOPK * (i + 1))
                if later(g, 2):
                    dve.wait_ge(f_o[q], 16 * i)
                STEPS = 6
                for t in range(TG):
                    n = [0]

                    def link(ins):
                        n[0] += 1
                        ins.then_inc(f_c, 1)
                        dve.wait_ge(f_c, STEPS * (TG * g + t) + n[0])

                    w = wtop[:, bass.ds(TG * g + t, 1), :].rearrange("p a k -> p (a k)")
                    a = acc[:, t % 2]
                    link(nc.vector.scalar_tensor_tensor(a, yg[:, q, t, 0], w[:, 0:1], shf[:, q, t], ALU.mult, ALU.add))
                    link(nc.vector.scalar_tensor_tensor(a, yg[:, q, t, 1], w[:, 1:2], a, ALU.mult, ALU.add))
                    link(nc.vector.tensor_reduce(top[:, t % 2, 0], a, AX.X, ALU.max, apply_absolute_value=True))
                    link(nc.vector.tensor_scalar(top[:, t % 2, 0], top[:, t % 2, 0], EPS, None, ALU.add))
                    link(nc.vector.reciprocal(top[:, t % 2, 1], top[:, t % 2, 0]))
                    link(nc.vector.scalar_tensor_tensor(a, a, top[:, t % 2, 1], gate_fb[:], ALU.mult, ALU.mult))
                    nc.vector.tensor_tensor(outb[:, q, t], X[:, bass.ds(TG * g + t, 1), :].rearrange("p a c -> p (a c)"),
                                            a, ALU.add).then_inc(f_ok, 1)

            pairs(dve, body)
    ctx.close()


_INS = ["L0_attn_x", "L0_attn_Wq", "L0_attn_bq", "L0_attn_Wk", "L0_attn_bk", "L0_attn_Wv", "L0_attn_bv",
        "L0_attn_Wo", "L0_attn_bo", "L0_attn_ln_g", "L0_attn_ln_b", "L0_ffn_gate_w", "L0_ffn_bias",
        "L0_ffn_up_w", "L0_ffn_up_b", "L0_ffn_down_w", "L0_ffn_down_b", "L0_ffn_sw_up", "L0_ffn_sb_up",
        "L0_ffn_sw_down", "L0_ffn_sb_down", "L0_c", "L0_wmod"]


def kernel(**inputs):
    import numpy as _np
    import concourse.bacc as _bacc
    from concourse.bass_utils import run_bass_kernel_spmd as _run

    nc = _bacc.Bacc("TRN2", target_bir_lowering=False, num_devices=1)
    arrays, args = {}, []
    for name in _INS:
        a = _np.ascontiguousarray(inputs[name])
        arrays[f"in_{name}"] = a
        args.append(nc.dram_tensor(f"in_{name}", a.shape, F32, kind="ExternalInput").ap())
    scratch = [nc.dram_tensor("expert_in", (E * REG, C), F32, kind="Internal").ap(),
               nc.dram_tensor("expert_out", (ET * P, C), F32, kind="Internal").ap(),
               nc.dram_tensor("shared_out", (N, C), F32, kind="Internal").ap()]
    out = nc.dram_tensor("out", (1, N, C), F32, kind="ExternalOutput").ap()
    adaln_block(nc, *args, *scratch, out)
    r = _run(nc, [arrays], core_ids=[0])
    return r.results[0]["out"]
```

```python
from contextlib import ExitStack

import concourse.bass as bass
from concourse import mybir

ALU = mybir.AluOpType
ACT = mybir.ActivationFunctionType
F32 = mybir.dt.float32
F32R = mybir.dt.float32r
BF16 = mybir.dt.bfloat16
U32 = mybir.dt.uint32
I32 = mybir.dt.int32
AX = mybir.AxisListType

P = 128
N, C = 4096, 256
NT = N // P
TG = 4
NG = NT // TG
CK = C // P
HEADS, D = 16, 16
KV = 2
E, TOPK = 8, 2
INNER = 4 * C
MK = INNER // P
TR = 2 * P
REG = N + TR
ET = N * TOPK // TR + E - 1
ETL = ET + 1
META = 16
ROW = C + META
SLOT = 4 * CK * INNER
EPS_LN, EPS = 1e-5, 1e-6
HALF = 512
SRAW = 229312 - 2 * CK * INNER * 4


class Map:

    def __init__(self, nc, start):
        self.nc, self.at = nc, start

    def __call__(self, name, shape, dtype):
        size = 1
        for n in shape[1:]:
            size *= n
        size *= mybir.dt.size(dtype)
        t = self.nc.alloc_sbuf_tensor_at(name, shape, dtype, offset=self.at)
        self.at += -(-size // 64) * 64
        return t


def adaln_block(nc, x, Wq, bq, Wk, bk, Wv, bv, Wo, bo, ln_g, ln_b, gate_w, gate_b, up_w, up_b,
                down_w, down_b, sw_up, sb_up, sw_down, sb_down, c, wmod, hs, shd, out):
    f32 = lambda ap: ap.bitcast(F32)
    ctx = ExitStack()
    sem = lambda name: ctx.enter_context(nc.semaphore(name))
    x_v = x[0].rearrange("(p t) c -> p t c", t=NT)
    out_v = out[0].rearrange("(p t) c -> p t c", t=NT)
    shd_v = shd[0:N, :].rearrange("(p t) c -> p t c", t=NT)

    waited = sem("waited")

    def wait(eng, semaphore, value):
        eng.wait_ge(semaphore, value)
        if not isinstance(value, int):
            eng.sem_inc(waited, 1)

    def rsqrt(link, y, x, t, between=lambda n: None):
        link(nc.vector.tensor_scalar(t.bitcast(I32), x.bitcast(I32), 1, None, ALU.logical_shift_right))
        link(nc.vector.tensor_scalar(y.bitcast(I32), t.bitcast(I32), -1.0, float(0x5F3759DF), ALU.mult, ALU.add))
        for n in range(3):
            between(n)
            link(nc.vector.tensor_tensor(t, y, y, ALU.mult))
            link(nc.vector.scalar_tensor_tensor(t, x, -0.5, t, ALU.mult, ALU.mult))
            link(nc.vector.scalar_tensor_tensor(y, t, 1.5, y, ALU.add, ALU.mult))

    RSQRT = 11

    keep = Map(nc, -(-nc.sbuf_base // 64) * 64)
    ident = keep("ident", [P, P], F32)
    one_f = keep("one_f", [P, P], F32)
    X = keep("X", [P, NT, C], F32)
    scale_a = keep("scale_a", [P, C], F32)
    shift_a = keep("shift_a", [P, C], F32)
    mv1 = keep("mv1", [P, NT, 2], F32)
    rs1 = keep("rs1", [P, 3, NT], F32)
    gate_a = keep("gate_a", [P, C], F32)
    scale_b = keep("scale_b", [P, C], F32)
    shift_b = keep("shift_b", [P, C], F32)
    gate_fb = keep("gate_fb", [P, C], F32)
    bo_row = keep("bo_row", [P, C], F32)
    sbd_row = keep("sbd_row", [P, C], F32)
    idt = keep("idt", [P, NT], U32)
    run = keep("run", [P, E], F32)
    expo = keep("expo", [P, 2, 128], F32)
    iota_e = keep("iota_e", [P, E], F32)
    reg_e = keep("reg_e", [P, E], F32)
    etab = keep("etab", [P, ETL], I32)
    ktab = keep("ktab", [P, ETL], I32)
    stab = keep("stab", [P, ETL], I32)
    rtab = keep("rtab", [P, ETL], I32)
    ntab = keep("ntab", [P, ETL], I32)
    phase = keep.at

    att = Map(nc, phase)
    su = att("su", [P, 2, CK, INNER], F32R)
    sd = att("sd", [P, 2, MK, C], F32R)
    wo = att("wo", [P, 2, CK, C], F32R)
    gw = att("gw", [P, 2, CK, E], F32R)
    gb_row = att("gb_row", [P, E], F32)
    sbu = att("sbu", [P, MK], F32)
    state = att("state", [P, CK, P], F32)
    heads = att("heads", [P, P // D], F32)
    tri = att("tri", [P, P], BF16)
    one_b = att("one_b", [P, P], BF16)
    qT = att("qT", [P, CK, NT * P], F32)
    after_q = att.at

    p1w = Map(nc, after_q)
    wkq = p1w("wkq", [P, 2, CK, (KV + 1) * C], F32R)
    wv = p1w("wv", [P, CK, KV * C], F32)
    bk_row = p1w("bk_row", [P, KV * C], F32)
    bv_row = p1w("bv_row", [P, KV * C], F32)
    bq_col = p1w("bq_col", [P, CK], F32)
    blocks = p1w("blocks", [P, P], F32)

    st = Map(nc, p1w.at)
    wnat = st("wnat", [P, 2 * KV + 2, CK, C], F32)
    mw = st("mw", [P, CK, 6 * C], F32)
    c_col = st("c_col", [P, CK], F32)
    c_act = st("c_act", [P, CK], F32)
    c_rows = st("c_rows", [P, CK, P], F32)
    mod = st("mod", [P, 6, C], F32)
    ga_abs = st("ga_abs", [P, 2, C], F32)
    ga_sgn = st("ga_sgn", [P, 2, C], F32)
    eye2 = st("eye2", [P, CK, C], F32)
    wtmp = st("wtmp", [P, CK, C], F32)
    lng_col = st("lng_col", [P, CK], F32)
    lnb_col = st("lnb_col", [P, CK], F32)
    lnb_rows = st("lnb_rows", [P, CK, P], F32)
    gw_raw = st("gw_raw", [P, CK, E], F32)
    bn0 = st("bn0", [P, NT, 6], F32)
    sraw = Map(nc, SRAW)("sraw", [P, 2, CK, INNER], F32)

    ld_c, ld_mod, ld_w, ld_row, ld_sh = [sem(n) for n in ("ld_c", "ld_mod", "ld_w", "ld_row", "ld_sh")]
    consts, c_silu, c_spread = sem("consts"), sem("c_silu"), sem("c_spread")
    mod_mm, mod_ok, wt_mm, wt_ok, dve0, pool0 = [sem(n) for n in (
        "mod_mm", "mod_ok", "wt_mm", "wt_ok", "dve0", "pool0")]
    bo_mm, x_stat = sem("bo_mm"), sem("x_stat")
    x_in = sem("x_in")

    with ExitStack() as mem, nc.Block() as block:
        ps = [mem.enter_context(nc.psum_tensor(f"set_ps{i}", [P, HALF], F32)) for i in range(8)]
        N_W, N_ROW = 6, 10

        @block.sync
        def _(sp):
            narrow = ctx.enter_context(nc.allow_non_contiguous_dma(reason="short vectors, a channel per partition"))
            sp.dma_start(c_col[:], c.rearrange("a (k p) -> p (a k)", p=P)).then_inc(ld_c, 16)
            sp.dma_start(mw[:], wmod.rearrange("(k p) n -> p k n", p=P)).then_inc(ld_mod, 16)
            for i, w in enumerate((Wq, Wk[0], Wk[1], Wv[0], Wv[1], Wo)):
                sp.dma_start(wnat[:, i], w.rearrange("(k p) n -> p k n", p=P)).then_inc(ld_w, 16)
            for dst, src in (
                (bk_row[:], bk.rearrange("k c -> (k c)").partition_broadcast(P)),
                (bv_row[:], bv.rearrange("k c -> (k c)").partition_broadcast(P)),
                (bo_row[:], bo.partition_broadcast(P)), (sbd_row[:], sb_down.partition_broadcast(P)),
                (gb_row[:], gate_b.partition_broadcast(P)),
                (bq_col[:], bq.rearrange("(k p) -> p k", p=P)),
                (lng_col[:], ln_g.rearrange("(k p) -> p k", p=P)),
                (lnb_col[:], ln_b.rearrange("(k p) -> p k", p=P)),
                (sbu[:], sb_up.rearrange("(k p) -> p k", p=P)),
                (gw_raw[:], gate_w.rearrange("(k p) e -> p k e", p=P)),
            ):
                sp.dma_start(dst, src).then_inc(ld_row, 16)
            with sp.Fori(0, NG) as g:
                sp.dma_start(X[:, bass.ds(g * TG, TG), :], x_v[:, bass.ds(g * TG, TG), :]).then_inc(x_in, 16)
                wait(sp, x_in, 16 * g + 16)
            sp.dma_start(sraw[:, 0], sw_up.rearrange("(k p) n -> p k n", p=P)).then_inc(ld_sh, 16)
            sp.dma_start(sraw[:, 1].rearrange("p k n -> p (k n)").rearrange("p (k n) -> p k n", k=MK),
                         sw_down.rearrange("(k p) n -> p k n", p=P)).then_inc(ld_sh, 16)

        @block.gpsimd
        def _(pool):
            step = [0]

            def link(ins):
                step[0] += 1
                ins.then_inc(pool0, 1)
                pool.wait_ge(pool0, step[0])

            link(nc.gpsimd.memset(ident[:], 0.0))
            link(nc.gpsimd.affine_select(out=ident[:], in_=ident[:], compare_op=ALU.not_equal, fill=1.0, base=0,
                                         pattern=[[-1, P]], channel_multiplier=1))
            link(nc.gpsimd.memset(eye2[:], 0.0))
            for k in range(CK):
                link(nc.gpsimd.affine_select(out=eye2[:, k], in_=eye2[:, k], compare_op=ALU.not_equal, fill=1.0,
                                             base=P * k, pattern=[[-1, C]], channel_multiplier=1))
            link(nc.gpsimd.memset(one_f[:], 1.0))
            link(nc.gpsimd.memset(one_b[:], 1.0))
            link(nc.gpsimd.memset(run[:], 0.0))
            link(nc.gpsimd.memset(expo[:, 0], 0.5))
            link(nc.gpsimd.memset(expo[:, 1], -0.5))
            link(nc.gpsimd.affine_select(out=tri[:], in_=one_b[:], compare_op=ALU.is_gt, fill=0.0, base=0,
                                         pattern=[[1, P]], channel_multiplier=-1))
            link(nc.gpsimd.affine_select(out=heads[:], in_=one_f[:, :P // D], compare_op=ALU.is_ge, fill=0.0,
                                         base=0, pattern=[[-D, P // D]], channel_multiplier=1))
            link(nc.gpsimd.affine_select(out=heads[:], in_=heads[:], compare_op=ALU.is_ge, fill=0.0,
                                         base=D - 1, pattern=[[D, P // D]], channel_multiplier=-1))
            bl = blocks[:].rearrange("p (h d) -> p h d", d=D)
            link(nc.gpsimd.affine_select(out=bl, in_=one_f[:].rearrange("p (h d) -> p h d", d=D),
                                         compare_op=ALU.is_ge, fill=0.0,
                                         base=0, pattern=[[-D, P // D], [0, D]], channel_multiplier=1))
            link(nc.gpsimd.affine_select(out=bl, in_=bl, compare_op=ALU.is_ge, fill=0.0,
                                         base=D - 1, pattern=[[D, P // D], [0, D]], channel_multiplier=-1))
            link(nc.gpsimd.iota(idt[:], [[1, NT]], base=0, channel_multiplier=NT))
            link(nc.gpsimd.iota(iota_e[:], [[1, E]], base=0, channel_multiplier=0,
                                allow_small_or_imprecise_dtypes=True))
            nc.gpsimd.iota(reg_e[:], [[REG, E]], base=0, channel_multiplier=0,
                           allow_small_or_imprecise_dtypes=True).then_inc(consts, 1)

        @block.scalar
        def _(act):
            act.wait_ge(ld_c, 16)
            nc.scalar.activation(c_act[:], c_col[:], ACT.Silu).then_inc(c_silu, 1)

        @block.tensor
        def _(pe):
            pe.wait_ge(c_spread, 1)
            pe.wait_ge(ld_mod, 16)
            for n in range(3):
                for k in range(CK):
                    mm = nc.tensor.matmul(ps[n][:], c_rows[:, k], mw[:, k, n * HALF:(n + 1) * HALF],
                                          start=(k == 0), stop=(k == CK - 1))
                mm.then_inc(mod_mm, 1)
            pe.wait_ge(ld_w, 16 * N_W)
            pe.wait_ge(consts, 1)
            for i in range(6):
                if i >= 3:
                    pe.wait_ge(wt_ok, i - 2)
                for k in range(CK):
                    for o in range(CK):
                        mm = nc.tensor.transpose(ps[3 + i % 3][:, k * C + o * P:k * C + (o + 1) * P],
                                                 wnat[:, i, o, k * P:(k + 1) * P], ident[:])
                mm.then_inc(wt_mm, 1)
            pe.wait_ge(wt_ok, 6)
            for k in range(CK):
                mm = nc.tensor.matmul(ps[6][:, 0:C], lnb_rows[:, k], wtmp[:, k], start=(k == 0), stop=(k == CK - 1))
            mm.then_inc(bo_mm, 1)

        @block.vector
        def _(dve):
            step = [0]

            def link(ins):
                step[0] += 1
                ins.then_inc(dve0, 1)
                dve.wait_ge(dve0, step[0])

            dve.wait_ge(c_silu, 1)
            nc.vector.tensor_copy(c_rows[:], c_act[:].unsqueeze(2).broadcast_to([P, CK, P])).then_inc(c_spread, 1)
            dve.wait_ge(mod_mm, 3)
            for n in range(3):
                link(nc.vector.tensor_copy(mod[:, 2 * n:2 * n + 2].rearrange("p a c -> p (a c)"), ps[n][:]))
            nc.vector.tensor_copy(shift_a[:], mod[:, 0])
            nc.vector.tensor_scalar(scale_a[:], mod[:, 1], 1.0, None, ALU.add)
            nc.vector.tensor_copy(shift_b[:], mod[:, 3])
            nc.vector.tensor_scalar(scale_b[:], mod[:, 4], 1.0, None, ALU.add)
            for i, (m, dst) in enumerate(((2, gate_a), (5, gate_fb))):
                link(nc.vector.tensor_scalar(ga_sgn[:, i], mod[:, m], 0.0, 2.0, ALU.is_ge, ALU.mult))
                link(nc.vector.scalar_tensor_tensor(ga_abs[:, i], mod[:, m], -1.0, mod[:, m], ALU.mult, ALU.max))
                link(nc.vector.tensor_scalar(ga_abs[:, i], ga_abs[:, i], 0.25, None, ALU.max))
                link(nc.vector.scalar_tensor_tensor(dst[:], ga_sgn[:, i], -1.0, ga_abs[:, i], ALU.add, ALU.mult))
            dve.wait_ge(ld_row, 16 * N_ROW)
            dve.wait_ge(consts, 1)
            flat = lambda t: t.rearrange("p k n -> p (k n)")
            for i in range(5):
                dve.wait_ge(wt_mm, i + 1)
                t2 = ps[3 + i % 3][:].rearrange("p (k n) -> p k n", k=CK)
                if i < 3:
                    col = (KV * C if i == 0 else (i - 1) * C)
                    nc.vector.tensor_tensor(wtmp[:], t2, eye2[:], ALU.add).then_inc(wt_ok, 1)
                    dve.wait_ge(wt_ok, i + 1)
                    link(nc.vector.tensor_copy(wkq[:, 0, :, col:col + C], wtmp[:]))
                    link(nc.vector.tensor_tensor(wkq[:, 1, :, col:col + C], wtmp[:],
                                                 f32(wkq[:, 0, :, col:col + C]), ALU.subtract))
                else:
                    nc.vector.tensor_tensor(wv[:, :, (i - 3) * C:(i - 2) * C], t2, eye2[:], ALU.add).then_inc(wt_ok, 1)
            dve.wait_ge(wt_mm, 6)
            link(nc.vector.tensor_copy(lnb_rows[:], lnb_col[:].unsqueeze(2).broadcast_to([P, CK, P])))
            nc.vector.tensor_copy(flat(wtmp[:]), ps[5][:]).then_inc(wt_ok, 1)
            dve.wait_ge(bo_mm, 1)
            link(nc.vector.tensor_tensor(bo_row[:], ps[6][:, 0:C], bo_row[:], ALU.add))
            link(nc.vector.tensor_tensor(bo_row[:], bo_row[:], gate_a[:], ALU.mult))
            for k in range(CK):
                link(nc.vector.scalar_tensor_tensor(wtmp[:, k], wtmp[:, k], lng_col[:, k:k + 1], gate_a[:],
                                                    ALU.mult, ALU.mult))
            link(nc.vector.tensor_copy(wo[:, 0], wtmp[:]))
            link(nc.vector.tensor_tensor(wo[:, 1], wtmp[:], f32(wo[:, 0]), ALU.subtract))
            link(nc.vector.tensor_copy(gw[:, 0], gw_raw[:]))
            link(nc.vector.tensor_tensor(gw[:, 1], gw_raw[:], f32(gw[:, 0]), ALU.subtract))
            link(nc.vector.tensor_scalar(sbd_row[:], sbd_row[:], 0.1, None, ALU.mult))
            with dve.Fori(0, NG) as g:
                wait(dve, x_in, 16 * g + 16)
                for t in range(TG):
                    nc.vector.bn_stats(bn0[:, bass.ds(TG * g + t, 1)].rearrange("p a n -> p (a n)"),
                                       X[:, bass.ds(TG * g + t, 1), :].rearrange("p a c -> p (a c)")
                                       ).then_inc(x_stat, 1)
            dve.wait_ge(x_stat, NT)
            for t in range(NT):
                last = nc.vector.bn_aggr(mv1[:, t], bn0[:, t])
            link(last)
            link(nc.vector.tensor_scalar(rs1[:, 1], mv1[:, :, 1], EPS_LN, None, ALU.add))
            rsqrt(link, rs1[:, 2], rs1[:, 1], rs1[:, 0])

    b1 = Map(nc, p1w.at)
    z1 = b1("z1", [P, TG, C], F32)
    h1 = b1("h1", [P, 2, TG, C + 1], F32)
    hT = b1("hT", [P, 2, 2, CK, HALF], F32R)
    kraw = b1("kraw", [P, 2, KV * C], F32)
    ks = b1("ks", [P, TG, KV * C], F32)
    ksq = b1("ksq", [P, 2, KV * C], F32)
    kn = b1("kn", [P, TG, KV * C], F32)
    kss = b1("kss", [P, TG, KV * HEADS], F32)
    krs = b1("krs", [P, TG, KV * HEADS], F32)
    kinv = b1("kinv", [P, TG, KV * HEADS], F32)
    ktmp = b1("ktmp", [P, TG, KV * HEADS], F32)
    zero_w = b1("zero_w", [P, C + 1], F32)
    assert b1.at <= SRAW and st.at <= SRAW

    names = ("z1_ok", "h1_ml", "h1_ok", "tp1", "hi1", "lo1", "k_mm", "k_ev", "k_silu", "k_sq", "k_red",
             "k_inv", "k_n", "g_mm", "q_mm", "q_silu", "h1_one", "sw_hi", "sw_lo")
    (z1_ok, h1_ml, h1_ok, tp1, hi1, lo1, k_mm, k_ev, k_silu, k_sq, k_red, k_inv, k_n, g_mm, q_mm, q_silu,
     h1_one, sw_hi, sw_lo) = [sem(n) for n in names]
    later = lambda g, n: not isinstance(g, int) or g >= n

    def groups(eng, body):
        body(0, 0, True)
        body(1, 1, True)
        with eng.Fori(1, NG // 2 - 1) as i:
            body(2 * i, 0, True)
            body(2 * i + 1, 1, True)
        body(NG - 2, 0, True)
        body(NG - 1, 1, False)

    with ExitStack() as mem:
        psG = mem.enter_context(nc.psum_tensor("psG", [P, 4, HALF], F32))
        with ExitStack() as mem1, nc.Block() as block:
            psK = mem1.enter_context(nc.psum_tensor("psK", [P, HALF], F32))
            psQ = mem1.enter_context(nc.psum_tensor("psQ", [P, HALF], F32))
            psT = mem1.enter_context(nc.psum_tensor("psT", [P, 2, HALF], F32))

            @block.vector
            def _(dve):
                def normalise(g, t):
                    if later(g, 1):
                        dve.wait_ge(h1_ok, TG * (g - 1) + t + 1)
                    n = TG * g + t
                    nc.vector.tensor_scalar(z1[:, t], X[:, bass.ds(n, 1), :].rearrange("p a c -> p (a c)"),
                                            mv1[:, bass.ds(n, 1), 0], rs1[:, 2, bass.ds(n, 1)],
                                            ALU.subtract, ALU.mult).then_inc(z1_ok, 1)

                def low(g, q, k):
                    dve.wait_ge(hi1, 2 * g + k + 1)
                    nc.vector.tensor_tensor(hT[:, q, 1, k], psT[:, k], f32(hT[:, q, 0, k]), ALU.subtract
                                            ).then_inc(lo1, 1)

                def unit(f, t):
                    if later(f, 1):
                        dve.wait_ge(g_mm, TG * (f - 1) + t + 1)
                    nc.vector.scalar_tensor_tensor(
                        kn[:, t].rearrange("p (h d) -> p h d", d=D),
                        ks[:, t].rearrange("p (h d) -> p h d", d=D), 0.5,
                        kinv[:, t].unsqueeze(2).broadcast_to([P, KV * HEADS, D]), ALU.add, ALU.mult
                    ).then_inc(k_n, 1)

                nc.vector.memset(h1[:, :, :, C:C + 1], 1.0).then_inc(h1_one, 1)
                nc.vector.memset(zero_w[:], 0.0).then_inc(h1_one, 1)
                for t in range(TG):
                    normalise(0, t)
                low(0, 0, 0)
                low(0, 0, 1)

                def body(g, q, more):
                    prev = later(g, 1)

                    def evac(t):
                        dve.wait_ge(k_mm, TG * g + t + 1)
                        if prev or t >= 2:
                            dve.wait_ge(k_silu, TG * g + t - 1)
                        nc.vector.tensor_tensor(kraw[:, t % 2], psK[:], bk_row[:], ALU.add).then_inc(k_ev, 1)

                    def reduce(t):
                        dve.wait_ge(k_sq, TG * g + t + 1)
                        nc.vector.tensor_reduce(kss[:, t], ksq[:, t % 2].rearrange("p (h d) -> p h d", d=D),
                                                AX.X, ALU.add).then_inc(k_red, 1)

                    n = [0]
                    STEPS = RSQRT + 3

                    def link(ins):
                        n[0] += 1
                        ins.then_inc(k_inv, 1)
                        dve.wait_ge(k_inv, STEPS * g + n[0])

                    def between(n):
                        if more and n >= 1:
                            low(g + 1, 1 - q, n - 1)

                    flat = lambda t: t[:].rearrange("p t h -> p (t h)")
                    if prev:
                        unit(g - 1, 0)
                    evac(0)
                    if prev:
                        unit(g - 1, 1)
                        unit(g - 1, 2)
                    evac(1)
                    if prev:
                        unit(g - 1, 3)
                    reduce(0)
                    evac(2)
                    reduce(1)
                    if more:
                        normalise(g + 1, 0)
                        normalise(g + 1, 1)
                    evac(3)
                    if more:
                        normalise(g + 1, 2)
                        normalise(g + 1, 3)
                    reduce(2)
                    reduce(3)
                    dve.wait_ge(k_red, TG * g + TG)
                    rsqrt(link, flat(krs), flat(kss), flat(ktmp), between)
                    link(nc.vector.tensor_scalar(flat(kss), flat(krs), EPS, 1.0, ALU.mult, ALU.add))
                    link(nc.vector.reciprocal(flat(ktmp), flat(kss)))
                    link(nc.vector.tensor_tensor(flat(kinv), flat(krs), flat(ktmp), ALU.mult))
                    assert n[0] == STEPS

                groups(dve, body)
                for t in range(TG):
                    unit(NG - 1, t)

            @block.gpsimd
            def _(pool):
                def modulate(g, q, t):
                    wait(pool, z1_ok, TG * g + t + 1)
                    nc.gpsimd.tensor_tensor(z1[:, t], z1[:, t], scale_a[:], ALU.mult).then_inc(h1_ml, 1)
                    wait(pool, h1_ml, TG * g + t + 1)
                    if later(g, 2):
                        wait(pool, g_mm, TG * (g - 2) + t + 1)
                    nc.gpsimd.tensor_tensor(h1[:, q, t, 0:C], z1[:, t], shift_a[:], ALU.add).then_inc(h1_ok, 1)

                for t in range(TG):
                    modulate(0, 0, t)

                def body(g, q, more):
                    for t in range(TG):
                        if more:
                            modulate(g + 1, 1 - q, t)
                        if isinstance(g, int) and g == 1:
                            split(t)

                def split(n):
                    a, k = n // 2, n % 2
                    src = sraw[:, a, k]
                    w = (su[:, :, k], sd[:, :, k * MK // 2:(k + 1) * MK // 2].rearrange("p b m n -> p b (m n)"))[a]
                    if n == 0:
                        pool.wait_ge(ld_sh, 32)
                    nc.gpsimd.tensor_copy(w[:, 0], src).then_inc(sw_hi, 1)
                    pool.wait_ge(sw_hi, n + 1)
                    nc.gpsimd.tensor_tensor(w[:, 1], src, f32(w[:, 0]), ALU.subtract).then_inc(sw_lo, 1)

                groups(pool, body)

            @block.scalar
            def _(act):
                def high(g, q, k):
                    act.wait_ge(tp1, 2 * g + k + 1)
                    nc.scalar.copy(hT[:, q, 0, k], psT[:, k]).then_inc(hi1, 1)

                high(0, 0, 0)
                high(0, 0, 1)

                def body(g, q, more):
                    def key(t):
                        act.wait_ge(k_ev, TG * g + t + 1)
                        if later(g, 1):
                            act.wait_ge(k_n, TG * (g - 1) + t + 1)
                        nc.scalar.activation(ks[:, t], kraw[:, t % 2], ACT.Silu).then_inc(k_silu, 1)
                        act.wait_ge(k_silu, TG * g + t + 1)
                        if later(g, 1) or t >= 2:
                            act.wait_ge(k_red, TG * g + t - 1)
                        nc.scalar.activation(ksq[:, t % 2], ks[:, t], ACT.Square, bias=expo[:, 0, 0:1]).then_inc(k_sq, 1)

                    def query(k):
                        act.wait_ge(q_mm, CK * g + k + 1)
                        nc.scalar.activation(qT[:, k, bass.ds(HALF * g, HALF)], psQ[:], ACT.Silu,
                                             bias=bq_col[:, k:k + 1]).then_inc(q_silu, 1)

                    for t in range(TG):
                        key(t)
                    query(0)
                    if more:
                        high(g + 1, 1 - q, 0)
                        high(g + 1, 1 - q, 1)
                    query(1)

                groups(act, body)

            @block.tensor
            def _(pe):
                pe.wait_ge(h1_one, 2)

                def turn(g, q, k):
                    if k == 0:
                        pe.wait_ge(h1_ok, TG * g + TG)
                    for t in range(TG):
                        mm = nc.tensor.transpose(psT[:, k, t * P:(t + 1) * P], h1[:, q, t, k * P:(k + 1) * P], ident[:])
                    mm.then_inc(tp1, 1)

                def keys(g, q, t):
                    if t == 0:
                        pe.wait_ge(lo1, 2 * g + 2)
                    if later(g, 1) or t:
                        pe.wait_ge(k_ev, TG * g + t)
                    n = 0
                    for k in range(CK):
                        for a, b in ((0, 0), (0, 1), (1, 0)):
                            mm = nc.tensor.matmul(psK[:], hT[:, q, a, k, t * P:(t + 1) * P],
                                                  wkq[:, b, k, 0:KV * C], start=(n == 0), stop=(n == 3 * CK - 1))
                            n += 1
                    mm.then_inc(k_mm, 1)

                def queries(g, q, o):
                    if later(g, 1) or o:
                        pe.wait_ge(q_silu, CK * g + o)
                    n = 0
                    for k in range(CK):
                        for a, b in ((0, 0), (0, 1), (1, 0)):
                            col = KV * C + o * P
                            mm = nc.tensor.matmul(psQ[:], wkq[:, b, k, col:col + P], hT[:, q, a, k],
                                                  start=(n == 0), stop=(n == 3 * CK - 1))
                            n += 1
                    mm.then_inc(q_mm, 1)

                def sums(f, r, t):
                    pe.wait_ge(k_n, TG * f + t + 1)
                    for j in range(4):
                        mm = nc.tensor.matmul(psG[:, j, 0:C + 1], kn[:, t, j * P:(j + 1) * P], h1[:, r, t],
                                              start=False, stop=False, skip_group_check=True)
                    mm.then_inc(g_mm, 1)

                for j in range(4):
                    nc.tensor.matmul(psG[:, j, 0:C + 1], zero_w[:, 0:P], zero_w[:],
                                     start=True, stop=False, skip_group_check=True)
                turn(0, 0, 0)
                turn(0, 0, 1)

                def body(g, q, more):
                    for t in range(TG):
                        keys(g, q, t)
                        if later(g, 1):
                            sums(g - 1, 1 - q, t)
                    queries(g, q, 0)
                    if more:
                        turn(g + 1, 1 - q, 0)
                        turn(g + 1, 1 - q, 1)
                    queries(g, q, 1)

                groups(pe, body)
                for t in range(TG):
                    sums(NG - 1, 1, t)

        s1 = Map(nc, p1w.at)
        Gs = s1("Gs", [P, 4, C + 1], F32)
        GT = s1("GT", [P, 4, CK, P], F32)
        sts = s1("sts", [P, 4, P], F32)
        g_cp, g_tp, g_tc, s_mm, s_dve = [sem(n) for n in ("g_cp", "g_tp", "g_tc", "s_mm", "s_dve")]
        with ExitStack() as mem1, nc.Block() as block:
            psA = mem1.enter_context(nc.psum_tensor("psA", [P, 2, HALF], F32))
            psS = mem1.enter_context(nc.psum_tensor("psS", [P, HALF], F32))

            @block.vector
            def _(dve):
                for j in range(4):
                    nc.vector.tensor_copy(Gs[:, j], psG[:, j, 0:C + 1]).then_inc(g_cp, 1)
                for b in range(2):
                    dve.wait_ge(g_tp, b + 1)
                    nc.vector.tensor_copy(GT[:, 2 * b:2 * b + 2].rearrange("p j k n -> p (j k n)"), psA[:, b]
                                          ).then_inc(g_tc, 1)
                dve.wait_ge(s_mm, 1)
                dve.wait_ge(g_cp, 4)
                for j in range(4):
                    kv, hf = j // 2, j % 2
                    nc.vector.scalar_tensor_tensor(sts[:, j], bv_row[:, kv * C + hf * P:kv * C + hf * P + P],
                                                   Gs[:, j, C:C + 1], psS[:, j * P:(j + 1) * P],
                                                   ALU.mult, ALU.add).then_inc(s_dve, 1)
                dve.wait_ge(s_dve, 4)
                for hf in range(CK):
                    nc.vector.scalar_tensor_tensor(sts[:, hf], sts[:, hf], float(N) ** -KV, sts[:, 2 + hf],
                                                   ALU.mult, ALU.mult).then_inc(s_dve, 1)
                dve.wait_ge(s_dve, 6)
                for hf in range(CK):
                    nc.vector.tensor_tensor(state[:, hf], sts[:, hf], blocks[:], ALU.mult)

            @block.tensor
            def _(pe):
                for j in range(4):
                    pe.wait_ge(g_cp, j + 1)
                    for k in range(CK):
                        at = (j % 2) * C + k * P
                        mm = nc.tensor.transpose(psA[:, j // 2, at:at + P], Gs[:, j, k * P:(k + 1) * P], ident[:])
                    if j % 2:
                        mm.then_inc(g_tp, 1)
                pe.wait_ge(g_tc, 2)
                for j in range(4):
                    kv, hf = j // 2, j % 2
                    for k in range(CK):
                        at = kv * C + hf * P
                        mm = nc.tensor.matmul(psS[:, j * P:(j + 1) * P], GT[:, j, k], wv[:, k, at:at + P],
                                              start=(k == 0), stop=(k == CK - 1))
                mm.then_inc(s_mm, 1)

    b2 = Map(nc, after_q)
    q5 = b2("q5", [P, CK, HALF], F32)
    qsq = b2("qsq", [P, CK, HALF], F32)
    nq = b2("nq", [P, 4, TG * HEADS], F32)
    oz = b2("oz", [P, TG, C], F32)
    bn2 = b2("bn2", [P, 2, TG, 6], F32)
    mv2 = b2("mv2", [P, 2, TG, 2], F32)
    rs2 = b2("rs2", [P, 2, 2, TG], F32)
    zT = b2("zT", [P, 2, CK, HALF], F32R)
    z2 = b2("z2", [P, TG, C], F32)
    h2 = b2("h2", [P, 2, TG, ROW], F32)
    h2T = b2("h2T", [P, 2, 2, CK, HALF], F32R)
    gf = b2("gf", [P, 2, HALF], F32)
    ghi = b2("ghi", [P, 3, HALF], F32R)
    glo = b2("glo", [P, 3, HALF], F32R)
    sh = b2("sh", [P, TG, C], F32)
    lg = b2("lg", [P, TG, E], F32)
    sc = b2("sc", [P, TG, E], F32)
    mx = b2("mx", [P, TG, E], F32)
    ix = b2("ix", [P, TG, E], U32)
    ixf = b2("ixf", [P, TG, TOPK], F32)
    oh = b2("oh", [P, TOPK, TG, E], F32)
    ohb = b2("ohb", [P, TG, E], BF16)
    rk = b2("rk", [P, TG, E], F32)
    rk2 = b2("rk2", [P, TG, E], F32)
    pf = b2("pf", [P, TG, TOPK], F32)
    post = b2("post", [P, 2, TG, TOPK], U32)
    dn = b2("dn", [P, 2, TG], F32)
    wt = b2("wt", [P, TG, TOPK], F32)
    wd = b2("wd", [P, 2, TG, E], F32)

    names = ("q_pre", "nm_mm", "nm_ev", "rq_ok", "o_mm", "o_ev", "stat2", "self2", "rse2",
             "rstd2", "zo_ok", "tz_mm", "tz_hi", "tz_lo", "xb_ok", "a_mm", "x_ev", "z2_ok", "h2_ml", "h2_ok",
             "th_mm", "th_hi", "th_lo", "gt_mm", "gt_ev", "gt_sc", "rt_dve", "rt_oh", "rt_mm", "pos_ok",
             "scat", "u_mm", "u_g", "u_hi", "u_lo", "d_mm", "sh_ev", "sh_st")
    (q_pre, nm_mm, nm_ev, rq_ok, o_mm, o_ev, stat2, self2, rse2, rstd2, zo_ok, tz_mm, tz_hi,
     tz_lo, xb_ok, a_mm, x_ev, z2_ok, h2_ml, h2_ok, th_mm, th_hi, th_lo, gt_mm, gt_ev, gt_sc, rt_dve, rt_oh,
     rt_mm, pos_ok, scat, u_mm, u_g, u_hi, u_lo, d_mm, sh_ev, sh_st) = [sem(n) for n in names]

    def staggered(eng, body):
        body(0, 0, True, False)
        body(1, 1, True, True)
        body(2, 0, True, True)
        with eng.Fori(1, NG // 2 - 1) as i:
            body(2 * i + 1, 1, True, True)
            body(2 * i + 2, 0, True, True)
        body(NG - 1, 1, True, True)
        body(NG, 0, False, True)

    PASSES = ((0, 0), (0, 1), (1, 0))

    with ExitStack() as mem, nc.Block() as block:
        psU = mem.enter_context(nc.psum_tensor("psU", [P, 2, HALF], F32))
        psY = mem.enter_context(nc.psum_tensor("psY", [P, 2, HALF], F32))
        psZ = mem.enter_context(nc.psum_tensor("psZ", [P, 2, HALF], F32))
        psO = mem.enter_context(nc.psum_tensor("psO", [P, HALF], F32))
        psM = mem.enter_context(nc.psum_tensor("psM", [P, HALF], F32))
        NORM, GATE, RANK, TOTAL = 0, 64, 96, 128

        @block.tensor
        def _(pe):
            def body(g, q, att_on, ffn_on):
                f, r = g - 1, 1 - q

                def norms():
                    pe.wait_ge(q_pre, 2 * g + 2)
                    if later(g, 2):
                        pe.wait_ge(rt_dve, 20 * g - 20)
                    for t in range(TG):
                        for k in range(CK):
                            at = NORM + t * HEADS + k * (P // D)
                            mm = nc.tensor.matmul(psM[:, at:at + P // D], qsq[:, k, t * P:(t + 1) * P], heads[:],
                                                  start=True, stop=True)
                    mm.then_inc(nm_mm, 1)

                def outs(h):
                    if later(g, 1) or h:
                        pe.wait_ge(o_ev, 2 * g + 1) if h else pe.wait_ge(x_ev, 2 * g)
                    for t in (2 * h, 2 * h + 1):
                        for k in range(CK):
                            at = (t % 2) * C + k * P
                            mm = nc.tensor.matmul(psO[:, at:at + P], q5[:, k, t * P:(t + 1) * P], state[:, k],
                                                  start=True, stop=True)
                    mm.then_inc(o_mm, 1)

                def turn_z(k):
                    pe.wait_ge(zo_ok, TG * g + TG)
                    if later(g, 1):
                        pe.wait_ge(th_lo, 2 * g - 1 + k)
                    for t in range(TG):
                        mm = nc.tensor.transpose(psZ[:, k, t * P:(t + 1) * P], oz[:, t, k * P:(k + 1) * P], ident[:])
                    mm.then_inc(tz_mm, 1)

                def attend(h):
                    pe.wait_ge(x_ev, 2 * g + 1) if h else pe.wait_ge(o_ev, 2 * g + 2)
                    if not h:
                        pe.wait_ge(tz_lo, 2 * g + 2)
                    for t in (2 * h, 2 * h + 1):
                        n = 0
                        for k in range(CK):
                            for a, b in PASSES:
                                mm = nc.tensor.matmul(psO[:, (t % 2) * C:(t % 2 + 1) * C],
                                                      zT[:, a, k, t * P:(t + 1) * P], wo[:, b, k],
                                                      start=(n == 0), stop=(n == 5))
                                n += 1
                    mm.then_inc(a_mm, 1)

                def turn_h(k):
                    pe.wait_ge(h2_ok, TG * g + TG)
                    pe.wait_ge(tz_lo, 2 * g + 1 + k)
                    for t in range(TG):
                        mm = nc.tensor.transpose(psZ[:, k, t * P:(t + 1) * P], h2[:, q, t, k * P:(k + 1) * P], ident[:])
                    mm.then_inc(th_mm, 1)

                def gate():
                    pe.wait_ge(th_lo, 2 * f + 2)
                    if att_on:
                        pe.wait_ge(nm_ev, g + 1)
                    for t in range(TG):
                        n = 0
                        for k in range(CK):
                            for a, b in PASSES:
                                mm = nc.tensor.matmul(psM[:, GATE + t * E:GATE + (t + 1) * E],
                                                      h2T[:, r, a, k, t * P:(t + 1) * P], gw[:, b, k],
                                                      start=(n == 0), stop=(n == 5))
                                n += 1
                    mm.then_inc(gt_mm, 1)

                def rank():
                    pe.wait_ge(rt_oh, f + 1)
                    nc.tensor.matmul(psM[:, RANK:RANK + TG * E], tri[:], ohb[:].rearrange("p t e -> p (t e)"),
                                     start=True, stop=False, skip_group_check=True)
                    for t in range(TG - 1):
                        n = TG - 1 - t
                        nc.tensor.matmul(psM[:, RANK + (t + 1) * E:RANK + TG * E].rearrange("p (t e) -> p t e", e=E),
                                         one_b[:], ohb[:, t:t + 1].broadcast_to([P, n, E]), start=False,
                                         stop=(t == TG - 2), skip_group_check=True)
                    for t in range(TG):
                        mm = nc.tensor.matmul(psM[:, TOTAL:TOTAL + E], one_b[:], ohb[:, t], start=(t == 0),
                                              stop=(t == TG - 1))
                    mm.then_inc(rt_mm, 1)

                def up(m):
                    if later(f, 1) or m >= 2:
                        pe.wait_ge(u_g, MK * f + m - 1)
                    if m == 0:
                        pe.wait_ge(th_lo, 2 * f + 2)
                    n = 0
                    for k in range(CK):
                        for a, b in PASSES:
                            mm = nc.tensor.matmul(psU[:, m % 2], su[:, b, k, m * P:(m + 1) * P], h2T[:, r, a, k],
                                                  start=(n == 0), stop=(n == 5))
                            n += 1
                    mm.then_inc(u_mm, 1)

                def down(m):
                    pe.wait_ge(u_lo, MK * f + m + 1)
                    if m == 0 and later(f, 1):
                        pe.wait_ge(sh_ev, 2 * f)
                    for t in range(TG):
                        for n, (a, b) in enumerate(PASSES):
                            lhs = (ghi, glo)[a][:, m % 3, t * P:(t + 1) * P]
                            mm = nc.tensor.matmul(psY[:, t // 2, (t % 2) * C:(t % 2 + 1) * C], lhs, sd[:, b, m],
                                                  start=(m == 0 and t % 2 == 0 and n == 0),
                                                  stop=(m == MK - 1 and n == 2), skip_group_check=True)
                    mm.then_inc(d_mm, 1)

                def chunk(m):
                    if ffn_on:
                        if m < MK:
                            up(m)
                        if m >= 2:
                            down(m - 2)

                if att_on:
                    norms()
                    outs(0)
                if ffn_on:
                    gate()
                chunk(0)
                if att_on:
                    outs(1)
                chunk(1)
                chunk(2)
                if ffn_on:
                    rank()
                if att_on:
                    turn_z(0)
                    turn_z(1)
                chunk(3)
                if att_on:
                    attend(0)
                chunk(4)
                if att_on:
                    attend(1)
                for m in range(5, MK + 2):
                    chunk(m)
                if att_on:
                    turn_h(0)
                    turn_h(1)

            staggered(pe, body)

        @block.scalar
        def _(act):
            def body(g, q, att_on, ffn_on):
                f, r = g - 1, 1 - q

                def queries():
                    if later(g, 1):
                        act.wait_ge(o_mm, 2 * g)
                    src = qT[:, :, bass.ds(HALF * g, HALF)]
                    nc.scalar.activation(q5[:], src, ACT.Identity, bias=expo[:, 0, 0:1]).then_inc(q_pre, 1)
                    nc.scalar.activation(qsq[:], src, ACT.Square, bias=expo[:, 0, 0:1]).then_inc(q_pre, 1)

                def high(mm, out, dst, k):
                    act.wait_ge(mm, 2 * g + k + 1)
                    nc.scalar.copy(dst[:, 0, k], psZ[:, k]).then_inc(out, 1)

                def gelu(m):
                    act.wait_ge(u_mm, MK * f + m + 1)
                    if later(f, 1) or m >= 2:
                        act.wait_ge(u_lo, MK * f + m - 1)
                    nc.scalar.activation(gf[:, m % 2], psU[:, m % 2], ACT.Gelu, bias=sbu[:, m:m + 1]).then_inc(u_g, 1)
                    act.wait_ge(u_g, MK * f + m + 1)
                    if later(f, 1) or m >= 3:
                        act.wait_ge(d_mm, MK * f + m - 2)
                    nc.scalar.copy(ghi[:, m % 3], gf[:, m % 2]).then_inc(u_hi, 1)

                def score():
                    act.wait_ge(gt_ev, f + 1)
                    nc.scalar.activation(sc[:], lg[:], ACT.Sigmoid).then_inc(gt_sc, 1)

                if att_on and isinstance(g, int) and g == 0:
                    queries()
                if ffn_on:
                    score()
                    gelu(0)
                    gelu(1)
                    gelu(2)
                if att_on:
                    high(tz_mm, tz_hi, zT, 0)
                    high(tz_mm, tz_hi, zT, 1)
                if ffn_on:
                    for m in range(3, MK):
                        gelu(m)
                if att_on:
                    if not (isinstance(g, int) and g == NG - 1):
                        g2 = g + 1
                        act.wait_ge(o_mm, 2 * g2)
                        src = qT[:, :, bass.ds(HALF * g2, HALF)]
                        nc.scalar.activation(q5[:], src, ACT.Identity, bias=expo[:, 0, 0:1]).then_inc(q_pre, 1)
                        nc.scalar.activation(qsq[:], src, ACT.Square, bias=expo[:, 0, 0:1]).then_inc(q_pre, 1)
                    high(th_mm, th_hi, h2T[:, q], 0)
                    high(th_mm, th_hi, h2T[:, q], 1)

            staggered(act, body)

        @block.vector
        def _(dve):
            def body(g, q, att_on, ffn_on):
                f, r = g - 1, 1 - q

                def tile(t):
                    return X[:, bass.ds(TG * g + t, 1), :].rearrange("p a c -> p (a c)")

                def norm_read():
                    dve.wait_ge(nm_mm, g + 1)
                    nc.vector.tensor_copy(nq[:, 0], psM[:, NORM:NORM + TG * HEADS]).then_inc(nm_ev, 1)

                def norm_inverse():
                    n = [0]
                    STEPS = RSQRT + 3

                    def link(ins):
                        n[0] += 1
                        ins.then_inc(rq_ok, 1)
                        dve.wait_ge(rq_ok, STEPS * g + n[0])

                    dve.wait_ge(nm_ev, g + 1)
                    rsqrt(link, nq[:, 2], nq[:, 0], nq[:, 3])
                    link(nc.vector.tensor_scalar(nq[:, 0], nq[:, 2], EPS, 1.0, ALU.mult, ALU.add))
                    link(nc.vector.reciprocal(nq[:, 3], nq[:, 0]))
                    link(nc.vector.tensor_tensor(nq[:, 1], nq[:, 2], nq[:, 3], ALU.mult))
                    assert n[0] == STEPS

                def out_read(h):
                    dve.wait_ge(o_mm, 2 * g + h + 1)
                    inv = nq[:, 1, 2 * h * HEADS:(2 * h + 2) * HEADS].unsqueeze(2).broadcast_to([P, 2 * HEADS, D])
                    nc.vector.tensor_tensor(oz[:, 2 * h:2 * h + 2].rearrange("p t (h d) -> p (t h) d", d=D),
                                            psO[:].rearrange("p (h d) -> p h d", d=D), inv, ALU.mult
                                            ).then_inc(o_ev, 1)
                    wait(dve, o_ev, 2 * g + h + 1)
                    for t in (2 * h, 2 * h + 1):
                        nc.vector.bn_stats(bn2[:, 0, t], oz[:, t]).then_inc(self2, 1)
                        wait(dve, self2, 8 * g + t + 1)
                        nc.vector.bn_aggr(mv2[:, 0, t], bn2[:, 0, t]).then_inc(stat2, 1)

                def out_norm():
                    dve.wait_ge(rstd2, 2 * g + 1)
                    for t in range(TG):
                        nc.vector.tensor_scalar(oz[:, t], oz[:, t], mv2[:, 0, t, 0:1], rs2[:, 0, 1, t:t + 1],
                                                ALU.subtract, ALU.mult).then_inc(zo_ok, 1)

                def low_z(k):
                    dve.wait_ge(tz_hi, 2 * g + k + 1)
                    nc.vector.tensor_tensor(zT[:, 1, k], psZ[:, k], f32(zT[:, 0, k]), ALU.subtract).then_inc(tz_lo, 1)

                def x_read(h):
                    dve.wait_ge(a_mm, 2 * g + h + 1)
                    dve.wait_ge(xb_ok, g + 1)
                    pair = X[:, bass.ds(TG * g + 2 * h, 2), :].rearrange("p t c -> p (t c)")
                    nc.vector.tensor_tensor(pair, psO[:], pair, ALU.add).then_inc(x_ev, 1)
                    wait(dve, x_ev, 2 * g + h + 1)
                    for t in (2 * h, 2 * h + 1):
                        nc.vector.bn_stats(bn2[:, 1, t], tile(t)).then_inc(self2, 1)
                        wait(dve, self2, 8 * g + TG + t + 1)
                        nc.vector.bn_aggr(mv2[:, 1, t], bn2[:, 1, t]).then_inc(stat2, 1)

                def x_norm():
                    dve.wait_ge(rstd2, 2 * g + 2)
                    if later(g, 1):
                        dve.wait_ge(h2_ok, TG * g)
                    for t in range(TG):
                        nc.vector.tensor_scalar(z2[:, t], tile(t), mv2[:, 1, t, 0:1], rs2[:, 1, 1, t:t + 1],
                                                ALU.subtract, ALU.mult).then_inc(z2_ok, 1)

                def low_h(k):
                    dve.wait_ge(th_hi, 2 * g + k + 1)
                    nc.vector.tensor_tensor(h2T[:, q, 1, k], psZ[:, k], f32(h2T[:, q, 0, k]), ALU.subtract
                                            ).then_inc(th_lo, 1)

                def low_g(m):
                    if ffn_on:
                        dve.wait_ge(u_hi, MK * f + m + 1)
                        nc.vector.tensor_tensor(glo[:, m % 3], gf[:, m % 2], f32(ghi[:, m % 3]), ALU.subtract
                                                ).then_inc(u_lo, 1)

                ROUTE = 20
                n = [0]

                def step(ins):
                    n[0] += 1
                    ins.then_inc(rt_dve, 1)
                    wait(dve, rt_dve, ROUTE * f + n[0])

                def gate_read():
                    dve.wait_ge(gt_mm, f + 1)
                    nc.vector.tensor_tensor(lg[:], psM[:, GATE:GATE + TG * E].rearrange("p (t e) -> p t e", e=E),
                                            gb_row[:].unsqueeze(1).broadcast_to([P, TG, E]), ALU.add
                                            ).then_inc(gt_ev, 1)

                def choose():
                    wait(dve, gt_sc, f + 1)
                    for t in range(TG):
                        step(nc.vector.max(mx[:, t], sc[:, t]))
                    for t in range(TG):
                        step(nc.vector.max_index(ix[:, t], mx[:, t], sc[:, t]))
                    step(nc.vector.tensor_copy(ixf[:], ix[:, :, 0:TOPK]))
                    for k in range(TOPK):
                        step(nc.vector.tensor_tensor(oh[:, k], iota_e[:].unsqueeze(1).broadcast_to([P, TG, E]),
                                                     ixf[:, :, k:k + 1].broadcast_to([P, TG, E]), ALU.is_equal))
                    nc.vector.tensor_tensor(ohb[:], oh[:, 0], oh[:, 1], ALU.add).then_inc(rt_oh, 1)
                    step(nc.vector.tensor_tensor(dn[:, 0], mx[:, :, 0], mx[:, :, 1], ALU.add))
                    step(nc.vector.tensor_scalar(dn[:, 0], dn[:, 0], EPS, None, ALU.add))
                    step(nc.vector.reciprocal(dn[:, 1], dn[:, 0]))
                    step(nc.vector.scalar_tensor_tensor(wt[:], mx[:, :, 0:TOPK], 0.1,
                                                        dn[:, 1].unsqueeze(2).broadcast_to([P, TG, TOPK]),
                                                        ALU.mult, ALU.mult))
                    for k in range(TOPK):
                        last = nc.vector.tensor_tensor(wd[:, k], oh[:, k], wt[:, :, k:k + 1].broadcast_to([P, TG, E]),
                                                       ALU.mult)
                    step(last)
                    nc.vector.tensor_tensor(h2[:, r, :, C + 1:C + 1 + E], wd[:, 0], wd[:, 1], ALU.add)
                    nc.vector.tensor_copy(h2[:, r, :, C:C + 1].bitcast(U32), idt[:, bass.ds(TG * f, TG)].unsqueeze(2))

                def place():
                    dve.wait_ge(rt_mm, f + 1)
                    step(nc.vector.tensor_tensor(rk[:], psM[:, RANK:RANK + TG * E].rearrange("p (t e) -> p t e", e=E),
                                                 run[:].unsqueeze(1).broadcast_to([P, TG, E]), ALU.add))
                    step(nc.vector.tensor_tensor(rk[:], rk[:], reg_e[:].unsqueeze(1).broadcast_to([P, TG, E]), ALU.add))
                    step(nc.vector.tensor_tensor(run[:], psM[:, TOTAL:TOTAL + E], run[:], ALU.add))
                    for k in range(TOPK):
                        nc.vector.tensor_tensor(rk2[:], rk[:], oh[:, k], ALU.mult).then_inc(pf_ok, 1)
                        dve.wait_ge(pf_ok, 2 * TOPK * f + 2 * k + 1)
                        nc.vector.tensor_reduce(pf[:, :, k], rk2[:], AX.X, ALU.add).then_inc(pf_ok, 1)
                        dve.wait_ge(pf_ok, 2 * TOPK * f + 2 * k + 2)
                    step(nc.vector.tensor_copy(post[:, r], pf[:]))
                    assert n[0] == ROUTE
                    nc.vector.sem_inc(pos_ok, 1)

                def shared_read():
                    dve.wait_ge(d_mm, MK * f + MK)
                    if later(f, 1):
                        dve.wait_ge(sh_st, 16 * f)
                    for h in range(2):
                        nc.vector.scalar_tensor_tensor(sh[:, 2 * h:2 * h + 2],
                                                       psY[:, h].rearrange("p (t c) -> p t c", c=C), 0.1,
                                                       sbd_row[:].unsqueeze(1).broadcast_to([P, 2, C]),
                                                       ALU.mult, ALU.add).then_inc(sh_ev, 1)

                if att_on:
                    norm_read()
                if ffn_on:
                    gate_read()
                if att_on:
                    norm_inverse()
                    out_read(0)
                low_g(0)
                if ffn_on:
                    choose()
                if att_on:
                    out_read(1)
                low_g(1)
                if att_on:
                    out_norm()
                low_g(2)
                if ffn_on:
                    place()
                if att_on:
                    low_z(0)
                    low_z(1)
                low_g(3)
                if att_on:
                    x_read(0)
                low_g(4)
                if att_on:
                    x_read(1)
                low_g(5)
                if att_on:
                    x_norm()
                low_g(6)
                low_g(7)
                if ffn_on:
                    shared_read()
                if att_on:
                    low_h(0)
                    low_h(1)

            pf_ok = sem("pf_ok")
            staggered(dve, body)

        @block.gpsimd
        def _(pool):
            def body(g, q, att_on, ffn_on):
                f, r = g - 1, 1 - q

                def rstd(i):
                    wait(pool, stat2, 8 * g + TG * (i + 1))
                    nc.gpsimd.tensor_scalar(rs2[:, i, 0], mv2[:, i, :, 1], EPS_LN, None, ALU.add).then_inc(rse2, 1)
                    wait(pool, rse2, 2 * g + i + 1)
                    nc.gpsimd.tensor_tensor(rs2[:, i, 1], rs2[:, i, 0], expo[:, 1, 0:TG], ALU.pow).then_inc(rstd2, 1)

                def bias():
                    xg = X[:, bass.ds(TG * g, TG), :]
                    nc.gpsimd.tensor_tensor(xg, xg, bo_row[:].unsqueeze(1).broadcast_to([P, TG, C]), ALU.add
                                            ).then_inc(xb_ok, 1)

                def scatter():
                    wait(pool, pos_ok, f + 1)
                    for t in range(TG):
                        for k in range(TOPK):
                            nc.gpsimd.indirect_dma_start(
                                out=hs[:, :], out_offset=bass.IndirectOffsetOnAxis(ap=post[:, r, t, k:k + 1], axis=0),
                                in_=h2[:, r, t], in_offset=None).then_inc(scat, 16)

                def modulate():
                    for t in range(TG):
                        wait(pool, z2_ok, TG * g + t + 1)
                        nc.gpsimd.tensor_tensor(z2[:, t], z2[:, t], scale_b[:], ALU.mult).then_inc(h2_ml, 1)
                        wait(pool, h2_ml, TG * g + t + 1)
                        if t == 0 and later(g, 2):
                            wait(pool, th_mm, 2 * g - 2)
                        nc.gpsimd.tensor_tensor(h2[:, q, t, 0:C], z2[:, t], shift_b[:], ALU.add).then_inc(h2_ok, 1)

                if later(g, 2):
                    wait(pool, scat, 16 * TG * TOPK * (g - 1))
                if att_on:
                    bias()
                    rstd(0)
                if ffn_on:
                    scatter()
                if att_on:
                    rstd(1)
                    modulate()

            nc.gpsimd.memset(h2[:, :, :, C:ROW], 0.0)
            staggered(pool, body)

        @block.sync
        def _(sp):
            with sp.Fori(0, NG) as f:
                sp.wait_ge(sh_ev, 2 * f + 2)
                sp.dma_start(shd_v[:, bass.ds(TG * f, TG), :], sh[:]).then_inc(sh_st, 16)
            sp.wait_ge(sh_st, 16 * NG)

    b3 = Map(nc, phase)
    W = CK * INNER
    wup = b3("wup", [P, 2, 2, CK, INNER], F32R)
    wdn = b3("wdn", [P, 2, 2, MK, C], F32R)
    raw_up = b3("raw_up", [P, CK, INNER], F32)
    raw_dn = b3("raw_dn", [P, MK, C], F32)
    ubias = b3("ubias", [P, E * MK], F32)
    dbias = b3("dbias", [P, E, C], F32)
    hin = b3("hin", [P, 2, 2, C], F32)
    meta = b3("meta", [P, 2, 2, META], F32)
    eT = b3("eT", [P, 2, 2, CK, TR], F32R)
    gu = b3("gu", [P, 2, 2, TR], F32)
    gTh = b3("gTh", [P, 2, MK, TR], F32R)
    gTl = b3("gTl", [P, 2, MK, TR], F32R)
    yc = b3("yc", [P, 2, C], F32)
    yb = b3("yb", [P, 2, 2, C], F32)
    ub_raw = b3("ub_raw", [E * MK, P], F32)
    io_t = b3("io_t", [P, ETL], F32)
    io_k = b3("io_k", [P, E, NT // 2], F32)
    tcmp = b3("tcmp", [P, E, NT // 2], F32)
    ntl = b3("ntl", [P, E], F32)
    used = b3("used", [P, E], F32)
    upto = b3("upto", [P, E, E], F32)
    tsel = b3("tsel", [P, E, E], F32)
    tend = b3("tend", [P, E], F32)
    tbeg = b3("tbeg", [P, E], F32)
    nxt = b3("nxt", [P, E], F32)
    jump = b3("jump", [P, E], F32)
    gecm = b3("gecm", [P, ETL, E], F32)
    gej = b3("gej", [P, ETL, E], F32)
    tabf = b3("tabf", [P, 4, ETL], F32)
    pari = b3("pari", [P, ETL], I32)
    padf = b3("padf", [P, 2, E], F32)
    padp = b3("padp", [P, 2, E], U32)
    iop = b3("iop", [P, 1], F32)
    prow = b3("prow", [P, ROW], F32)

    tb_c, tb_d, tb_pool, pad_ok, pad_st, db_in, ub_in, ub_mm, end_st = [sem(n) for n in (
        "tb_c", "tb_d", "tb_pool", "pad_ok", "pad_st", "db_in", "ub_in", "ub_mm", "end_st")]
    with ExitStack() as mem, nc.Block() as block:
        psB = mem.enter_context(nc.psum_tensor("psB", [P, E * MK], F32))

        @block.gpsimd
        def _(pool):
            n = [0]

            def link(ins):
                n[0] += 1
                ins.then_inc(tb_pool, 1)
                wait(pool, tb_pool, n[0])

            link(nc.gpsimd.iota(io_t[:], [[1, ETL]], base=0, channel_multiplier=0,
                                allow_small_or_imprecise_dtypes=True))
            link(nc.gpsimd.iota(io_k[:], [[0, E], [TR, NT // 2]], base=0, channel_multiplier=0,
                                allow_small_or_imprecise_dtypes=True))
            link(nc.gpsimd.iota(iop[:], [[1, 1]], base=0, channel_multiplier=1,
                                allow_small_or_imprecise_dtypes=True))
            link(nc.gpsimd.memset(upto[:], 1.0))
            link(nc.gpsimd.affine_select(out=upto[:], in_=upto[:], compare_op=ALU.is_ge, fill=0.0, base=0,
                                         pattern=[[1, E], [-1, E]], channel_multiplier=0))
            link(nc.gpsimd.memset(prow[:], 0.0))
            nc.gpsimd.iota(prow[:, C:C + 1].bitcast(U32), [[0, 1]], base=N, channel_multiplier=1).then_inc(tb_c, 1)
            pool.wait_ge(pad_ok, 1)
            pool.wait_ge(tb_c, 1)
            for e in range(E):
                for h in range(2):
                    nc.gpsimd.indirect_dma_start(out=hs[:, :],
                                                 out_offset=bass.IndirectOffsetOnAxis(ap=padp[:, h, e:e + 1], axis=0),
                                                 in_=prow[:], in_offset=None).then_inc(pad_st, 16)
            pool.wait_ge(pad_st, 32 * E)
            pool.wait_ge(scat, 16 * TG * TOPK * NG)

        @block.sync
        def _(sp):
            sp.dma_start(ub_raw[:], up_b.rearrange("e (m p) -> (e m) p", p=P)).then_inc(ub_in, 16)
            sp.dma_start(dbias[:], down_b.partition_broadcast(P)).then_inc(db_in, 16)
            sp.wait_ge(tb_c, 1)
            for h in range(2):
                sp.dma_start(hs[E * REG + h * P:E * REG + (h + 1) * P, :], prow[:]).then_inc(end_st, 16)
            sp.dma_start(shd[N:N + P, :], prow[:, 0:C]).then_inc(end_st, 16)
            sp.wait_ge(end_st, 48)
            sp.wait_ge(db_in, 16)

        @block.tensor
        def _(pe):
            pe.wait_ge(ub_in, 16)
            nc.tensor.transpose(psB[:], ub_raw[:], ident[0:E * MK, 0:E * MK]).then_inc(ub_mm, 1)

        @block.scalar
        def _(act):
            act.wait_ge(ub_mm, 1)
            nc.scalar.copy(ubias[:], psB[:])

        @block.vector
        def _(dve):
            n = [0]

            def link(ins):
                n[0] += 1
                ins.then_inc(tb_d, 1)
                dve.wait_ge(tb_d, n[0])

            per_tile = lambda a: a.unsqueeze(1).broadcast_to([P, ETL, a.shape[-1]])
            dve.wait_ge(tb_c, 1)
            link(nc.vector.tensor_tensor(padf[:, 0], run[:], reg_e[:], ALU.add))
            link(nc.vector.tensor_scalar(padf[:, 0], padf[:, 0], iop[:, 0:1], None, ALU.add))
            link(nc.vector.tensor_scalar(padf[:, 1], padf[:, 0], float(P), None, ALU.add))
            nc.vector.tensor_copy(padp[:], padf[:]).then_inc(pad_ok, 1)
            link(nc.vector.tensor_tensor(tcmp[:], run[:].unsqueeze(2).broadcast_to([P, E, NT // 2]), io_k[:], ALU.is_gt))
            link(nc.vector.tensor_reduce(ntl[:], tcmp[:], AX.X, ALU.add))
            link(nc.vector.tensor_scalar(used[:], run[:], 0.0, None, ALU.is_gt))
            link(nc.vector.tensor_tensor(tsel[:], upto[:], ntl[:].unsqueeze(1).broadcast_to([P, E, E]), ALU.mult))
            link(nc.vector.tensor_reduce(tend[:], tsel[:], AX.X, ALU.add))
            link(nc.vector.tensor_tensor(tbeg[:], tend[:], ntl[:], ALU.subtract))
            link(nc.vector.tensor_tensor(tsel[:], tend[:].unsqueeze(2).broadcast_to([P, E, E]),
                                         tend[:].unsqueeze(1).broadcast_to([P, E, E]), ALU.is_ge))
            link(nc.vector.tensor_reduce(nxt[:], tsel[:], AX.X, ALU.add))
            link(nc.vector.scalar_tensor_tensor(nxt[:], nxt[:], float(E), nxt[:], ALU.is_lt, ALU.mult))
            link(nc.vector.tensor_tensor(nxt[:], nxt[:], used[:], ALU.mult))
            link(nc.vector.tensor_tensor(gecm[:], io_t[:].unsqueeze(2).broadcast_to([P, ETL, E]), per_tile(tend[:]),
                                         ALU.is_ge))
            last = gecm[:, :, 0:E - 1]
            link(nc.vector.tensor_reduce(tabf[:, 0], last, AX.X, ALU.add))
            nc.vector.tensor_copy(etab[:], tabf[:, 0])
            link(nc.vector.tensor_tensor(gej[:], gecm[:], per_tile(used[:]), ALU.mult))
            link(nc.vector.tensor_reduce(tabf[:, 1], gej[:], AX.X, ALU.add))
            link(nc.vector.tensor_copy(ktab[:], tabf[:, 1]))
            link(nc.vector.tensor_scalar(pari[:], ktab[:], 1, None, ALU.bitwise_and))
            link(nc.vector.tensor_copy(tabf[:, 3], pari[:]))
            link(nc.vector.scalar_tensor_tensor(tabf[:, 3], gecm[:, :, E - 1], 2.0, tabf[:, 3], ALU.mult, ALU.max))
            nc.vector.tensor_copy(stab[:], tabf[:, 3])
            link(nc.vector.tensor_scalar(jump[:], ntl[:], -float(TR), float(REG), ALU.mult, ALU.add))
            link(nc.vector.tensor_tensor(gej[:, :, 0:E - 1], last, per_tile(jump[:, 0:E - 1]), ALU.mult))
            link(nc.vector.tensor_reduce(tabf[:, 2], gej[:, :, 0:E - 1], AX.X, ALU.add))
            link(nc.vector.scalar_tensor_tensor(tabf[:, 2], io_t[:], float(TR), tabf[:, 2], ALU.mult, ALU.add))
            end = float(E * REG)
            link(nc.vector.tensor_scalar(tabf[:, 3], gecm[:, :, E - 1], -1.0, 1.0, ALU.mult, ALU.add))
            link(nc.vector.scalar_tensor_tensor(tabf[:, 2], tabf[:, 2], -end, tabf[:, 3], ALU.add, ALU.mult))
            link(nc.vector.tensor_scalar(tabf[:, 2], tabf[:, 2], end, None, ALU.add))
            nc.vector.tensor_copy(rtab[:], tabf[:, 2])
            link(nc.vector.tensor_tensor(gej[:], io_t[:].unsqueeze(2).broadcast_to([P, ETL, E]), per_tile(tbeg[:]),
                                         ALU.is_equal))
            link(nc.vector.tensor_tensor(gej[:], gej[:], per_tile(nxt[:]), ALU.mult))
            link(nc.vector.tensor_reduce(tabf[:, 0], gej[:], AX.X, ALU.add))
            nc.vector.tensor_copy(ntab[:], tabf[:, 0])

    up_v = up_w.rearrange("e (k p) n -> e p k n", p=P)
    down_v = down_w.rearrange("e (k p) n -> e p k n", p=P)
    names = ("up_in", "dn_in", "w_hi", "w_ok", "ht_mm", "ht_hi", "ht_lo", "eu_mm", "eu_g", "eu_hi", "eu_lo",
             "ey_mm", "ey_ev", "y_ok", "y_st")
    (up_in, dn_in, w_hi, w_ok, ht_mm, ht_hi, ht_lo, eu_mm, eu_g, eu_hi, eu_lo, ey_mm, ey_ev, y_ok,
     y_st) = [sem(n) for n in names]
    h_in = [sem(f"h_in{i}") for i in range(2)]
    m_in = [sem(f"m_in{i}") for i in range(2)]
    MC = MK // 2

    def tiles(eng, body):
        body(0, 0, True, 0)
        body(1, 1, True, 0)
        with eng.Fori(1, ET // 2) as i:
            body(2 * i, 0, True, i)
            body(2 * i + 1, 1, True, i)
        body(ET - 1, 0, False, ET // 2)

    def entry(eng, table, j, most):
        return eng.value_load(table[0:1, bass.ds(j, 1)], min_val=0, max_val=most)

    assert ET % 2 == 1
    with ExitStack() as mem, nc.Block() as block:
        psU = mem.enter_context(nc.psum_tensor("psUp", [P, MC, HALF], F32))
        psH = mem.enter_context(nc.psum_tensor("psH", [P, HALF], F32))
        psE = mem.enter_context(nc.psum_tensor("psE", [P, 2, HALF], F32))

        @block.sync
        def _(sp):
            def weights(e):
                sp.dma_start(raw_up[:], up_v[bass.ds(e, 1)].rearrange("a p k n -> p (a k) n")).then_inc(up_in, 16)
                sp.dma_start(raw_dn[:], down_v[bass.ds(e, 1)].rearrange("a p k n -> p (a k) n")).then_inc(dn_in, 16)

            def rows(j, u):
                if later(j, 2):
                    wait(sp, ht_mm, j - 1)
                row = entry(sp, rtab, j, E * REG)
                sp.dma_start(hin[:, u], hs[bass.ds(row, TR), 0:C].rearrange("(h p) c -> p h c", p=P)
                             ).then_inc(h_in[u], 16)

            def ahead(j):
                e = entry(sp, ntab, j, E - 1)
                k = entry(sp, ktab, j, E - 1)
                with sp.If_ne(sp.to_reg(e), 0):
                    wait(sp, w_ok, 2 * k + 2)
                    weights(e)

            weights(entry(sp, etab, 0, E - 1))
            rows(0, 0)
            rows(1, 1)
            ahead(0)
            with sp.Fori(1, ETL // 2) as i:
                rows(2 * i, 0)
                ahead(2 * i - 1)
                rows(2 * i + 1, 1)
                ahead(2 * i)

        @block.tensor
        def _(pe):
            def turn_h(j, u, i):
                pe.wait_ge(h_in[u], 16 * i + 16)
                if later(j, 1):
                    pe.wait_ge(ht_lo, j)
                for k in range(CK):
                    for h in range(2):
                        mm = nc.tensor.transpose(psH[:, k * TR + h * P:k * TR + (h + 1) * P],
                                                 hin[:, u, h, k * P:(k + 1) * P], ident[:])
                mm.then_inc(ht_mm, 1)

            def up(j, u):
                slot = entry(pe, stab, j, 2)
                k_exp = entry(pe, ktab, j, E)

                def free(m):
                    if later(j, 1):
                        pe.wait_ge(eu_g, MK * j - MK + m + 1)

                for s in range(2):
                    with pe.If_eq(pe.to_reg(slot), s):
                        pe.wait_ge(w_ok, 2 * k_exp + 1)
                        pe.wait_ge(ht_lo, j + 1)
                        for c in range(MC):
                            free(2 * c + 1)
                            for m in (2 * c, 2 * c + 1):
                                n = 0
                                for k in range(CK):
                                    for a, b in PASSES:
                                        mm = nc.tensor.matmul(psU[:, c, (m % 2) * TR:(m % 2 + 1) * TR],
                                                              wup[:, s, a, k, m * P:(m + 1) * P], eT[:, u, b, k],
                                                              start=(n == 0), stop=(n == 5))
                                        n += 1
                            mm.then_inc(eu_mm, 1)
                with pe.If_eq(pe.to_reg(slot), 2):
                    for c in range(MC):
                        free(2 * c + 1)
                        nc.tensor.matmul(psU[:, c, 0:1], one_f[:], one_f[:, 0:1], start=True, stop=True
                                         ).then_inc(eu_mm, 1)

            def down(j, u):
                slot = entry(pe, stab, j, 2)
                k_exp = entry(pe, ktab, j, E)
                if later(j, 2):
                    pe.wait_ge(ey_ev, j - 1)
                for s in range(2):
                    with pe.If_eq(pe.to_reg(slot), s):
                        pe.wait_ge(w_ok, 2 * k_exp + 2)
                        pe.wait_ge(eu_lo, MC * j + MC)
                        for h in range(2):
                            n = 0
                            for m in range(MK):
                                for a, b in PASSES:
                                    mm = nc.tensor.matmul(psE[:, u, h * C:(h + 1) * C],
                                                          (gTh, gTl)[a][:, u, m, h * P:(h + 1) * P], wdn[:, s, b, m],
                                                          start=(n == 0), stop=(n == 3 * MK - 1))
                                    n += 1
                        mm.then_inc(ey_mm, 1)
                with pe.If_eq(pe.to_reg(slot), 2):
                    nc.tensor.matmul(psE[:, u, 0:1], one_f[:], one_f[:, 0:1], start=True, stop=True
                                     ).then_inc(ey_mm, 1)

            turn_h(0, 0, 0)
            up(0, 0)
            turn_h(1, 1, 0)

            def body(j, u, more, i):
                if more:
                    up(j + 1, 1 - u)
                    turn_h(j + 2, u, i + 1)
                down(j, u)

            tiles(pe, body)

        @block.scalar
        def _(act):
            def split(n, s):
                for i in range(2):
                    wait(act, (up_in, dn_in)[i], 16 * n + 16)
                    src = (raw_up, raw_dn)[i][:].rearrange("p k n -> p (k n)")
                    dst = (wup, wdn)[i][:, s, 0].rearrange("p k n -> p (k n)")
                    for h in range(2):
                        at = slice(h * W // 2, (h + 1) * W // 2)
                        nc.scalar.copy(dst[:, at], src[:, at]).then_inc(w_hi, 1)

            def ahead(j):
                e = entry(act, ntab, j, E - 1)
                k = entry(act, ktab, j, E)
                with act.If_ne(act.to_reg(e), 0):
                    slot = entry(act, stab, j, 2)
                    if later(j, 1):
                        wait(act, ey_mm, j)
                    for s in range(2):
                        with act.If_eq(act.to_reg(slot), 1 - s):
                            split(k + 1, s)

            def high(j, u):
                act.wait_ge(ht_mm, j + 1)
                nc.scalar.copy(eT[:, u, 0].rearrange("p k n -> p (k n)"), psH[:]).then_inc(ht_hi, 1)

            def gelu(j, u):
                e = entry(act, etab, j, E - 1)
                for c in range(MC):
                    wait(act, eu_mm, MC * j + c + 1)
                    if later(j, 1) or c >= 2:
                        wait(act, eu_lo, MC * j + c - 1)
                    for m in range(2):
                        nc.scalar.activation(gu[:, c % 2, m], psU[:, c, m * TR:(m + 1) * TR], ACT.Gelu,
                                             bias=ubias[:, bass.ds(e * MK + 2 * c + m, 1)]).then_inc(eu_g, 1)
                    act.wait_ge(eu_g, MK * j + 2 * c + 2)
                    if later(j, 2):
                        act.wait_ge(ey_mm, j - 1)
                    nc.scalar.copy(gTh[:, u, 2 * c:2 * c + 2], gu[:, c % 2]).then_inc(eu_hi, 1)

            def body(j, u, more, i):
                ahead(j)
                if more:
                    gelu(j + 1, 1 - u)
                    high(j + 2, u)

            split(0, 0)
            high(0, 0)
            gelu(0, 0)
            high(1, 1)
            tiles(act, body)

        @block.vector
        def _(dve):
            def split(n, s):
                for i in range(2):
                    src = (raw_up, raw_dn)[i][:].rearrange("p k n -> p (k n)")
                    hi, lo = [(wup, wdn)[i][:, s, a].rearrange("p k n -> p (k n)") for a in range(2)]
                    for h in range(2):
                        at = slice(h * W // 2, (h + 1) * W // 2)
                        dve.wait_ge(w_hi, 4 * n + 2 * i + h + 1)
                        ins = nc.vector.tensor_tensor(lo[:, at], src[:, at], f32(hi[:, at]), ALU.subtract)
                    ins.then_inc(w_ok, 1)

            def ahead(j):
                e = entry(dve, ntab, j, E - 1)
                k = entry(dve, ktab, j, E)
                with dve.If_ne(dve.to_reg(e), 0):
                    slot = entry(dve, stab, j, 2)
                    for s in range(2):
                        with dve.If_eq(dve.to_reg(slot), 1 - s):
                            split(k + 1, s)

            def low(j, u):
                dve.wait_ge(ht_hi, j + 1)
                nc.vector.tensor_tensor(eT[:, u, 1].rearrange("p k n -> p (k n)"), psH[:],
                                        f32(eT[:, u, 0].rearrange("p k n -> p (k n)")), ALU.subtract).then_inc(ht_lo, 1)

            def low_g(j, u):
                for c in range(MC):
                    dve.wait_ge(eu_hi, MC * j + c + 1)
                    nc.vector.tensor_tensor(gTl[:, u, 2 * c:2 * c + 2], gu[:, c % 2], f32(gTh[:, u, 2 * c:2 * c + 2]),
                                            ALU.subtract).then_inc(eu_lo, 1)

            def result(j, u, i):
                e = entry(dve, etab, j, E - 1)
                wait(dve, ey_mm, j + 1)
                if later(j, 1):
                    wait(dve, y_ok, j)
                nc.vector.tensor_tensor(yc[:], psE[:, u].rearrange("p (h c) -> p h c", c=C),
                                        dbias[:, bass.ds(e, 1), :].broadcast_to([P, 2, C]), ALU.add).then_inc(ey_ev, 1)
                wait(dve, ey_ev, j + 1)
                wait(dve, m_in[u], 16 * i + 16)
                nc.vector.tensor_tensor(yb[:, u], yc[:],
                                        meta[:, u, :, bass.ds(e + 1, 1)].broadcast_to([P, 2, C]), ALU.mult
                                        ).then_inc(y_ok, 1)

            def body(j, u, more, i):
                ahead(j)
                if more:
                    low_g(j + 1, 1 - u)
                    low(j + 2, u)
                result(j, u, i)

            split(0, 0)
            low(0, 0)
            low_g(0, 0)
            low(1, 1)
            tiles(dve, body)

        @block.gpsimd
        def _(pool):
            def tails(j, u):
                row = entry(pool, rtab, j, E * REG)
                pool.dma_start(meta[:, u], hs[bass.ds(row, TR), C:ROW].rearrange("(h p) c -> p h c", p=P)
                               ).then_inc(m_in[u], 16)

            def body(j, u, more, i):
                wait(pool, y_ok, j + 1)
                for h in range(2):
                    nc.gpsimd.indirect_dma_start(
                        out=shd[:, :], out_offset=bass.IndirectOffsetOnAxis(ap=meta[:, u, h, 0:1].bitcast(U32), axis=0),
                        in_=yb[:, u, h], in_offset=None, compute_op=ALU.add).then_inc(y_st, 16)
                    wait(pool, y_st, 16 * (2 * j + h + 1))
                if more:
                    tails(j + 2, u)

            tails(0, 0)
            tails(1, 1)
            tiles(pool, body)
            pool.wait_ge(m_in[0], 16 * (ETL // 2))
            pool.wait_ge(m_in[1], 16 * (ETL // 2))

    b4 = Map(nc, phase)
    acc = b4("acc", [P, 2, TG, C], F32)
    outb = b4("outb", [P, 2, TG, C], F32)
    top = b4("top", [P, 2, TG], F32)
    f_s, f_o = [[sem(f"{n}{i}") for i in range(2)] for n in ("f_s", "f_o")]
    f_c, f_a, f_ok = [sem(n) for n in ("f_c", "f_a", "f_ok")]

    def pairs(eng, body):
        body(0, 0, 0)
        body(1, 1, 0)
        with eng.Fori(1, NG // 2) as i:
            body(2 * i, 0, i)
            body(2 * i + 1, 1, i)

    with nc.Block() as block:
        @block.sync
        def _(sp):
            def body(g, q, i):
                if later(g, 2):
                    sp.wait_ge(f_ok, g - 1)
                sp.dma_start(acc[:, q], shd_v[:, bass.ds(TG * g, TG), :]).then_inc(f_s[q], 16)

            pairs(sp, body)

        @block.gpsimd
        def _(pool):
            def body(g, q, i):
                wait(pool, f_a, TG * g + TG)
                if later(g, 2):
                    wait(pool, f_o[q], 16 * i)
                nc.gpsimd.tensor_tensor(outb[:, q], X[:, bass.ds(TG * g, TG), :], acc[:, q], ALU.add).then_inc(f_ok, 1)

            pairs(pool, body)

        @block.scalar
        def _(act):
            def body(g, q, i):
                act.wait_ge(f_ok, g + 1)
                act.dma_start(out_v[:, bass.ds(TG * g, TG), :], outb[:, q]).then_inc(f_o[q], 16)

            pairs(act, body)
            for q in range(2):
                act.wait_ge(f_o[q], 16 * (NG // 2))

        @block.vector
        def _(dve):
            def body(g, q, i):
                n = [0]
                STEPS = 3

                def link(ins):
                    n[0] += 1
                    ins.then_inc(f_c, 1)
                    dve.wait_ge(f_c, STEPS * g + n[0])

                dve.wait_ge(f_s[q], 16 * i + 16)
                link(nc.vector.tensor_reduce(top[:, 0], acc[:, q], AX.X, ALU.max, apply_absolute_value=True))
                link(nc.vector.tensor_scalar(top[:, 0], top[:, 0], EPS, None, ALU.add))
                link(nc.vector.reciprocal(top[:, 1], top[:, 0]))
                for t in range(TG):
                    nc.vector.scalar_tensor_tensor(acc[:, q, t], acc[:, q, t], top[:, 1, t:t + 1], gate_fb[:],
                                                   ALU.mult, ALU.mult).then_inc(f_a, 1)

            pairs(dve, body)
    ctx.close()


_INS = ["L0_attn_x", "L0_attn_Wq", "L0_attn_bq", "L0_attn_Wk", "L0_attn_bk", "L0_attn_Wv", "L0_attn_bv",
        "L0_attn_Wo", "L0_attn_bo", "L0_attn_ln_g", "L0_attn_ln_b", "L0_ffn_gate_w", "L0_ffn_bias",
        "L0_ffn_up_w", "L0_ffn_up_b", "L0_ffn_down_w", "L0_ffn_down_b", "L0_ffn_sw_up", "L0_ffn_sb_up",
        "L0_ffn_sw_down", "L0_ffn_sb_down", "L0_c", "L0_wmod"]


def kernel(**inputs):
    import numpy as _np
    import concourse.bacc as _bacc
    from concourse.bass_utils import run_bass_kernel_spmd as _run

    nc = _bacc.Bacc("TRN2", target_bir_lowering=False, num_devices=1)
    arrays, args = {}, []
    for name in _INS:
        a = _np.ascontiguousarray(inputs[name])
        arrays[f"in_{name}"] = a
        args.append(nc.dram_tensor(f"in_{name}", a.shape, F32, kind="ExternalInput").ap())
    scratch = [nc.dram_tensor("expert_in", (E * REG + TR, ROW), F32, kind="Internal").ap(),
               nc.dram_tensor("ffn_out", (N + P, C), F32, kind="Internal").ap()]
    out = nc.dram_tensor("out", (1, N, C), F32, kind="ExternalOutput").ap()
    adaln_block(nc, *args, *scratch, out)
    r = _run(nc, [arrays], core_ids=[0])
    return r.results[0]["out"]
```

```python
from contextlib import ExitStack

import concourse.bass as bass
from concourse import mybir

ALU = mybir.AluOpType
ACT = mybir.ActivationFunctionType
F32 = mybir.dt.float32
F32R = mybir.dt.float32r
BF16 = mybir.dt.bfloat16
U32 = mybir.dt.uint32
I32 = mybir.dt.int32
AX = mybir.AxisListType

P = 128
N, C = 4096, 256
NT = N // P
TG = 4
NG = NT // TG
CK = C // P
HEADS, D = 16, 16
KV = 2
E, TOPK = 8, 2
INNER = 4 * C
MK = INNER // P
TR = 2 * P
REG = N + TR
ET = N * TOPK // TR + E - 1
ETL = ET + 1
META = 16
ROW = C + META
SLOT = 4 * CK * INNER
EPS_LN, EPS = 1e-5, 1e-6
HALF = 512
SRAW = 229312 - 2 * CK * INNER * 4


class Map:

    def __init__(self, nc, start):
        self.nc, self.at = nc, start

    def __call__(self, name, shape, dtype):
        size = 1
        for n in shape[1:]:
            size *= n
        size *= mybir.dt.size(dtype)
        t = self.nc.alloc_sbuf_tensor_at(name, shape, dtype, offset=self.at)
        self.at += -(-size // 64) * 64
        return t


def adaln_block(nc, x, Wq, bq, Wk, bk, Wv, bv, Wo, bo, ln_g, ln_b, gate_w, gate_b, up_w, up_b,
                down_w, down_b, sw_up, sb_up, sw_down, sb_down, c, wmod, hs, shd, out):
    f32 = lambda ap: ap.bitcast(F32)
    ctx = ExitStack()
    sem = lambda name: ctx.enter_context(nc.semaphore(name))
    x_v = x[0].rearrange("(p t) c -> p t c", t=NT)
    out_v = out[0].rearrange("(p t) c -> p t c", t=NT)
    shd_v = shd[0:N, :].rearrange("(p t) c -> p t c", t=NT)

    waited = sem("waited")

    def wait(eng, semaphore, value):
        eng.wait_ge(semaphore, value)
        if not isinstance(value, int):
            eng.sem_inc(waited, 1)

    def rsqrt(link, y, x, t, between=lambda n: None):
        link(nc.vector.tensor_scalar(t.bitcast(I32), x.bitcast(I32), 1, None, ALU.logical_shift_right))
        link(nc.vector.tensor_scalar(y.bitcast(I32), t.bitcast(I32), -1.0, float(0x5F3759DF), ALU.mult, ALU.add))
        for n in range(3):
            between(n)
            link(nc.vector.tensor_tensor(t, y, y, ALU.mult))
            link(nc.vector.scalar_tensor_tensor(t, x, -0.5, t, ALU.mult, ALU.mult))
            link(nc.vector.scalar_tensor_tensor(y, t, 1.5, y, ALU.add, ALU.mult))

    RSQRT = 11

    keep = Map(nc, -(-nc.sbuf_base // 64) * 64)
    ident = keep("ident", [P, P], F32)
    one_f = keep("one_f", [P, P], F32)
    X = keep("X", [P, NT, C], F32)
    scale_a = keep("scale_a", [P, C], F32)
    shift_a = keep("shift_a", [P, C], F32)
    mv1 = keep("mv1", [P, NT, 2], F32)
    rs1 = keep("rs1", [P, 3, NT], F32)
    gate_a = keep("gate_a", [P, C], F32)
    scale_b = keep("scale_b", [P, C], F32)
    shift_b = keep("shift_b", [P, C], F32)
    gate_fb = keep("gate_fb", [P, C], F32)
    bo_row = keep("bo_row", [P, C], F32)
    sbd_row = keep("sbd_row", [P, C], F32)
    idt = keep("idt", [P, NT], U32)
    run = keep("run", [P, E], F32)
    expo = keep("expo", [P, 2, 128], F32)
    iota_e = keep("iota_e", [P, E], F32)
    reg_e = keep("reg_e", [P, E], F32)
    etab = keep("etab", [P, ETL], I32)
    ktab = keep("ktab", [P, ETL], I32)
    stab = keep("stab", [P, ETL], I32)
    rtab = keep("rtab", [P, ETL], I32)
    ntab = keep("ntab", [P, ETL], I32)
    ubias = keep("ubias", [P, E * MK], F32)
    phase = keep.at

    att = Map(nc, phase)
    su = att("su", [P, 2, CK, INNER], F32R)
    sd = att("sd", [P, 2, MK, C], F32R)
    wo = att("wo", [P, 2, CK, C], F32R)
    gw = att("gw", [P, 2, CK, E], F32R)
    gb_row = att("gb_row", [P, E], F32)
    sbu = att("sbu", [P, MK], F32)
    state = att("state", [P, CK, P], F32)
    heads = att("heads", [P, P // D], F32)
    tri = att("tri", [P, P], BF16)
    one_b = att("one_b", [P, P], BF16)
    q_at = att.at
    qT = att("qT", [P, CK, NT * P], F32)
    after_q = att.at

    p1w = Map(nc, after_q)
    wkq = p1w("wkq", [P, 2, CK, (KV + 1) * C], F32R)
    wv = p1w("wv", [P, CK, KV * C], F32)
    bk_row = p1w("bk_row", [P, KV * C], F32)
    bv_row = p1w("bv_row", [P, KV * C], F32)
    bq_col = p1w("bq_col", [P, CK], F32)
    blocks = p1w("blocks", [P, P], F32)

    st = Map(nc, p1w.at)
    wnat = st("wnat", [P, 2 * KV + 2, CK, C], F32)
    mw = st("mw", [P, CK, 6 * C], F32)
    c_col = st("c_col", [P, CK], F32)
    c_act = st("c_act", [P, CK], F32)
    c_rows = st("c_rows", [P, CK, P], F32)
    mod = st("mod", [P, 6, C], F32)
    ga_abs = st("ga_abs", [P, 2, C], F32)
    ga_sgn = st("ga_sgn", [P, 2, C], F32)
    eye2 = st("eye2", [P, CK, C], F32)
    wtmp = st("wtmp", [P, CK, C], F32)
    lng_col = st("lng_col", [P, CK], F32)
    lnb_col = st("lnb_col", [P, CK], F32)
    zero_c = st("zero_c", [P, 1], F32)
    lnb_rows = st("lnb_rows", [P, CK, P], F32)
    gw_raw = st("gw_raw", [P, CK, E], F32)
    ub_raw = st("ub_raw", [E * MK, P], F32)
    bn0 = st("bn0", [P, NT, 6], F32)
    sraw = Map(nc, SRAW)("sraw", [P, 2, CK, INNER], F32)

    ld_c, ld_mod, ld_w, ld_row, ld_sh = [sem(n) for n in ("ld_c", "ld_mod", "ld_w", "ld_row", "ld_sh")]
    consts, c_silu, c_spread = sem("consts"), sem("c_silu"), sem("c_spread")
    mod_mm, mod_ok, wt_mm, wt_ok, dve0, pool0 = [sem(n) for n in (
        "mod_mm", "mod_ok", "wt_mm", "wt_ok", "dve0", "pool0")]
    bo_mm, x_stat, ub_mm = sem("bo_mm"), sem("x_stat"), sem("ub_mm")
    wo_ga, wo_hi = sem("wo_ga"), sem("wo_hi")
    XD = 4
    x_in = [sem(f"x_in{q}") for q in range(XD)]

    with ExitStack() as mem, nc.Block() as block:
        ps = [mem.enter_context(nc.psum_tensor(f"set_ps{i}", [P, HALF], F32)) for i in range(8)]
        N_W, N_ROW = 6, 11

        @block.sync
        def _(sp):
            narrow = ctx.enter_context(nc.allow_non_contiguous_dma(reason="short vectors, a channel per partition"))
            sp.dma_start(c_col[:], c.rearrange("a (k p) -> p (a k)", p=P)).then_inc(ld_c, 16)
            with sp.Fori(0, NG // XD) as i:
                for q in range(XD):
                    group = bass.ds((XD * i + q) * TG, TG)
                    sp.dma_start(X[:, group, :], x_v[:, group, :]).then_inc(x_in[q], 16)
                for q in range(XD):
                    wait(sp, x_in[q], 16 * i + 16)
            sp.dma_start(sraw[:, 0], sw_up.rearrange("(k p) n -> p k n", p=P)).then_inc(ld_sh, 16)
            sp.dma_start(sraw[:, 1].rearrange("p k n -> p (k n)").rearrange("p (k n) -> p k n", k=MK),
                         sw_down.rearrange("(k p) n -> p k n", p=P)).then_inc(ld_sh, 16)

        @block.gpsimd
        def _(pool):
            step = [0]

            def link(ins):
                step[0] += 1
                ins.then_inc(pool0, 1)
                pool.wait_ge(pool0, step[0])

            link(nc.gpsimd.memset(ident[:], 0.0))
            link(nc.gpsimd.affine_select(out=ident[:], in_=ident[:], compare_op=ALU.not_equal, fill=1.0, base=0,
                                         pattern=[[-1, P]], channel_multiplier=1))
            link(nc.gpsimd.memset(eye2[:], 0.0))
            for k in range(CK):
                link(nc.gpsimd.affine_select(out=eye2[:, k], in_=eye2[:, k], compare_op=ALU.not_equal, fill=1.0,
                                             base=P * k, pattern=[[-1, C]], channel_multiplier=1))
            link(nc.gpsimd.memset(one_f[:], 1.0))
            link(nc.gpsimd.memset(one_b[:], 1.0))
            link(nc.gpsimd.memset(run[:], 0.0))
            link(nc.gpsimd.memset(expo[:, 0], 0.5))
            link(nc.gpsimd.memset(expo[:, 1], -0.5))
            link(nc.gpsimd.affine_select(out=tri[:], in_=one_b[:], compare_op=ALU.is_gt, fill=0.0, base=0,
                                         pattern=[[1, P]], channel_multiplier=-1))
            link(nc.gpsimd.affine_select(out=heads[:], in_=one_f[:, :P // D], compare_op=ALU.is_ge, fill=0.0,
                                         base=0, pattern=[[-D, P // D]], channel_multiplier=1))
            link(nc.gpsimd.affine_select(out=heads[:], in_=heads[:], compare_op=ALU.is_ge, fill=0.0,
                                         base=D - 1, pattern=[[D, P // D]], channel_multiplier=-1))
            bl = blocks[:].rearrange("p (h d) -> p h d", d=D)
            link(nc.gpsimd.affine_select(out=bl, in_=one_f[:].rearrange("p (h d) -> p h d", d=D),
                                         compare_op=ALU.is_ge, fill=0.0,
                                         base=0, pattern=[[-D, P // D], [0, D]], channel_multiplier=1))
            link(nc.gpsimd.affine_select(out=bl, in_=bl, compare_op=ALU.is_ge, fill=0.0,
                                         base=D - 1, pattern=[[D, P // D], [0, D]], channel_multiplier=-1))
            link(nc.gpsimd.iota(idt[:], [[1, NT]], base=0, channel_multiplier=NT))
            link(nc.gpsimd.iota(iota_e[:], [[1, E]], base=0, channel_multiplier=0,
                                allow_small_or_imprecise_dtypes=True))
            link(nc.gpsimd.memset(zero_c[:], 0.0))
            nc.gpsimd.iota(reg_e[:], [[REG, E]], base=0, channel_multiplier=0,
                           allow_small_or_imprecise_dtypes=True).then_inc(consts, 1)
            pool.wait_ge(ld_row, 16 * N_ROW)
            link(nc.gpsimd.tensor_copy(gw[:, 0], gw_raw[:]))
            link(nc.gpsimd.tensor_tensor(gw[:, 1], gw_raw[:], f32(gw[:, 0]), ALU.subtract))
            nc.gpsimd.tensor_scalar(sbd_row[:], sbd_row[:], 0.1, None, ALU.mult)
            pool.wait_ge(wt_ok, 6)
            pool.wait_ge(bo_mm, 1)
            nc.gpsimd.tensor_tensor(wtmp[:], wtmp[:], gate_a[:].unsqueeze(1).broadcast_to([P, CK, C]), ALU.mult
                                    ).then_inc(wo_ga, 1)
            pool.wait_ge(wo_hi, CK + 1)
            nc.gpsimd.tensor_tensor(wo[:, 1], wtmp[:], f32(wo[:, 0]), ALU.subtract)

        @block.scalar
        def _(act):
            act.dma_start(mw[:], wmod.rearrange("(k p) n -> p k n", p=P)).then_inc(ld_mod, 16)
            act.wait_ge(ld_c, 16)
            nc.scalar.activation(c_act[:], c_col[:], ACT.Silu).then_inc(c_silu, 1)
            for i, w in enumerate((Wq, Wk[0], Wk[1], Wv[0], Wv[1], Wo)):
                act.dma_start(wnat[:, i], w.rearrange("(k p) n -> p k n", p=P)).then_inc(ld_w, 16)
            for dst, src in (
                (bk_row[:], bk.rearrange("k c -> (k c)").partition_broadcast(P)),
                (bv_row[:], bv.rearrange("k c -> (k c)").partition_broadcast(P)),
                (bo_row[:], bo.partition_broadcast(P)), (sbd_row[:], sb_down.partition_broadcast(P)),
                (gb_row[:], gate_b.partition_broadcast(P)),
                (bq_col[:], bq.rearrange("(k p) -> p k", p=P)),
                (lng_col[:], ln_g.rearrange("(k p) -> p k", p=P)),
                (lnb_col[:], ln_b.rearrange("(k p) -> p k", p=P)),
                (sbu[:], sb_up.rearrange("(k p) -> p k", p=P)),
                (gw_raw[:], gate_w.rearrange("(k p) e -> p k e", p=P)),
                (ub_raw[:], up_b.rearrange("e (m p) -> (e m) p", p=P)),
            ):
                act.dma_start(dst, src).then_inc(ld_row, 16)
            act.wait_ge(ub_mm, 1)
            nc.scalar.copy(ubias[:], ps[7][:, 0:E * MK])
            act.wait_ge(wo_ga, 1)
            for k in range(CK):
                nc.scalar.activation(wtmp[:, k], wtmp[:, k], ACT.Identity, bias=zero_c[:], scale=lng_col[:, k:k + 1]
                                     ).then_inc(wo_hi, 1)
            act.wait_ge(wo_hi, CK)
            nc.scalar.copy(wo[:, 0], wtmp[:]).then_inc(wo_hi, 1)

        @block.tensor
        def _(pe):
            pe.wait_ge(c_spread, 1)
            pe.wait_ge(ld_mod, 16)
            for n in range(3):
                for k in range(CK):
                    mm = nc.tensor.matmul(ps[n][:], c_rows[:, k], mw[:, k, n * HALF:(n + 1) * HALF],
                                          start=(k == 0), stop=(k == CK - 1))
                mm.then_inc(mod_mm, 1)
            pe.wait_ge(ld_w, 16 * N_W)
            pe.wait_ge(consts, 1)
            for i in range(6):
                if i >= 3:
                    pe.wait_ge(wt_ok, i - 2)
                for k in range(CK):
                    for o in range(CK):
                        mm = nc.tensor.transpose(ps[3 + i % 3][:, k * C + o * P:k * C + (o + 1) * P],
                                                 wnat[:, i, o, k * P:(k + 1) * P], ident[:])
                mm.then_inc(wt_mm, 1)
            pe.wait_ge(wt_ok, 6)
            for k in range(CK):
                mm = nc.tensor.matmul(ps[6][:, 0:C], lnb_rows[:, k], wtmp[:, k], start=(k == 0), stop=(k == CK - 1))
            mm.then_inc(bo_mm, 1)
            pe.wait_ge(ld_row, 16 * N_ROW)
            nc.tensor.transpose(ps[7][:, 0:E * MK], ub_raw[:], ident[0:E * MK, 0:E * MK]).then_inc(ub_mm, 1)

        @block.vector
        def _(dve):
            step = [0]

            def link(ins):
                step[0] += 1
                ins.then_inc(dve0, 1)
                dve.wait_ge(dve0, step[0])

            dve.wait_ge(c_silu, 1)
            nc.vector.tensor_copy(c_rows[:], c_act[:].unsqueeze(2).broadcast_to([P, CK, P])).then_inc(c_spread, 1)
            def statistics(i):
                for q in range(XD):
                    dve.wait_ge(x_in[q], 16 * i + 16)
                    for t in range(TG):
                        n = TG * (XD * i + q) + t
                        nc.vector.bn_stats(bn0[:, n], X[:, n]).then_inc(x_stat, 1)

            statistics(0)
            dve.wait_ge(mod_mm, 3)
            for n in range(3):
                link(nc.vector.tensor_copy(mod[:, 2 * n:2 * n + 2].rearrange("p a c -> p (a c)"), ps[n][:]))
            nc.vector.tensor_copy(shift_a[:], mod[:, 0])
            nc.vector.tensor_scalar(scale_a[:], mod[:, 1], 1.0, None, ALU.add)
            nc.vector.tensor_copy(shift_b[:], mod[:, 3])
            nc.vector.tensor_scalar(scale_b[:], mod[:, 4], 1.0, None, ALU.add)
            for i, (m, dst) in enumerate(((2, gate_a), (5, gate_fb))):
                link(nc.vector.tensor_scalar(ga_sgn[:, i], mod[:, m], 0.0, 2.0, ALU.is_ge, ALU.mult))
                link(nc.vector.scalar_tensor_tensor(ga_abs[:, i], mod[:, m], -1.0, mod[:, m], ALU.mult, ALU.max))
                link(nc.vector.tensor_scalar(ga_abs[:, i], ga_abs[:, i], 0.25, None, ALU.max))
                link(nc.vector.scalar_tensor_tensor(dst[:], ga_sgn[:, i], -1.0, ga_abs[:, i], ALU.add, ALU.mult))
            statistics(1)
            dve.wait_ge(ld_row, 16 * N_ROW)
            dve.wait_ge(consts, 1)
            flat = lambda t: t.rearrange("p k n -> p (k n)")
            for i in range(5):
                dve.wait_ge(wt_mm, i + 1)
                t2 = ps[3 + i % 3][:].rearrange("p (k n) -> p k n", k=CK)
                if i < 3:
                    col = (KV * C if i == 0 else (i - 1) * C)
                    nc.vector.tensor_tensor(wtmp[:], t2, eye2[:], ALU.add).then_inc(wt_ok, 1)
                    dve.wait_ge(wt_ok, i + 1)
                    link(nc.vector.tensor_copy(wkq[:, 0, :, col:col + C], wtmp[:]))
                    link(nc.vector.tensor_tensor(wkq[:, 1, :, col:col + C], wtmp[:],
                                                 f32(wkq[:, 0, :, col:col + C]), ALU.subtract))
                else:
                    nc.vector.tensor_tensor(wv[:, :, (i - 3) * C:(i - 2) * C], t2, eye2[:], ALU.add).then_inc(wt_ok, 1)
            dve.wait_ge(wt_mm, 6)
            link(nc.vector.tensor_copy(lnb_rows[:], lnb_col[:].unsqueeze(2).broadcast_to([P, CK, P])))
            nc.vector.tensor_copy(flat(wtmp[:]), ps[5][:]).then_inc(wt_ok, 1)
            dve.wait_ge(bo_mm, 1)
            link(nc.vector.tensor_tensor(bo_row[:], ps[6][:, 0:C], bo_row[:], ALU.add))
            link(nc.vector.tensor_tensor(bo_row[:], bo_row[:], gate_a[:], ALU.mult))
            dve.wait_ge(x_stat, NT)
            for t in range(NT):
                last = nc.vector.bn_aggr(mv1[:, t], bn0[:, t])
            link(last)
            link(nc.vector.tensor_scalar(rs1[:, 1], mv1[:, :, 1], EPS_LN, None, ALU.add))
            rsqrt(link, rs1[:, 2], rs1[:, 1], rs1[:, 0])

    b1 = Map(nc, p1w.at)
    z1 = b1("z1", [P, TG, C], F32)
    h1 = b1("h1", [P, 2, TG, C + 1], F32)
    hT = b1("hT", [P, 2, 2, CK, HALF], F32R)
    kraw = b1("kraw", [P, 2, KV * C], F32)
    ks = b1("ks", [P, TG, KV * C], F32)
    ksq = b1("ksq", [P, 2, KV * C], F32)
    kn = b1("kn", [P, TG, KV * C], F32)
    kss = b1("kss", [P, TG, KV * HEADS], F32)
    krs = b1("krs", [P, TG, KV * HEADS], F32)
    kinv = b1("kinv", [P, TG, KV * HEADS], F32)
    ktmp = b1("ktmp", [P, TG, KV * HEADS], F32)
    zero_w = b1("zero_w", [P, C + 1], F32)
    assert b1.at <= SRAW and st.at <= SRAW

    names = ("z1_ok", "h1_ok", "tp1", "hi1", "lo1", "k_mm", "k_ev", "k_silu", "k_sq", "k_red",
             "k_inv", "k_n", "g_mm", "q_mm", "q_silu", "h1_one", "sw_hi", "sw_lo")
    (z1_ok, h1_ok, tp1, hi1, lo1, k_mm, k_ev, k_silu, k_sq, k_red, k_inv, k_n, g_mm, q_mm, q_silu,
     h1_one, sw_hi, sw_lo) = [sem(n) for n in names]
    later = lambda g, n: not isinstance(g, int) or g >= n

    def groups(eng, body):
        body(0, 0, True)
        body(1, 1, True)
        with eng.Fori(1, NG // 2 - 1) as i:
            body(2 * i, 0, True)
            body(2 * i + 1, 1, True)
        body(NG - 2, 0, True)
        body(NG - 1, 1, False)

    with ExitStack() as mem:
        psG = mem.enter_context(nc.psum_tensor("psG", [P, 4, HALF], F32))
        with ExitStack() as mem1, nc.Block() as block:
            psK = mem1.enter_context(nc.psum_tensor("psK", [P, HALF], F32))
            psQ = mem1.enter_context(nc.psum_tensor("psQ", [P, HALF], F32))
            psT = mem1.enter_context(nc.psum_tensor("psT", [P, 2, HALF], F32))

            @block.vector
            def _(dve):
                def normalise(g, q, t):
                    if later(g, 1):
                        dve.wait_ge(h1_ok, TG * (g - 1) + t + 1)
                    n = TG * g + t
                    nc.vector.scalar_tensor_tensor(z1[:, t], X[:, bass.ds(n, 1), :].rearrange("p a c -> p (a c)"),
                                                   mv1[:, bass.ds(n, 1), 0], scale_a[:],
                                                   ALU.subtract, ALU.mult).then_inc(z1_ok, 1)

                def modulate(g, q, t):
                    wait(dve, z1_ok, TG * g + t + 1)
                    if later(g, 2):
                        wait(dve, g_mm, TG * (g - 2) + t + 1)
                    nc.vector.scalar_tensor_tensor(h1[:, q, t, 0:C], z1[:, t], rs1[:, 2, bass.ds(TG * g + t, 1)],
                                                   shift_a[:], ALU.mult, ALU.add).then_inc(h1_ok, 1)

                def low(g, q, k):
                    dve.wait_ge(hi1, 2 * g + k + 1)
                    nc.vector.tensor_tensor(hT[:, q, 1, k], psT[:, k], f32(hT[:, q, 0, k]), ALU.subtract
                                            ).then_inc(lo1, 1)

                def unit(f, t):
                    if later(f, 1):
                        dve.wait_ge(g_mm, TG * (f - 1) + t + 1)
                    nc.vector.scalar_tensor_tensor(
                        kn[:, t].rearrange("p (h d) -> p h d", d=D),
                        ks[:, t].rearrange("p (h d) -> p h d", d=D), 0.5,
                        kinv[:, t].unsqueeze(2).broadcast_to([P, KV * HEADS, D]), ALU.add, ALU.mult
                    ).then_inc(k_n, 1)

                nc.vector.memset(h1[:, :, :, C:C + 1], 1.0).then_inc(h1_one, 1)
                nc.vector.memset(zero_w[:], 0.0).then_inc(h1_one, 1)
                for t in range(TG):
                    normalise(0, 0, t)
                for t in range(TG):
                    modulate(0, 0, t)
                low(0, 0, 0)
                low(0, 0, 1)

                def body(g, q, more):
                    prev = later(g, 1)

                    def evac(t):
                        dve.wait_ge(k_mm, TG * g + t + 1)
                        if prev or t >= 2:
                            dve.wait_ge(k_silu, TG * g + t - 1)
                        nc.vector.tensor_tensor(kraw[:, t % 2], psK[:], bk_row[:], ALU.add).then_inc(k_ev, 1)

                    def reduce(t):
                        dve.wait_ge(k_sq, TG * g + t + 1)
                        nc.vector.tensor_reduce(kss[:, t], ksq[:, t % 2].rearrange("p (h d) -> p h d", d=D),
                                                AX.X, ALU.add).then_inc(k_red, 1)

                    n = [0]
                    STEPS = RSQRT + 3

                    def link(ins):
                        n[0] += 1
                        ins.then_inc(k_inv, 1)
                        dve.wait_ge(k_inv, STEPS * g + n[0])

                    def between(n):
                        if more and n >= 1:
                            low(g + 1, 1 - q, n - 1)

                    flat = lambda t: t[:].rearrange("p t h -> p (t h)")
                    evac(0)
                    if prev:
                        unit(g - 1, 0)
                        unit(g - 1, 1)
                    evac(1)
                    if prev:
                        unit(g - 1, 2)
                        unit(g - 1, 3)
                    reduce(0)
                    if more:
                        normalise(g + 1, 1 - q, 0)
                    evac(2)
                    reduce(1)
                    if more:
                        normalise(g + 1, 1 - q, 1)
                        modulate(g + 1, 1 - q, 0)
                        normalise(g + 1, 1 - q, 2)
                    evac(3)
                    if more:
                        modulate(g + 1, 1 - q, 1)
                        normalise(g + 1, 1 - q, 3)
                        modulate(g + 1, 1 - q, 2)
                    reduce(2)
                    if more:
                        modulate(g + 1, 1 - q, 3)
                    reduce(3)
                    dve.wait_ge(k_red, TG * g + TG)
                    rsqrt(link, flat(krs), flat(kss), flat(ktmp), between)
                    link(nc.vector.tensor_scalar(flat(kss), flat(krs), EPS, 1.0, ALU.mult, ALU.add))
                    link(nc.vector.reciprocal(flat(ktmp), flat(kss)))
                    link(nc.vector.tensor_tensor(flat(kinv), flat(krs), flat(ktmp), ALU.mult))
                    assert n[0] == STEPS

                groups(dve, body)
                for t in range(TG):
                    unit(NG - 1, t)

            @block.gpsimd
            def _(pool):
                def split(n):
                    a, k = n // 2, n % 2
                    src = sraw[:, a, k]
                    w = (su[:, :, k], sd[:, :, k * MK // 2:(k + 1) * MK // 2].rearrange("p b m n -> p b (m n)"))[a]
                    if n == 0:
                        pool.wait_ge(ld_sh, 32)
                    nc.gpsimd.tensor_copy(w[:, 0], src).then_inc(sw_hi, 1)
                    pool.wait_ge(sw_hi, n + 1)
                    nc.gpsimd.tensor_tensor(w[:, 1], src, f32(w[:, 0]), ALU.subtract).then_inc(sw_lo, 1)

                for n in range(4):
                    split(n)

            @block.scalar
            def _(act):
                def high(g, q, k):
                    act.wait_ge(tp1, 2 * g + k + 1)
                    nc.scalar.copy(hT[:, q, 0, k], psT[:, k]).then_inc(hi1, 1)

                high(0, 0, 0)
                high(0, 0, 1)

                def body(g, q, more):
                    def key(t):
                        act.wait_ge(k_ev, TG * g + t + 1)
                        if later(g, 1):
                            act.wait_ge(k_n, TG * (g - 1) + t + 1)
                        nc.scalar.activation(ks[:, t], kraw[:, t % 2], ACT.Silu).then_inc(k_silu, 1)
                        act.wait_ge(k_silu, TG * g + t + 1)
                        if later(g, 1) or t >= 2:
                            act.wait_ge(k_red, TG * g + t - 1)
                        nc.scalar.activation(ksq[:, t % 2], ks[:, t], ACT.Square, bias=expo[:, 0, 0:1]).then_inc(k_sq, 1)

                    def query(k):
                        act.wait_ge(q_mm, CK * g + k + 1)
                        nc.scalar.activation(qT[:, k, bass.ds(HALF * g, HALF)], psQ[:], ACT.Silu,
                                             bias=bq_col[:, k:k + 1]).then_inc(q_silu, 1)

                    for t in range(TG):
                        key(t)
                    query(0)
                    if more:
                        high(g + 1, 1 - q, 0)
                        high(g + 1, 1 - q, 1)
                    query(1)

                groups(act, body)

            @block.tensor
            def _(pe):
                pe.wait_ge(h1_one, 2)

                def turn(g, q, k):
                    if k == 0:
                        pe.wait_ge(h1_ok, TG * g + TG)
                    for t in range(TG):
                        mm = nc.tensor.transpose(psT[:, k, t * P:(t + 1) * P], h1[:, q, t, k * P:(k + 1) * P], ident[:])
                    mm.then_inc(tp1, 1)

                def keys(g, q, t):
                    if t == 0:
                        pe.wait_ge(lo1, 2 * g + 2)
                    if later(g, 1) or t:
                        pe.wait_ge(k_ev, TG * g + t)
                    n = 0
                    for k in range(CK):
                        for a, b in ((0, 0), (0, 1), (1, 0)):
                            mm = nc.tensor.matmul(psK[:], hT[:, q, a, k, t * P:(t + 1) * P],
                                                  wkq[:, b, k, 0:KV * C], start=(n == 0), stop=(n == 3 * CK - 1))
                            n += 1
                    mm.then_inc(k_mm, 1)

                def queries(g, q, o):
                    if later(g, 1) or o:
                        pe.wait_ge(q_silu, CK * g + o)
                    n = 0
                    for k in range(CK):
                        for a, b in ((0, 0), (0, 1), (1, 0)):
                            col = KV * C + o * P
                            mm = nc.tensor.matmul(psQ[:], wkq[:, b, k, col:col + P], hT[:, q, a, k],
                                                  start=(n == 0), stop=(n == 3 * CK - 1))
                            n += 1
                    mm.then_inc(q_mm, 1)

                def sums(f, r, t):
                    pe.wait_ge(k_n, TG * f + t + 1)
                    for j in range(4):
                        mm = nc.tensor.matmul(psG[:, j, 0:C + 1], kn[:, t, j * P:(j + 1) * P], h1[:, r, t],
                                              start=False, stop=False, skip_group_check=True)
                    mm.then_inc(g_mm, 1)

                for j in range(4):
                    nc.tensor.matmul(psG[:, j, 0:C + 1], zero_w[:, 0:P], zero_w[:],
                                     start=True, stop=False, skip_group_check=True)
                turn(0, 0, 0)
                turn(0, 0, 1)

                def body(g, q, more):
                    keys(g, q, 0)
                    for t in range(TG):
                        if t < TG - 1:
                            keys(g, q, t + 1)
                        if later(g, 1):
                            sums(g - 1, 1 - q, t)
                    queries(g, q, 0)
                    if more:
                        turn(g + 1, 1 - q, 0)
                        turn(g + 1, 1 - q, 1)
                    queries(g, q, 1)

                groups(pe, body)
                for t in range(TG):
                    sums(NG - 1, 1, t)

        s1 = Map(nc, p1w.at)
        Gs = s1("Gs", [P, 4, C + 1], F32)
        GT = s1("GT", [P, 4, CK, P], F32)
        sts = s1("sts", [P, 4, P], F32)
        g_cp, g_tp, g_tc, s_mm, s_dve = [sem(n) for n in ("g_cp", "g_tp", "g_tc", "s_mm", "s_dve")]
        with ExitStack() as mem1, nc.Block() as block:
            psA = mem1.enter_context(nc.psum_tensor("psA", [P, 2, HALF], F32))
            psS = mem1.enter_context(nc.psum_tensor("psS", [P, HALF], F32))

            @block.vector
            def _(dve):
                for j in range(4):
                    nc.vector.tensor_copy(Gs[:, j], psG[:, j, 0:C + 1]).then_inc(g_cp, 1)
                for b in range(2):
                    dve.wait_ge(g_tp, b + 1)
                    nc.vector.tensor_copy(GT[:, 2 * b:2 * b + 2].rearrange("p j k n -> p (j k n)"), psA[:, b]
                                          ).then_inc(g_tc, 1)
                dve.wait_ge(s_mm, 1)
                dve.wait_ge(g_cp, 4)
                for j in range(4):
                    kv, hf = j // 2, j % 2
                    nc.vector.scalar_tensor_tensor(sts[:, j], bv_row[:, kv * C + hf * P:kv * C + hf * P + P],
                                                   Gs[:, j, C:C + 1], psS[:, j * P:(j + 1) * P],
                                                   ALU.mult, ALU.add).then_inc(s_dve, 1)
                dve.wait_ge(s_dve, 4)
                for hf in range(CK):
                    nc.vector.scalar_tensor_tensor(sts[:, hf], sts[:, hf], float(N) ** -KV, sts[:, 2 + hf],
                                                   ALU.mult, ALU.mult).then_inc(s_dve, 1)
                dve.wait_ge(s_dve, 6)
                for hf in range(CK):
                    nc.vector.tensor_tensor(state[:, hf], sts[:, hf], blocks[:], ALU.mult)

            @block.tensor
            def _(pe):
                for j in range(4):
                    pe.wait_ge(g_cp, j + 1)
                    for k in range(CK):
                        at = (j % 2) * C + k * P
                        mm = nc.tensor.transpose(psA[:, j // 2, at:at + P], Gs[:, j, k * P:(k + 1) * P], ident[:])
                    if j % 2:
                        mm.then_inc(g_tp, 1)
                pe.wait_ge(g_tc, 2)
                for j in range(4):
                    kv, hf = j // 2, j % 2
                    for k in range(CK):
                        at = kv * C + hf * P
                        mm = nc.tensor.matmul(psS[:, j * P:(j + 1) * P], GT[:, j, k], wv[:, k, at:at + P],
                                              start=(k == 0), stop=(k == CK - 1))
                mm.then_inc(s_mm, 1)

    b2 = Map(nc, after_q)
    q5 = b2("q5", [P, CK, HALF], F32)
    qsq = b2("qsq", [P, CK, HALF], F32)
    nq = b2("nq", [P, 4, TG * HEADS], F32)
    oz = b2("oz", [P, TG, C], F32)
    bn2 = b2("bn2", [P, 2, TG, 6], F32)
    mv2 = b2("mv2", [P, 2, TG, 2], F32)
    rs2 = b2("rs2", [P, 2, 2, TG], F32)
    zT = b2("zT", [P, 2, CK, HALF], F32R)
    z2 = b2("z2", [P, TG, C], F32)
    lgT = z2[0:E, 0:HALF // C].rearrange("e a c -> e (a c)")
    h2 = b2("h2", [P, 2, TG, ROW], F32)
    h2T = b2("h2T", [P, 2, 2, CK, HALF], F32R)
    gf = b2("gf", [P, 2, HALF], F32)
    ghi = b2("ghi", [P, 3, HALF], F32R)
    glo = b2("glo", [P, 3, HALF], F32R)
    sh = b2("sh", [P, TG, C], F32)
    lg = b2("lg", [P, TG, E], F32)
    sc = b2("sc", [P, TG, E], F32)
    mx = b2("mx", [P, TG, E], F32)
    ix = b2("ix", [P, TG, E], U32)
    ixf = b2("ixf", [P, TG, TOPK], F32)
    oh = b2("oh", [P, TOPK, TG, E], F32)
    ohb = b2("ohb", [P, TG, E], BF16)
    rk = b2("rk", [P, TG, E], F32)
    rk2 = b2("rk2", [P, TG, E], F32)
    pf = b2("pf", [P, TG, TOPK], F32)
    post = b2("post", [P, 2, TG, TOPK], U32)
    dn = b2("dn", [P, 2, TG], F32)
    wt = b2("wt", [P, TG, TOPK], F32)
    wd = b2("wd", [P, 2, TG, E], F32)

    io_t = b2("io_t", [P, ETL], F32)
    io_k = b2("io_k", [P, E, NT // 2], F32)
    ntl = b2("ntl", [P, E], F32)
    used = b2("used", [P, E], F32)
    upto = b2("upto", [P, E, E], F32)
    tsel = b2("tsel", [P, E, E], F32)
    tend = b2("tend", [P, E], F32)
    tbeg = b2("tbeg", [P, E], F32)
    nxt = b2("nxt", [P, E], F32)
    jump = b2("jump", [P, E], F32)
    gecm = b2("gecm", [P, ETL, E], F32)
    gej = b2("gej", [P, ETL, E], F32)
    tcmp = gej[:].rearrange("p j e -> p (j e)")[:, 0:E * NT // 2].rearrange("p (e t) -> p e t", e=E)
    tabf = b2("tabf", [P, 4, ETL], F32)
    pari = b2("pari", [P, ETL], I32)
    padf = b2("padf", [P, E], F32)
    padt = b2("padt", [P, E], I32)
    prow = b2("prow", [P, ROW], F32)
    raw = Map(nc, SRAW)
    raw_up = raw("raw_up", [P, CK, INNER], F32)
    raw_dn = raw("raw_dn", [P, MK, C], F32)
    W = CK * INNER
    slot0, slot1 = Map(nc, q_at), Map(nc, phase)
    wup = [m(f"wup{i}", [P, 2, CK, INNER], F32R) for i, m in enumerate((slot0, slot1))]
    wdn = [m(f"wdn{i}", [P, 2, MK, C], F32R) for i, m in enumerate((slot0, slot1))]
    assert b2.at <= SRAW, (b2.at, SRAW)
    tb_c, tb_d, tb_pool, tab_ok, pad_st, db_in, end_st, up_in, dn_in, w_hi, w_ok = [sem(n) for n in (
        "tb_c", "tb_d", "tb_pool", "tab_ok", "pad_st", "db_in", "end_st", "up_in", "dn_in", "w_hi", "w_ok")]

    def entry(eng, table, j, most):
        return eng.value_load(table[0:1, bass.ds(j, 1)], min_val=0, max_val=most)

    up_v = up_w.rearrange("e (k p) n -> e p k n", p=P)
    down_v = down_w.rearrange("e (k p) n -> e p k n", p=P)
    def weights(sp, e):
        sp.dma_start(raw_up[:], up_v[bass.ds(e, 1)].rearrange("a p k n -> p (a k) n")).then_inc(up_in, 16)
        sp.dma_start(raw_dn[:], down_v[bass.ds(e, 1)].rearrange("a p k n -> p (a k) n")).then_inc(dn_in, 16)

    def split_hi(act, n, s):
        for i in range(2):
            wait(act, (up_in, dn_in)[i], 16 * n + 16)
            src = (raw_up, raw_dn)[i][:].rearrange("p k n -> p (k n)")
            dst = (wup, wdn)[i][s][:, 0].rearrange("p k n -> p (k n)")
            for h in range(2):
                at = slice(h * W // 2, (h + 1) * W // 2)
                nc.scalar.copy(dst[:, at], src[:, at]).then_inc(w_hi, 1)

    def split_lo(dve, n, s):
        for i in range(2):
            src = (raw_up, raw_dn)[i][:].rearrange("p k n -> p (k n)")
            hi, lo = [(wup, wdn)[i][s][:, a].rearrange("p k n -> p (k n)") for a in range(2)]
            for h in range(2):
                at = slice(h * W // 2, (h + 1) * W // 2)
                dve.wait_ge(w_hi, 4 * n + 2 * i + h + 1)
                ins = nc.vector.tensor_tensor(lo[:, at], src[:, at], f32(hi[:, at]), ALU.subtract)
            ins.then_inc(w_ok, 1)

    names = ("q_pre", "nm_mm", "nm_ev", "rq_ok", "o_mm", "o_ev", "stat2", "self2", "rse2",
             "rstd2", "zo_ok", "tz_mm", "tz_hi", "tz_lo", "xb_ok", "a_mm", "x_ev", "z2_ok", "h2_set", "h2_ok",
             "th_mm", "th_hi", "th_lo", "gt_row", "gt_cp", "gt_mm", "gt_ev", "gt_sc", "rt_dve", "rt_oh", "rt_mm", "pos_ok",
             "scat", "u_mm", "u_g", "u_hi", "u_lo", "d_mm", "sh_ev", "sh_st")
    (q_pre, nm_mm, nm_ev, rq_ok, o_mm, o_ev, stat2, self2, rse2, rstd2, zo_ok, tz_mm, tz_hi,
     tz_lo, xb_ok, a_mm, x_ev, z2_ok, h2_set, h2_ok, th_mm, th_hi, th_lo, gt_row, gt_cp, gt_mm, gt_ev, gt_sc, rt_dve, rt_oh,
     rt_mm, pos_ok, scat, u_mm, u_g, u_hi, u_lo, d_mm, sh_ev, sh_st) = [sem(n) for n in names]

    def staggered(eng, body):
        body(0, 0, True, False)
        body(1, 1, True, True)
        body(2, 0, True, True)
        with eng.Fori(1, NG // 2 - 1) as i:
            body(2 * i + 1, 1, True, True)
            body(2 * i + 2, 0, True, True)
        body(NG - 1, 1, True, True)
        body(NG, 0, False, True)

    PASSES = ((0, 0), (0, 1), (1, 0))

    with ExitStack() as mem, nc.Block() as block:
        psU = mem.enter_context(nc.psum_tensor("psU", [P, 2, HALF], F32))
        psY = mem.enter_context(nc.psum_tensor("psY", [P, 2, HALF], F32))
        psZ = mem.enter_context(nc.psum_tensor("psZ", [P, 2, HALF], F32))
        psO = mem.enter_context(nc.psum_tensor("psO", [P, HALF], F32))
        psM = mem.enter_context(nc.psum_tensor("psM", [P, HALF], F32))
        NORM, GATE, RANK, TOTAL = 0, 64, 96, 128

        @block.tensor
        def _(pe):
            def body(g, q, att_on, ffn_on):
                f, r = g - 1, 1 - q

                def norms():
                    pe.wait_ge(q_pre, 2 * g + 2)
                    if later(g, 2):
                        pe.wait_ge(rt_dve, 20 * g - 20)
                    for t in range(TG):
                        for k in range(CK):
                            at = NORM + t * HEADS + k * (P // D)
                            mm = nc.tensor.matmul(psM[:, at:at + P // D], qsq[:, k, t * P:(t + 1) * P], heads[:],
                                                  start=True, stop=True)
                    mm.then_inc(nm_mm, 1)

                def outs(h):
                    if later(g, 1) or h:
                        pe.wait_ge(o_ev, 2 * g + 1) if h else pe.wait_ge(x_ev, 2 * g)
                    for t in (2 * h, 2 * h + 1):
                        for k in range(CK):
                            at = (t % 2) * C + k * P
                            mm = nc.tensor.matmul(psO[:, at:at + P], q5[:, k, t * P:(t + 1) * P], state[:, k],
                                                  start=True, stop=True)
                    mm.then_inc(o_mm, 1)

                def turn_z(k):
                    pe.wait_ge(zo_ok, TG * g + TG)
                    if later(g, 1):
                        pe.wait_ge(th_lo, 2 * g - 1 + k)
                    for t in range(TG):
                        mm = nc.tensor.transpose(psZ[:, k, t * P:(t + 1) * P], oz[:, t, k * P:(k + 1) * P], ident[:])
                    mm.then_inc(tz_mm, 1)

                def attend(h):
                    pe.wait_ge(x_ev, 2 * g + 1) if h else pe.wait_ge(o_ev, 2 * g + 2)
                    if not h:
                        pe.wait_ge(tz_lo, 2 * g + 2)
                    for t in (2 * h, 2 * h + 1):
                        n = 0
                        for k in range(CK):
                            for a, b in PASSES:
                                mm = nc.tensor.matmul(psO[:, (t % 2) * C:(t % 2 + 1) * C],
                                                      zT[:, a, k, t * P:(t + 1) * P], wo[:, b, k],
                                                      start=(n == 0), stop=(n == 5))
                                n += 1
                    mm.then_inc(a_mm, 1)

                def turn_h(k):
                    pe.wait_ge(h2_ok, TG * g + TG)
                    pe.wait_ge(tz_lo, 2 * g + 1 + k)
                    for t in range(TG):
                        mm = nc.tensor.transpose(psZ[:, k, t * P:(t + 1) * P], h2[:, q, t, k * P:(k + 1) * P], ident[:])
                    mm.then_inc(th_mm, 1)

                def gate():
                    pe.wait_ge(th_lo, 2 * f + 2)
                    if later(f, 1):
                        pe.wait_ge(u_g, MK * f)
                    n = 0
                    for k in range(CK):
                        for a, b in PASSES:
                            mm = nc.tensor.matmul(psU[0:E, 1], gw[:, b, k], h2T[:, r, a, k],
                                                  start=(n == 0), stop=(n == 5))
                            n += 1
                    mm.then_inc(gt_row, 1)

                def turn_gate():
                    wait(pe, gt_cp, f + 1)
                    if att_on:
                        wait(pe, nm_ev, g + 1)
                    for t in range(TG):
                        mm = nc.tensor.transpose(psM[:, GATE + t * E:GATE + (t + 1) * E],
                                                 lgT[:, t * P:(t + 1) * P], ident[0:E, 0:E])
                    mm.then_inc(gt_mm, 1)

                def rank():
                    pe.wait_ge(rt_oh, f + 1)
                    nc.tensor.matmul(psM[:, RANK:RANK + TG * E], tri[:], ohb[:].rearrange("p t e -> p (t e)"),
                                     start=True, stop=False, skip_group_check=True)
                    for t in range(TG - 1):
                        n = TG - 1 - t
                        nc.tensor.matmul(psM[:, RANK + (t + 1) * E:RANK + TG * E].rearrange("p (t e) -> p t e", e=E),
                                         one_b[:], ohb[:, t:t + 1].broadcast_to([P, n, E]), start=False,
                                         stop=(t == TG - 2), skip_group_check=True)
                    for t in range(TG):
                        mm = nc.tensor.matmul(psM[:, TOTAL:TOTAL + E], one_b[:], ohb[:, t], start=(t == 0),
                                              stop=(t == TG - 1))
                    mm.then_inc(rt_mm, 1)

                def up(m):
                    if later(f, 1) or m >= 2:
                        pe.wait_ge(u_g, MK * f + m - 1)
                    if m == 0:
                        pe.wait_ge(th_lo, 2 * f + 2)
                    n = 0
                    for k in range(CK):
                        for a, b in PASSES:
                            mm = nc.tensor.matmul(psU[:, m % 2], su[:, b, k, m * P:(m + 1) * P], h2T[:, r, a, k],
                                                  start=(n == 0), stop=(n == 5))
                            n += 1
                    mm.then_inc(u_mm, 1)

                def down(m):
                    pe.wait_ge(u_lo, MK * f + m + 1)
                    if m == 0 and later(f, 1):
                        pe.wait_ge(sh_ev, 2 * f)
                    for t in range(TG):
                        for n, (a, b) in enumerate(PASSES):
                            lhs = (ghi, glo)[a][:, m % 3, t * P:(t + 1) * P]
                            mm = nc.tensor.matmul(psY[:, t // 2, (t % 2) * C:(t % 2 + 1) * C], lhs, sd[:, b, m],
                                                  start=(m == 0 and t % 2 == 0 and n == 0),
                                                  stop=(m == MK - 1 and n == 2), skip_group_check=True)
                    mm.then_inc(d_mm, 1)

                def chunk(m):
                    if ffn_on:
                        if m < MK:
                            up(m)
                        if m >= 2:
                            down(m - 2)

                if att_on:
                    norms()
                if ffn_on:
                    gate()
                chunk(0)
                if att_on:
                    outs(0)
                if ffn_on:
                    turn_gate()
                chunk(1)
                if att_on:
                    outs(1)
                chunk(2)
                chunk(3)
                if ffn_on:
                    up(4)
                if att_on:
                    turn_z(0)
                    turn_z(1)
                if ffn_on:
                    down(2)
                if not att_on:
                    rank()
                if att_on:
                    attend(0)
                chunk(5)
                if att_on:
                    attend(1)
                if ffn_on and att_on:
                    rank()
                for m in range(6, MK + 2):
                    chunk(m)
                if att_on:
                    turn_h(0)
                    turn_h(1)

            staggered(pe, body)

        @block.scalar
        def _(act):
            def body(g, q, att_on, ffn_on):
                f, r = g - 1, 1 - q

                def queries():
                    if later(g, 1):
                        act.wait_ge(o_mm, 2 * g)
                    src = qT[:, :, bass.ds(HALF * g, HALF)]
                    nc.scalar.activation(q5[:], src, ACT.Identity, bias=expo[:, 0, 0:1]).then_inc(q_pre, 1)
                    nc.scalar.activation(qsq[:], src, ACT.Square, bias=expo[:, 0, 0:1]).then_inc(q_pre, 1)

                def high(mm, out, dst, k):
                    act.wait_ge(mm, 2 * g + k + 1)
                    nc.scalar.copy(dst[:, 0, k], psZ[:, k]).then_inc(out, 1)

                def gelu(m):
                    act.wait_ge(u_mm, MK * f + m + 1)
                    if later(f, 1) or m >= 2:
                        act.wait_ge(u_lo, MK * f + m - 1)
                    nc.scalar.activation(gf[:, m % 2], psU[:, m % 2], ACT.Gelu, bias=sbu[:, m:m + 1]).then_inc(u_g, 1)
                    act.wait_ge(u_g, MK * f + m + 1)
                    if later(f, 1) or m >= 3:
                        act.wait_ge(d_mm, MK * f + m - 2)
                    nc.scalar.copy(ghi[:, m % 3], gf[:, m % 2]).then_inc(u_hi, 1)

                def score():
                    act.wait_ge(gt_ev, f + 1)
                    nc.scalar.activation(sc[:], lg[:], ACT.Sigmoid).then_inc(gt_sc, 1)

                if att_on and isinstance(g, int) and g == 0:
                    queries()
                if ffn_on:
                    score()
                    for m in range(4):
                        gelu(m)
                if att_on:
                    high(tz_mm, tz_hi, zT, 0)
                    high(tz_mm, tz_hi, zT, 1)
                if ffn_on:
                    for m in range(4, MK):
                        gelu(m)
                if att_on:
                    if not (isinstance(g, int) and g == NG - 1):
                        g2 = g + 1
                        act.wait_ge(o_mm, 2 * g2)
                        src = qT[:, :, bass.ds(HALF * g2, HALF)]
                        nc.scalar.activation(q5[:], src, ACT.Identity, bias=expo[:, 0, 0:1]).then_inc(q_pre, 1)
                        nc.scalar.activation(qsq[:], src, ACT.Square, bias=expo[:, 0, 0:1]).then_inc(q_pre, 1)
                    high(th_mm, th_hi, h2T[:, q], 0)
                    high(th_mm, th_hi, h2T[:, q], 1)

            staggered(act, body)
            split_hi(act, 0, 0)
            act.wait_ge(sh_ev, 2 * NG)
            act.dma_start(shd_v[:, TG * (NG - 1):NT, :], sh[:]).then_inc(sh_st, 16)

        @block.vector
        def _(dve):
            def body(g, q, att_on, ffn_on):
                f, r = g - 1, 1 - q

                def tile(t):
                    return X[:, bass.ds(TG * g + t, 1), :].rearrange("p a c -> p (a c)")

                def norm_read():
                    dve.wait_ge(nm_mm, g + 1)
                    nc.vector.tensor_copy(nq[:, 0], psM[:, NORM:NORM + TG * HEADS]).then_inc(nm_ev, 1)

                def norm_inverse():
                    n = [0]
                    STEPS = RSQRT + 3

                    def link(ins):
                        n[0] += 1
                        ins.then_inc(rq_ok, 1)
                        dve.wait_ge(rq_ok, STEPS * g + n[0])

                    dve.wait_ge(nm_ev, g + 1)
                    rsqrt(link, nq[:, 2], nq[:, 0], nq[:, 3])
                    link(nc.vector.tensor_scalar(nq[:, 0], nq[:, 2], EPS, 1.0, ALU.mult, ALU.add))
                    link(nc.vector.reciprocal(nq[:, 3], nq[:, 0]))
                    link(nc.vector.tensor_tensor(nq[:, 1], nq[:, 2], nq[:, 3], ALU.mult))
                    assert n[0] == STEPS

                def out_read(h):
                    dve.wait_ge(o_mm, 2 * g + h + 1)
                    inv = nq[:, 1, 2 * h * HEADS:(2 * h + 2) * HEADS].unsqueeze(2).broadcast_to([P, 2 * HEADS, D])
                    nc.vector.tensor_tensor(oz[:, 2 * h:2 * h + 2].rearrange("p t (h d) -> p (t h) d", d=D),
                                            psO[:].rearrange("p (h d) -> p h d", d=D), inv, ALU.mult
                                            ).then_inc(o_ev, 1)
                    wait(dve, o_ev, 2 * g + h + 1)
                    for t in (2 * h, 2 * h + 1):
                        nc.vector.bn_stats(bn2[:, 0, t], oz[:, t]).then_inc(self2, 1)
                    for t in (2 * h, 2 * h + 1):
                        wait(dve, self2, 8 * g + t + 1)
                        nc.vector.bn_aggr(mv2[:, 0, t], bn2[:, 0, t]).then_inc(stat2, 1)

                def out_norm():
                    dve.wait_ge(rstd2, 2 * g + 1)
                    for t in range(TG):
                        nc.vector.tensor_scalar(oz[:, t], oz[:, t], mv2[:, 0, t, 0:1], rs2[:, 0, 1, t:t + 1],
                                                ALU.subtract, ALU.mult).then_inc(zo_ok, 1)

                def low_z(k):
                    dve.wait_ge(tz_hi, 2 * g + k + 1)
                    nc.vector.tensor_tensor(zT[:, 1, k], psZ[:, k], f32(zT[:, 0, k]), ALU.subtract).then_inc(tz_lo, 1)

                def x_read(h):
                    dve.wait_ge(a_mm, 2 * g + h + 1)
                    dve.wait_ge(xb_ok, g + 1)
                    pair = X[:, bass.ds(TG * g + 2 * h, 2), :].rearrange("p t c -> p (t c)")
                    nc.vector.tensor_tensor(pair, psO[:], pair, ALU.add).then_inc(x_ev, 1)
                    wait(dve, x_ev, 2 * g + h + 1)
                    for t in (2 * h, 2 * h + 1):
                        nc.vector.bn_stats(bn2[:, 1, t], tile(t)).then_inc(self2, 1)
                    for t in (2 * h, 2 * h + 1):
                        wait(dve, self2, 8 * g + TG + t + 1)
                        nc.vector.bn_aggr(mv2[:, 1, t], bn2[:, 1, t]).then_inc(stat2, 1)

                def x_mean():
                    if later(g, 1):
                        dve.wait_ge(h2_ok, TG * g)
                    for t in range(TG):
                        wait(dve, stat2, 8 * g + TG + t + 1)
                        nc.vector.scalar_tensor_tensor(z2[:, t], tile(t), mv2[:, 1, t, 0:1], scale_b[:],
                                                       ALU.subtract, ALU.mult).then_inc(z2_ok, 1)

                def x_norm():
                    dve.wait_ge(rstd2, 2 * g + 2)
                    if later(g, 2):
                        dve.wait_ge(th_mm, 2 * g - 2)
                        dve.wait_ge(scat, 16 * TG * TOPK * (g - 1))
                    for t in range(TG):
                        wait(dve, z2_ok, TG * g + t + 1)
                        nc.vector.scalar_tensor_tensor(h2[:, q, t, 0:C], z2[:, t], rs2[:, 1, 1, t:t + 1], shift_b[:],
                                                       ALU.mult, ALU.add).then_inc(h2_ok, 1)

                def low_h(k):
                    dve.wait_ge(th_hi, 2 * g + k + 1)
                    nc.vector.tensor_tensor(h2T[:, q, 1, k], psZ[:, k], f32(h2T[:, q, 0, k]), ALU.subtract
                                            ).then_inc(th_lo, 1)

                def low_g(m):
                    if ffn_on:
                        dve.wait_ge(u_hi, MK * f + m + 1)
                        nc.vector.tensor_tensor(glo[:, m % 3], gf[:, m % 2], f32(ghi[:, m % 3]), ALU.subtract
                                                ).then_inc(u_lo, 1)

                ROUTE = 20
                n = [0]

                def step(ins):
                    n[0] += 1
                    ins.then_inc(rt_dve, 1)
                    wait(dve, rt_dve, ROUTE * f + n[0])

                def gate_copy():
                    dve.wait_ge(gt_row, f + 1)
                    dve.wait_ge(h2_ok, TG * f + TG)
                    nc.vector.tensor_copy(lgT, psU[0:E, 1]).then_inc(gt_cp, 1)

                def gate_read():
                    dve.wait_ge(gt_mm, f + 1)
                    nc.vector.tensor_tensor(lg[:], psM[:, GATE:GATE + TG * E].rearrange("p (t e) -> p t e", e=E),
                                            gb_row[:].unsqueeze(1).broadcast_to([P, TG, E]), ALU.add
                                            ).then_inc(gt_ev, 1)

                def best():
                    wait(dve, gt_sc, f + 1)
                    for t in range(TG):
                        step(nc.vector.max(mx[:, t], sc[:, t]))
                    for t in range(TG):
                        step(nc.vector.max_index(ix[:, t], mx[:, t], sc[:, t]))

                def choose():
                    step(nc.vector.tensor_copy(ixf[:], ix[:, :, 0:TOPK]))
                    for k in range(TOPK):
                        step(nc.vector.tensor_tensor(oh[:, k], iota_e[:].unsqueeze(1).broadcast_to([P, TG, E]),
                                                     ixf[:, :, k:k + 1].broadcast_to([P, TG, E]), ALU.is_equal))
                    nc.vector.tensor_tensor(ohb[:], oh[:, 0], oh[:, 1], ALU.add).then_inc(rt_oh, 1)
                    step(nc.vector.tensor_tensor(dn[:, 0], mx[:, :, 0], mx[:, :, 1], ALU.add))
                    step(nc.vector.tensor_scalar(dn[:, 0], dn[:, 0], EPS, None, ALU.add))
                    step(nc.vector.reciprocal(dn[:, 1], dn[:, 0]))
                    step(nc.vector.scalar_tensor_tensor(wt[:], mx[:, :, 0:TOPK], 0.1,
                                                        dn[:, 1].unsqueeze(2).broadcast_to([P, TG, TOPK]),
                                                        ALU.mult, ALU.mult))
                    if isinstance(f, int) and f == 0:
                        dve.wait_ge(h2_set, 1)
                    for k in range(TOPK):
                        last = nc.vector.tensor_tensor(wd[:, k], oh[:, k], wt[:, :, k:k + 1].broadcast_to([P, TG, E]),
                                                       ALU.mult)
                    step(last)
                    nc.vector.tensor_tensor(h2[:, r, :, C + 1:C + 1 + E], wd[:, 0], wd[:, 1], ALU.add)
                    nc.vector.tensor_copy(h2[:, r, :, C:C + 1].bitcast(U32), idt[:, bass.ds(TG * f, TG)].unsqueeze(2))

                def place():
                    dve.wait_ge(rt_mm, f + 1)
                    step(nc.vector.tensor_tensor(rk[:], psM[:, RANK:RANK + TG * E].rearrange("p (t e) -> p t e", e=E),
                                                 run[:].unsqueeze(1).broadcast_to([P, TG, E]), ALU.add))
                    step(nc.vector.tensor_tensor(rk[:], rk[:], reg_e[:].unsqueeze(1).broadcast_to([P, TG, E]), ALU.add))
                    step(nc.vector.tensor_tensor(run[:], psM[:, TOTAL:TOTAL + E], run[:], ALU.add))
                    for k in range(TOPK):
                        nc.vector.tensor_tensor(rk2[:], rk[:], oh[:, k], ALU.mult).then_inc(pf_ok, 1)
                        dve.wait_ge(pf_ok, 2 * TOPK * f + 2 * k + 1)
                        nc.vector.tensor_reduce(pf[:, :, k], rk2[:], AX.X, ALU.add).then_inc(pf_ok, 1)
                        dve.wait_ge(pf_ok, 2 * TOPK * f + 2 * k + 2)
                    step(nc.vector.tensor_copy(post[:, r], pf[:]))
                    assert n[0] == ROUTE
                    nc.vector.sem_inc(pos_ok, 1)

                def shared_read():
                    dve.wait_ge(d_mm, MK * f + MK)
                    if later(f, 1):
                        dve.wait_ge(sh_st, 16 * f)
                    for h in range(2):
                        nc.vector.scalar_tensor_tensor(sh[:, 2 * h:2 * h + 2],
                                                       psY[:, h].rearrange("p (t c) -> p t c", c=C), 0.1,
                                                       sbd_row[:].unsqueeze(1).broadcast_to([P, 2, C]),
                                                       ALU.mult, ALU.add).then_inc(sh_ev, 1)

                tail = not att_on
                if att_on:
                    norm_read()
                    norm_inverse()
                if ffn_on:
                    gate_copy()
                if att_on:
                    out_read(0)
                if ffn_on:
                    gate_read()
                low_g(0)
                if att_on:
                    out_read(1)
                low_g(1)
                if ffn_on:
                    best()
                if att_on:
                    out_norm()
                low_g(2)
                if att_on:
                    low_z(0)
                    low_z(1)
                low_g(3)
                if ffn_on:
                    choose()
                if att_on:
                    x_read(0)
                low_g(4)
                if att_on:
                    x_read(1)
                    x_mean()
                if tail:
                    place()
                    dve.wait_ge(rt_dve, ROUTE * NG)
                    table_experts()
                low_g(5)
                low_g(6)
                if att_on:
                    x_norm()
                low_g(7)
                if ffn_on and not tail:
                    place()
                if tail:
                    table_slots()
                    table_rows()
                if ffn_on:
                    shared_read()
                if tail:
                    split_lo(dve, 0, 0)
                if att_on:
                    low_h(0)
                    low_h(1)

            tn = [0]

            def link(ins):
                tn[0] += 1
                ins.then_inc(tb_d, 1)
                dve.wait_ge(tb_d, tn[0])

            per_tile = lambda a: a.unsqueeze(1).broadcast_to([P, ETL, a.shape[-1]])

            def table_experts():
                dve.wait_ge(tb_c, 1)
                link(nc.vector.tensor_tensor(padf[:], run[:], reg_e[:], ALU.add))
                nc.vector.tensor_copy(padt[:], padf[:]).then_inc(tab_ok, 1)
                link(nc.vector.tensor_tensor(tcmp, run[:].unsqueeze(2).broadcast_to([P, E, NT // 2]), io_k[:], ALU.is_gt))
                link(nc.vector.tensor_reduce(ntl[:], tcmp, AX.X, ALU.add))
                link(nc.vector.tensor_tensor(tsel[:], upto[:], ntl[:].unsqueeze(1).broadcast_to([P, E, E]), ALU.mult))
                link(nc.vector.tensor_reduce(tend[:], tsel[:], AX.X, ALU.add))
                link(nc.vector.tensor_tensor(gecm[:], io_t[:].unsqueeze(2).broadcast_to([P, ETL, E]), per_tile(tend[:]),
                                             ALU.is_ge))
                last = gecm[:, :, 0:E - 1]
                link(nc.vector.tensor_reduce(tabf[:, 0], last, AX.X, ALU.add))
                nc.vector.tensor_copy(etab[:], tabf[:, 0]).then_inc(tab_ok, 1)

            def table_slots():
                link(nc.vector.tensor_scalar(used[:], run[:], 0.0, None, ALU.is_gt))
                link(nc.vector.tensor_tensor(tbeg[:], tend[:], ntl[:], ALU.subtract))
                link(nc.vector.tensor_tensor(tsel[:], tend[:].unsqueeze(2).broadcast_to([P, E, E]),
                                             tend[:].unsqueeze(1).broadcast_to([P, E, E]), ALU.is_ge))
                link(nc.vector.tensor_reduce(nxt[:], tsel[:], AX.X, ALU.add))
                link(nc.vector.scalar_tensor_tensor(nxt[:], nxt[:], float(E), nxt[:], ALU.is_lt, ALU.mult))
                link(nc.vector.tensor_tensor(nxt[:], nxt[:], used[:], ALU.mult))
                link(nc.vector.tensor_tensor(gej[:], gecm[:], per_tile(used[:]), ALU.mult))
                link(nc.vector.tensor_reduce(tabf[:, 1], gej[:], AX.X, ALU.add))
                link(nc.vector.tensor_copy(ktab[:], tabf[:, 1]))
                link(nc.vector.tensor_scalar(pari[:], ktab[:], 1, None, ALU.bitwise_and))
                link(nc.vector.tensor_copy(tabf[:, 3], pari[:]))
                link(nc.vector.scalar_tensor_tensor(tabf[:, 3], gecm[:, :, E - 1], 2.0, tabf[:, 3], ALU.mult, ALU.max))
                nc.vector.tensor_copy(stab[:], tabf[:, 3])

            def table_rows():
                last = gecm[:, :, 0:E - 1]
                link(nc.vector.tensor_scalar(jump[:], ntl[:], -float(TR), float(REG), ALU.mult, ALU.add))
                link(nc.vector.tensor_tensor(gej[:, :, 0:E - 1], last, per_tile(jump[:, 0:E - 1]), ALU.mult))
                link(nc.vector.tensor_reduce(tabf[:, 2], gej[:, :, 0:E - 1], AX.X, ALU.add))
                link(nc.vector.scalar_tensor_tensor(tabf[:, 2], io_t[:], float(TR), tabf[:, 2], ALU.mult, ALU.add))
                link(nc.vector.tensor_scalar(tabf[:, 3], gecm[:, :, E - 1], -1.0, 1.0, ALU.mult, ALU.add))
                link(nc.vector.tensor_tensor(tabf[:, 2], tabf[:, 2], tabf[:, 3], ALU.mult))
                nc.vector.tensor_copy(rtab[:], tabf[:, 2])
                link(nc.vector.tensor_tensor(gej[:], io_t[:].unsqueeze(2).broadcast_to([P, ETL, E]), per_tile(tbeg[:]),
                                             ALU.is_equal))
                link(nc.vector.tensor_tensor(gej[:], gej[:], per_tile(nxt[:]), ALU.mult))
                link(nc.vector.tensor_reduce(tabf[:, 0], gej[:], AX.X, ALU.add))
                nc.vector.tensor_copy(ntab[:], tabf[:, 0]).then_inc(tab_ok, 1)

            pf_ok = sem("pf_ok")
            staggered(dve, body)

        @block.gpsimd
        def _(pool):
            def body(g, q, att_on, ffn_on):
                f, r = g - 1, 1 - q

                def rstd(i):
                    wait(pool, stat2, 8 * g + TG * (i + 1))
                    nc.gpsimd.tensor_scalar(rs2[:, i, 0], mv2[:, i, :, 1], EPS_LN, None, ALU.add).then_inc(rse2, 1)
                    wait(pool, rse2, 2 * g + i + 1)
                    nc.gpsimd.tensor_tensor(rs2[:, i, 1], rs2[:, i, 0], expo[:, 1, 0:TG], ALU.pow).then_inc(rstd2, 1)

                def bias(g):
                    xg = X[:, bass.ds(TG * g, TG), :]
                    nc.gpsimd.tensor_tensor(xg, xg, bo_row[:].unsqueeze(1).broadcast_to([P, TG, C]), ALU.add
                                            ).then_inc(xb_ok, 1)

                def scatter():
                    wait(pool, pos_ok, f + 1)
                    for t in range(TG):
                        for k in range(TOPK):
                            nc.gpsimd.indirect_dma_start(
                                out=hs[:, :], out_offset=bass.IndirectOffsetOnAxis(ap=post[:, r, t, k:k + 1], axis=0),
                                in_=h2[:, r, t], in_offset=None).then_inc(scat, 16)

                if att_on:
                    if isinstance(g, int) and g == 0:
                        bias(0)
                    rstd(0)
                    rstd(1)
                if ffn_on:
                    scatter()
                if att_on and not (isinstance(g, int) and g == NG - 1):
                    bias(g + 1)

            nc.gpsimd.memset(h2[:, :, :, C:ROW], 0.0).then_inc(h2_set, 1)
            n = [0]

            def link(ins):
                n[0] += 1
                ins.then_inc(tb_pool, 1)
                wait(pool, tb_pool, n[0])

            link(nc.gpsimd.iota(io_t[:], [[1, ETL]], base=0, channel_multiplier=0,
                                allow_small_or_imprecise_dtypes=True))
            link(nc.gpsimd.iota(io_k[:], [[0, E], [TR, NT // 2]], base=0, channel_multiplier=0,
                                allow_small_or_imprecise_dtypes=True))
            link(nc.gpsimd.memset(upto[:], 1.0))
            link(nc.gpsimd.affine_select(out=upto[:], in_=upto[:], compare_op=ALU.is_ge, fill=0.0, base=0,
                                         pattern=[[1, E], [-1, E]], channel_multiplier=0))
            link(nc.gpsimd.memset(prow[:], 0.0))
            nc.gpsimd.iota(prow[:, C:C + 1].bitcast(U32), [[0, 1]], base=N, channel_multiplier=1).then_inc(tb_c, 1)
            staggered(pool, body)

        @block.sync
        def _(sp):
            with sp.Fori(0, NG - 1) as f:
                sp.wait_ge(sh_ev, 2 * f + 2)
                sp.dma_start(shd_v[:, bass.ds(TG * f, TG), :], sh[:]).then_inc(sh_st, 16)
            sp.wait_ge(tab_ok, 2)
            weights(sp, entry(sp, etab, 0, E - 1))
            sp.wait_ge(tb_c, 1)
            sp.wait_ge(tab_ok, 1)
            for e in range(E):
                row = entry(sp, padt, e, E * REG - TR)
                sp.dma_start(hs[bass.ds(row, TR), :].rearrange("(h p) c -> p h c", p=P),
                              prow[:].unsqueeze(1).broadcast_to([P, 2, ROW])).then_inc(pad_st, 16)
            sp.dma_start(shd[N:N + P, :], prow[:, 0:C]).then_inc(end_st, 16)
            sp.wait_ge(sh_st, 16 * NG)

    b3 = Map(nc, after_q)
    dbias = b3("dbias", [P, E, C], F32)
    hin = b3("hin", [P, 2, 2, C], F32)
    meta = b3("meta", [P, 2, 2, META], F32)
    eT = b3("eT", [P, 2, 2, CK, TR], F32R)
    gu = b3("gu", [P, 2, 2, TR], F32)
    gTh = b3("gTh", [P, 2, MK, TR], F32R)
    gTl = b3("gTl", [P, 2, MK, TR], F32R)
    yc = b3("yc", [P, 2, C], F32)
    yb = b3("yb", [P, 2, 2, C], F32)
    names = ("ht_mm", "ht_hi", "ht_lo", "eu_mm", "eu_g", "eu_hi", "eu_lo",
             "ey_mm", "ey_ev", "y_ok", "y_st")
    (ht_mm, ht_hi, ht_lo, eu_mm, eu_g, eu_hi, eu_lo, ey_mm, ey_ev, y_ok,
     y_st) = [sem(n) for n in names]
    h_in = [sem(f"h_in{i}") for i in range(2)]
    m_in = [sem(f"m_in{i}") for i in range(2)]
    MC = MK // 2

    def tiles(eng, body):
        body(0, 0, True, 0)
        body(1, 1, True, 0)
        with eng.Fori(1, ET // 2) as i:
            body(2 * i, 0, True, i)
            body(2 * i + 1, 1, True, i)
        body(ET - 1, 0, False, ET // 2)

    def needed(eng, j):
        return eng.If_ne(eng.to_reg(entry(eng, stab, j, 2)), 2)

    assert ET % 2 == 1
    with ExitStack() as mem, nc.Block() as block:
        psU = mem.enter_context(nc.psum_tensor("psUp", [P, MC, HALF], F32))
        psH = mem.enter_context(nc.psum_tensor("psH", [P, HALF], F32))
        psE = mem.enter_context(nc.psum_tensor("psE", [P, 2, HALF], F32))

        @block.sync
        def _(sp):
            def rows(j, u):
                row = entry(sp, rtab, j, E * REG - TR)
                if later(j, 2):
                    wait(sp, ht_mm, j - 1)
                sp.dma_start(hin[:, u], hs[bass.ds(row, TR), 0:C].rearrange("(h p) c -> p h c", p=P)
                             ).then_inc(h_in[u], 16)

            def ahead(j):
                e = entry(sp, ntab, j, E - 1)
                k = entry(sp, ktab, j, E)
                with sp.If_ne(sp.to_reg(e), 0):
                    wait(sp, w_ok, 2 * k + 2)
                    weights(sp, e)

            sp.wait_ge(scat, 16 * TG * TOPK * NG)
            sp.wait_ge(pad_st, 16 * E)
            rows(0, 0)
            rows(1, 1)
            sp.dma_start(dbias[:], down_b.partition_broadcast(P)).then_inc(db_in, 16)
            ahead(0)
            with sp.Fori(1, ETL // 2) as i:
                with needed(sp, 2 * i - 2):
                    rows(2 * i, 0)
                ahead(2 * i - 1)
                with needed(sp, 2 * i - 1):
                    rows(2 * i + 1, 1)
                ahead(2 * i)

        @block.tensor
        def _(pe):
            def turn_h(j, u, i):
                pe.wait_ge(h_in[u], 16 * i + 16)
                if later(j, 1):
                    pe.wait_ge(ht_lo, j)
                for k in range(CK):
                    for h in range(2):
                        mm = nc.tensor.transpose(psH[:, k * TR + h * P:k * TR + (h + 1) * P],
                                                 hin[:, u, h, k * P:(k + 1) * P], ident[:])
                mm.then_inc(ht_mm, 1)

            def up(j, u):
                slot = entry(pe, stab, j, 2)
                k_exp = entry(pe, ktab, j, E)

                def free(m):
                    if later(j, 1):
                        pe.wait_ge(eu_g, MK * j - MK + m + 1)

                for s in range(2):
                    with pe.If_eq(pe.to_reg(slot), s):
                        pe.wait_ge(w_ok, 2 * k_exp + 2)
                        pe.wait_ge(ht_lo, j + 1)
                        for c in range(MC):
                            free(2 * c + 1)
                            for m in (2 * c, 2 * c + 1):
                                n = 0
                                for k in range(CK):
                                    for a, b in PASSES:
                                        mm = nc.tensor.matmul(psU[:, c, (m % 2) * TR:(m % 2 + 1) * TR],
                                                              wup[s][:, a, k, m * P:(m + 1) * P], eT[:, u, b, k],
                                                              start=(n == 0), stop=(n == 5))
                                        n += 1
                            mm.then_inc(eu_mm, 1)

            def down(j, u, more, i):
                slot = entry(pe, stab, j, 2)
                for s in range(2):
                    with pe.If_eq(pe.to_reg(slot), s):
                        if more:
                            turn_h(j + 2, u, i + 1)
                        if later(j, 2):
                            pe.wait_ge(ey_ev, j - 1)
                        pe.wait_ge(eu_lo, MC * j + MC)
                        for h in range(2):
                            n = 0
                            for m in range(MK):
                                for a, b in PASSES:
                                    mm = nc.tensor.matmul(psE[:, u, h * C:(h + 1) * C],
                                                          (gTh, gTl)[a][:, u, m, h * P:(h + 1) * P], wdn[s][:, b, m],
                                                          start=(n == 0), stop=(n == 3 * MK - 1))
                                    n += 1
                        mm.then_inc(ey_mm, 1)

            turn_h(0, 0, 0)
            up(0, 0)
            turn_h(1, 1, 0)

            def body(j, u, more, i):
                if more:
                    up(j + 1, 1 - u)
                down(j, u, more, i)

            tiles(pe, body)

        @block.scalar
        def _(act):
            def ahead(j):
                e = entry(act, ntab, j, E - 1)
                k = entry(act, ktab, j, E)
                with act.If_ne(act.to_reg(e), 0):
                    slot = entry(act, stab, j, 2)
                    if later(j, 1):
                        wait(act, ey_mm, j)
                    for s in range(2):
                        with act.If_eq(act.to_reg(slot), 1 - s):
                            split_hi(act, k + 1, s)

            def high(j, u):
                act.wait_ge(ht_mm, j + 1)
                nc.scalar.copy(eT[:, u, 0].rearrange("p k n -> p (k n)"), psH[:]).then_inc(ht_hi, 1)

            def gelu(j, u):
                e = entry(act, etab, j, E - 1)
                with needed(act, j):
                    chunks(j, u, e)

            def chunks(j, u, e):
                for c in range(MC):
                    wait(act, eu_mm, MC * j + c + 1)
                    if later(j, 1) or c >= 2:
                        wait(act, eu_lo, MC * j + c - 1)
                    for m in range(2):
                        nc.scalar.activation(gu[:, c % 2, m], psU[:, c, m * TR:(m + 1) * TR], ACT.Gelu,
                                             bias=ubias[:, bass.ds(e * MK + 2 * c + m, 1)]).then_inc(eu_g, 1)
                    act.wait_ge(eu_g, MK * j + 2 * c + 2)
                    if later(j, 2):
                        act.wait_ge(ey_mm, j - 1)
                    nc.scalar.copy(gTh[:, u, 2 * c:2 * c + 2], gu[:, c % 2]).then_inc(eu_hi, 1)

            def body(j, u, more, i):
                with needed(act, j):
                    ahead(j)
                    if more:
                        gelu(j + 1, 1 - u)
                        high(j + 2, u)

            high(0, 0)
            gelu(0, 0)
            high(1, 1)
            tiles(act, body)

        @block.vector
        def _(dve):
            def ahead(j):
                e = entry(dve, ntab, j, E - 1)
                k = entry(dve, ktab, j, E)
                with dve.If_ne(dve.to_reg(e), 0):
                    slot = entry(dve, stab, j, 2)
                    for s in range(2):
                        with dve.If_eq(dve.to_reg(slot), 1 - s):
                            split_lo(dve, k + 1, s)

            def low(j, u):
                dve.wait_ge(ht_hi, j + 1)
                nc.vector.tensor_tensor(eT[:, u, 1].rearrange("p k n -> p (k n)"), psH[:],
                                        f32(eT[:, u, 0].rearrange("p k n -> p (k n)")), ALU.subtract).then_inc(ht_lo, 1)

            def low_g(j, u):
                with needed(dve, j):
                    for c in range(MC):
                        dve.wait_ge(eu_hi, MC * j + c + 1)
                        nc.vector.tensor_tensor(gTl[:, u, 2 * c:2 * c + 2], gu[:, c % 2],
                                                f32(gTh[:, u, 2 * c:2 * c + 2]), ALU.subtract).then_inc(eu_lo, 1)

            def result(j, u, i):
                e = entry(dve, etab, j, E - 1)
                if later(j, 1):
                    wait(dve, y_ok, j)
                wait(dve, m_in[u], 16 * i + 16)
                wait(dve, ey_mm, j + 1)
                nc.vector.tensor_tensor(yc[:], psE[:, u].rearrange("p (h c) -> p h c", c=C),
                                        dbias[:, bass.ds(e, 1), :].broadcast_to([P, 2, C]), ALU.add).then_inc(ey_ev, 1)
                wait(dve, ey_ev, j + 1)
                nc.vector.tensor_tensor(yb[:, u], yc[:],
                                        meta[:, u, :, bass.ds(e + 1, 1)].broadcast_to([P, 2, C]), ALU.mult
                                        ).then_inc(y_ok, 1)

            def body(j, u, more, i):
                with needed(dve, j):
                    ahead(j)
                    if more:
                        low_g(j + 1, 1 - u)
                        low(j + 2, u)
                    result(j, u, i)

            low(0, 0)
            low_g(0, 0)
            low(1, 1)
            dve.wait_ge(db_in, 16)
            tiles(dve, body)

        @block.gpsimd
        def _(pool):
            def tails(j, u):
                row = entry(pool, rtab, j, E * REG - TR)
                with needed(pool, j):
                    pool.dma_start(meta[:, u], hs[bass.ds(row, TR), C:ROW].rearrange("(h p) c -> p h c", p=P)
                                   ).then_inc(m_in[u], 16)

            def body(j, u, more, i):
                with needed(pool, j):
                    add(j, u)
                    if more:
                        tails(j + 2, u)

            def add(j, u):
                wait(pool, y_ok, j + 1)
                for h in range(2):
                    nc.gpsimd.indirect_dma_start(
                        out=shd[:, :], out_offset=bass.IndirectOffsetOnAxis(ap=meta[:, u, h, 0:1].bitcast(U32), axis=0),
                        in_=yb[:, u, h], in_offset=None, compute_op=ALU.add).then_inc(y_st, 16)
                    wait(pool, y_st, 16 * (2 * j + h + 1))

            pool.wait_ge(scat, 16 * TG * TOPK * NG)
            pool.wait_ge(pad_st, 16 * E)
            pool.wait_ge(end_st, 16)
            tails(0, 0)
            tails(1, 1)
            tiles(pool, body)

    b4 = Map(nc, phase)
    acc = b4("acc", [P, NT, C], F32)
    top = b4("top", [P, 2, TG], F32)
    QD = 4
    f_s, f_o = [[sem(f"{n}{i}") for i in range(QD)] for n in ("f_s", "f_o")]
    f_c, f_a, f_ok = [sem(n) for n in ("f_c", "f_a", "f_ok")]

    def groups4(eng, body):
        for q in range(QD):
            body(q, q, 0)
        with eng.Fori(1, NG // QD) as i:
            for q in range(QD):
                body(QD * i + q, q, i)

    with nc.Block() as block:
        @block.sync
        def _(sp):
            def body(g, q, i):
                if later(i, 1):
                    sp.wait_ge(f_s[q], 16 * i)
                sp.dma_start(acc[:, bass.ds(TG * g, TG)], shd_v[:, bass.ds(TG * g, TG), :]).then_inc(f_s[q], 16)

            groups4(sp, body)

        @block.gpsimd
        def _(pool):
            def body(g, q, i):
                wait(pool, f_a, TG * g + TG)
                xg = X[:, bass.ds(TG * g, TG), :]
                nc.gpsimd.tensor_tensor(xg, xg, acc[:, bass.ds(TG * g, TG), :], ALU.add).then_inc(f_ok, 1)

            groups4(pool, body)

        @block.scalar
        def _(act):
            def body(g, q, i):
                if later(i, 1):
                    act.wait_ge(f_o[q], 16 * i)
                act.wait_ge(f_ok, g + 1)
                act.dma_start(out_v[:, bass.ds(TG * g, TG), :], X[:, bass.ds(TG * g, TG), :]).then_inc(f_o[q], 16)

            groups4(act, body)
            for q in range(QD):
                act.wait_ge(f_o[q], 16 * (NG // QD))

        @block.vector
        def _(dve):
            def body(g, q, i):
                n = [0]
                STEPS = 3

                def link(ins):
                    n[0] += 1
                    ins.then_inc(f_c, 1)
                    dve.wait_ge(f_c, STEPS * g + n[0])

                dve.wait_ge(f_s[q], 16 * i + 16)
                link(nc.vector.tensor_reduce(top[:, 0], acc[:, bass.ds(TG * g, TG), :], AX.X, ALU.max,
                                             apply_absolute_value=True))
                link(nc.vector.tensor_scalar(top[:, 0], top[:, 0], EPS, None, ALU.add))
                link(nc.vector.reciprocal(top[:, 1], top[:, 0]))
                for t in range(TG):
                    row = acc[:, bass.ds(TG * g + t, 1), :].rearrange("p a c -> p (a c)")
                    nc.vector.scalar_tensor_tensor(row, row, top[:, 1, t:t + 1], gate_fb[:], ALU.mult, ALU.mult
                                                   ).then_inc(f_a, 1)

            groups4(dve, body)
    ctx.close()


_INS = ["L0_attn_x", "L0_attn_Wq", "L0_attn_bq", "L0_attn_Wk", "L0_attn_bk", "L0_attn_Wv", "L0_attn_bv",
        "L0_attn_Wo", "L0_attn_bo", "L0_attn_ln_g", "L0_attn_ln_b", "L0_ffn_gate_w", "L0_ffn_bias",
        "L0_ffn_up_w", "L0_ffn_up_b", "L0_ffn_down_w", "L0_ffn_down_b", "L0_ffn_sw_up", "L0_ffn_sb_up",
        "L0_ffn_sw_down", "L0_ffn_sb_down", "L0_c", "L0_wmod"]


def kernel(**inputs):
    import numpy as _np
    import concourse.bacc as _bacc
    from concourse.bass_utils import run_bass_kernel_spmd as _run

    nc = _bacc.Bacc("TRN2", target_bir_lowering=False, num_devices=1)
    arrays, args = {}, []
    for name in _INS:
        a = _np.ascontiguousarray(inputs[name])
        arrays[f"in_{name}"] = a
        args.append(nc.dram_tensor(f"in_{name}", a.shape, F32, kind="ExternalInput").ap())
    scratch = [nc.dram_tensor("expert_in", (E * REG, ROW), F32, kind="Internal").ap(),
               nc.dram_tensor("ffn_out", (N + P, C), F32, kind="Internal").ap()]
    out = nc.dram_tensor("out", (1, N, C), F32, kind="ExternalOutput").ap()
    adaln_block(nc, *args, *scratch, out)
    r = _run(nc, [arrays], core_ids=[0])
    return r.results[0]["out"]
```
